# Optimizing a Trainium2 kernel written in Bass

```python
import numpy as np
import jax
import jax.numpy as jnp

def _softmax(x, axis=-1):
    return jax.nn.softmax(x, axis=axis)

def _gelu(x):
    return jax.nn.gelu(x, approximate=True)

def _silu(x):
    return jax.nn.silu(x)

def _sigmoid(x):
    return jax.nn.sigmoid(x)

def _layernorm(x, axis=-1, eps=1e-05):
    m = jnp.mean(x, axis=axis, keepdims=True)
    v = jnp.var(x, axis=axis, keepdims=True)
    return (x - m) / jnp.sqrt(v + eps)

def _scatter_add(tgt, idx, src, axis=0):
    return tgt.at[idx].add(src)

def _segment_sum(src, seg, n):
    return jax.ops.segment_sum(src, seg, n)
kernel_name = 'mk_gps_d2_gnn_r8_4d6335'

def setup_inputs(seed: int=0):
    np.random.seed(seed)
    _w = jnp.asarray

    def _rec_inputs():
        import jax
        import jax.numpy as jnp
        _gk = jax.random.key(seed)
        x = -6.415e-05 + 1 * jax.random.normal(jax.random.fold_in(_gk, 1), (1250, 512), jnp.float32)
        _s = jax.random.randint(jax.random.fold_in(_gk, 2), (20000,), 0, 1250, jnp.int32)
        _d = jax.random.randint(jax.random.fold_in(_gk, 3), (20000,), 0, 1250, jnp.int32)
        _loop = jnp.arange(1250, dtype=jnp.int32)
        src = jnp.concatenate([_s, _d, _loop])
        dst = jnp.concatenate([_d, _s, _loop])
        _o = jnp.argsort(dst, stable=True)
        src = src[_o]
        dst = dst[_o]
        edge_attr_32 = jax.random.uniform(jax.random.fold_in(_gk, 11), (41250, 32), jnp.float32, 0.0, 1)
        edge_attr_4 = 0.000937891 + 0.999965 * jax.random.normal(jax.random.fold_in(_gk, 12), (41250, 4), jnp.float32)
        return (x, src, dst, edge_attr_32, edge_attr_4)
    x, src, dst, edge_attr_32, edge_attr_4 = _rec_inputs()

    def _L0_gnn_setup():
        import jax, jax.numpy as jnp
        import numpy as np
        import math
        N, E = (2500, 25000)
        MUL = 128
        D = MUL + 3 * MUL
        EDGE_ATTR = 32
        HID = 32
        LOG2 = math.log(2.0)

        def ssp(x):
            return jax.nn.softplus(x) - LOG2

        def split_irreps(x):
            return (x[:, :MUL], x[:, MUL:].reshape(x.shape[0], MUL, 3))

        def merge_irreps(x0, x1):
            return jnp.concatenate([x0, x1.reshape(x1.shape[0], MUL * 3)], axis=-1)

        def irrep_linear(x, W0, b0, W1):
            x0, x1 = split_irreps(x)
            y0 = x0 @ W0 + b0
            y1 = jnp.einsum('nuc,uv->nvc', x1, W1)
            return merge_irreps(y0, y1)
        key = jax.random.key(seed)
        ks = iter(jax.random.split(key, 32))

        def randn(shape, scale=1.0):
            return (scale * jax.random.normal(next(ks), shape)).astype(jnp.float32)
        inp = {'x': randn((N, D)), 'edge_sh': randn((E, 4)), 'edge_attr': jax.random.uniform(next(ks), (E, EDGE_ATTR), dtype=jnp.float32), 'edge_index': jax.random.randint(next(ks), (2, E), 0, N, dtype=jnp.int32), 'W_pre0': randn((MUL, MUL), MUL ** (-0.5)), 'b_pre0': jnp.zeros((MUL,), jnp.float32), 'W_pre1': randn((MUL, MUL), MUL ** (-0.5)), 'W_nd0': randn((MUL, MUL), MUL ** (-0.5)), 'b_nd0': jnp.zeros((MUL,), jnp.float32), 'W_nd1': randn((MUL, MUL), MUL ** (-0.5)), 'W_g1': randn((2 * MUL, 2 * MUL), (2 * MUL) ** (-0.5)), 'b_g1': jnp.zeros((2 * MUL,), jnp.float32), 'W_g2': randn((2 * MUL, 2 * MUL), (2 * MUL) ** (-0.5)), 'b_g2': jnp.zeros((2 * MUL,), jnp.float32), 'W_f1': randn((EDGE_ATTR, HID), EDGE_ATTR ** (-0.5)), 'W_f2': randn((HID, 4 * MUL), HID ** (-0.5)), 'W_s1': randn((3 * MUL, HID), (3 * MUL) ** (-0.5)), 'W_s2': randn((HID, 4 * MUL), HID ** (-0.5)), 'W_o0': randn((MUL, MUL), MUL ** (-0.5)), 'b_o0': jnp.zeros((MUL,), jnp.float32), 'W_o1': randn((MUL, MUL), MUL ** (-0.5))}
        return inp
    _L0_gnn_all = _L0_gnn_setup()
    _L0_gnn_in = {k: v for k, v in _L0_gnn_all.items() if k in ('W_pre0', 'b_pre0', 'W_pre1', 'W_nd0', 'b_nd0', 'W_nd1', 'W_g1', 'b_g1', 'W_g2', 'b_g2', 'W_f1', 'W_f2', 'W_s1', 'W_s2', 'W_o0', 'b_o0', 'W_o1')}
    del _L0_gnn_all

    def _L0_mix_setup():
        import jax, jax.numpy as jnp
        import numpy as np
        B, N, DIM = (2, 512, 512)
        HEADS, DIM_HEAD = (8, 64)
        INNER = HEADS * DIM_HEAD
        SCALE = DIM_HEAD ** (-0.5)
        LN_EPS = 1e-05

        def _layernorm(x, gamma, beta):
            mu = jnp.mean(x, axis=-1, keepdims=True)
            var = jnp.mean(jnp.square(x - mu), axis=-1, keepdims=True)
            return (x - mu) * jax.lax.rsqrt(var + LN_EPS) * gamma + beta
        key = jax.random.key(seed)
        ks = jax.random.split(key, 4)
        x = jax.random.normal(ks[0], (B, N, DIM), dtype=jnp.float32)
        w_qkv = jax.random.normal(ks[1], (DIM, 3 * INNER), dtype=jnp.float32) * DIM ** (-0.5)
        ln_gamma = jnp.ones((INNER,), dtype=jnp.float32)
        ln_beta = jnp.zeros((INNER,), dtype=jnp.float32)
        w_out = jax.random.normal(ks[2], (INNER, DIM), dtype=jnp.float32) * INNER ** (-0.5)
        b_out = jnp.zeros((DIM,), dtype=jnp.float32)
        return {'x': x, 'w_qkv': w_qkv, 'ln_gamma': ln_gamma, 'ln_beta': ln_beta, 'w_out': w_out, 'b_out': b_out}
    _L0_mix_all = _L0_mix_setup()
    _L0_mix_in = {k: v for k, v in _L0_mix_all.items() if k in ('w_qkv', 'ln_gamma', 'ln_beta', 'w_out', 'b_out')}
    del _L0_mix_all

    def _L0_ffn_setup():
        import jax, jax.numpy as jnp
        import numpy as np
        E = 64
        K = 2
        D = 512
        H = 256
        NSH = 2
        ROUTE_SCALE = 2.5
        CAP = 1024
        STD = 0.02
        key = jax.random.key(seed)
        ks = jax.random.split(key, 8)
        x = jax.random.normal(ks[0], (4, 256, D), dtype=jnp.float32)
        gate_w = jax.random.normal(ks[1], (E, D), dtype=jnp.float32) * STD
        w1 = jax.random.normal(ks[2], (E, D, H), dtype=jnp.float32) * STD
        w3 = jax.random.normal(ks[3], (E, D, H), dtype=jnp.float32) * STD
        w2 = jax.random.normal(ks[4], (E, H, D), dtype=jnp.float32) * STD
        sw1 = jax.random.normal(ks[5], (D, H * NSH), dtype=jnp.float32) * STD
        sw3 = jax.random.normal(ks[6], (D, H * NSH), dtype=jnp.float32) * STD
        sw2 = jax.random.normal(ks[7], (H * NSH, D), dtype=jnp.float32) * STD
        return {'x': x, 'gate_w': gate_w, 'w1': w1, 'w3': w3, 'w2': w2, 'sw1': sw1, 'sw3': sw3, 'sw2': sw2}
    _L0_ffn_all = _L0_ffn_setup()
    _L0_ffn_in = {k: v for k, v in _L0_ffn_all.items() if k in ('gate_w', 'w1', 'w3', 'w2', 'sw1', 'sw3', 'sw2')}
    del _L0_ffn_all

    def _L1_gnn_setup():
        import jax, jax.numpy as jnp
        import numpy as np
        N_NODES = 6250
        N_EDGES = 50000
        IN_DIM = 512
        OUT_DIM = 512
        key = jax.random.key(seed)
        k1, k2, k3, k4 = jax.random.split(key, 4)
        x = jax.random.normal(k1, (N_NODES, IN_DIM), dtype=jnp.float32)
        edge_index = jax.random.randint(k2, (2, N_EDGES), 0, N_NODES, dtype=jnp.int64)
        W = jax.random.normal(k3, (OUT_DIM, IN_DIM), dtype=jnp.float32) / np.sqrt(IN_DIM)
        b = jax.random.normal(k4, (OUT_DIM,), dtype=jnp.float32) * 0.01
        return {'x': x, 'edge_index': edge_index, 'W': W, 'b': b}
    _L1_gnn_all = _L1_gnn_setup()
    _L1_gnn_in = {k: v for k, v in _L1_gnn_all.items() if k in ('W', 'b')}
    del _L1_gnn_all

    def _L1_mix_setup():
        import jax, jax.numpy as jnp
        import numpy as np
        HEADS = 8
        DIM_HEAD = 64
        EPS = 0.0001

        def softmax_kernel(data, proj, is_query):
            data_normalizer = data.shape[-1] ** (-0.25)
            ratio = proj.shape[0] ** (-0.5)
            data_dash = jnp.einsum('bhnd,md->bhnm', data_normalizer * data, proj)
            diag = (data * data).sum(-1) * 0.5 * data_normalizer ** 2
            diag = diag[..., None]
            if is_query:
                stab = jnp.max(data_dash, axis=-1, keepdims=True)
            else:
                stab = jnp.max(data_dash)
            return ratio * (jnp.exp(data_dash - diag - stab) + EPS)

        def linear_attention(q, k, v):
            k_cumsum = k.sum(axis=-2)
            d_inv = 1.0 / jnp.einsum('bhnm,bhm->bhn', q, k_cumsum)
            context = jnp.einsum('bhnm,bhne->bhme', k, v)
            return jnp.einsum('bhme,bhnm,bhn->bhne', context, q, d_inv)
        key = jax.random.key(seed)
        ks = jax.random.split(key, 6)
        b, n, dim = (8, 512, 512)
        m, dh = (266, DIM_HEAD)
        x = jax.random.normal(ks[0], (b, n, dim), dtype=jnp.float32)
        s = dim ** (-0.5)
        Wq = jax.random.normal(ks[1], (dim, dim), dtype=jnp.float32) * s
        Wk = jax.random.normal(ks[2], (dim, dim), dtype=jnp.float32) * s
        Wv = jax.random.normal(ks[3], (dim, dim), dtype=jnp.float32) * s
        Wo = jax.random.normal(ks[4], (dim, dim), dtype=jnp.float32) * s
        bo = jnp.zeros((dim,), dtype=jnp.float32)
        proj = jax.random.normal(ks[5], (m, dh), dtype=jnp.float32)
        return {'x': x, 'Wq': Wq, 'Wk': Wk, 'Wv': Wv, 'Wo': Wo, 'bo': bo, 'proj': proj}
    _L1_mix_all = _L1_mix_setup()
    _L1_mix_in = {k: v for k, v in _L1_mix_all.items() if k in ('Wq', 'Wk', 'Wv', 'Wo', 'bo', 'proj')}
    del _L1_mix_all

    def _L1_ffn_setup():
        import jax, jax.numpy as jnp
        import numpy as np
        CAPACITY_FACTOR = 1.2
        key = jax.random.key(seed)
        k1, k2, k3 = jax.random.split(key, 3)
        B, S, D, E = (8, 512, 512, 16)
        x = jax.random.normal(k1, (B, S, D), dtype=jnp.float32)
        switch_w = jax.random.normal(k2, (E, D), dtype=jnp.float32) * 0.02
        switch_b = jnp.zeros((E,), dtype=jnp.float32)
        expert_w = jax.random.normal(k3, (E, D, D), dtype=jnp.float32) * 0.02
        expert_b = jnp.zeros((E, D), dtype=jnp.float32)
        return {'x': x, 'switch_w': switch_w, 'switch_b': switch_b, 'expert_w': expert_w, 'expert_b': expert_b}
    _L1_ffn_all = _L1_ffn_setup()
    _L1_ffn_in = {k: v for k, v in _L1_ffn_all.items() if k in ('switch_w', 'switch_b', 'expert_w', 'expert_b')}
    del _L1_ffn_all
    return {'x': x, 'src': src, 'dst': dst, 'edge_attr_32': edge_attr_32, 'edge_attr_4': edge_attr_4, 'L0_gnn_W_pre0': _L0_gnn_in['W_pre0'], 'L0_gnn_b_pre0': _L0_gnn_in['b_pre0'], 'L0_gnn_W_pre1': _L0_gnn_in['W_pre1'], 'L0_gnn_W_nd0': _L0_gnn_in['W_nd0'], 'L0_gnn_b_nd0': _L0_gnn_in['b_nd0'], 'L0_gnn_W_nd1': _L0_gnn_in['W_nd1'], 'L0_gnn_W_g1': _L0_gnn_in['W_g1'], 'L0_gnn_b_g1': _L0_gnn_in['b_g1'], 'L0_gnn_W_g2': _L0_gnn_in['W_g2'], 'L0_gnn_b_g2': _L0_gnn_in['b_g2'], 'L0_gnn_W_f1': _L0_gnn_in['W_f1'], 'L0_gnn_W_f2': _L0_gnn_in['W_f2'], 'L0_gnn_W_s1': _L0_gnn_in['W_s1'], 'L0_gnn_W_s2': _L0_gnn_in['W_s2'], 'L0_gnn_W_o0': _L0_gnn_in['W_o0'], 'L0_gnn_b_o0': _L0_gnn_in['b_o0'], 'L0_gnn_W_o1': _L0_gnn_in['W_o1'], 'L0_mix_w_qkv': _L0_mix_in['w_qkv'], 'L0_mix_ln_gamma': _L0_mix_in['ln_gamma'], 'L0_mix_ln_beta': _L0_mix_in['ln_beta'], 'L0_mix_w_out': _L0_mix_in['w_out'], 'L0_mix_b_out': _L0_mix_in['b_out'], 'L0_ffn_gate_w': _L0_ffn_in['gate_w'], 'L0_ffn_w1': _L0_ffn_in['w1'], 'L0_ffn_w3': _L0_ffn_in['w3'], 'L0_ffn_w2': _L0_ffn_in['w2'], 'L0_ffn_sw1': _L0_ffn_in['sw1'], 'L0_ffn_sw3': _L0_ffn_in['sw3'], 'L0_ffn_sw2': _L0_ffn_in['sw2'], 'L1_gnn_W': _L1_gnn_in['W'], 'L1_gnn_b': _L1_gnn_in['b'], 'L1_mix_Wq': _L1_mix_in['Wq'], 'L1_mix_Wk': _L1_mix_in['Wk'], 'L1_mix_Wv': _L1_mix_in['Wv'], 'L1_mix_Wo': _L1_mix_in['Wo'], 'L1_mix_bo': _L1_mix_in['bo'], 'L1_mix_proj': _L1_mix_in['proj'], 'L1_ffn_switch_w': _L1_ffn_in['switch_w'], 'L1_ffn_switch_b': _L1_ffn_in['switch_b'], 'L1_ffn_expert_w': _L1_ffn_in['expert_w'], 'L1_ffn_expert_b': _L1_ffn_in['expert_b']}

def reference(x, src, dst, edge_attr_32, edge_attr_4, L0_gnn_W_pre0, L0_gnn_b_pre0, L0_gnn_W_pre1, L0_gnn_W_nd0, L0_gnn_b_nd0, L0_gnn_W_nd1, L0_gnn_W_g1, L0_gnn_b_g1, L0_gnn_W_g2, L0_gnn_b_g2, L0_gnn_W_f1, L0_gnn_W_f2, L0_gnn_W_s1, L0_gnn_W_s2, L0_gnn_W_o0, L0_gnn_b_o0, L0_gnn_W_o1, L0_mix_w_qkv, L0_mix_ln_gamma, L0_mix_ln_beta, L0_mix_w_out, L0_mix_b_out, L0_ffn_gate_w, L0_ffn_w1, L0_ffn_w3, L0_ffn_w2, L0_ffn_sw1, L0_ffn_sw3, L0_ffn_sw2, L1_gnn_W, L1_gnn_b, L1_mix_Wq, L1_mix_Wk, L1_mix_Wv, L1_mix_Wo, L1_mix_bo, L1_mix_proj, L1_ffn_switch_w, L1_ffn_switch_b, L1_ffn_expert_w, L1_ffn_expert_b):
    import jax
    import jax.numpy as jnp

    def _L0_gnn_ref(x, edge_sh, edge_attr, edge_index, W_pre0, b_pre0, W_pre1, W_nd0, b_nd0, W_nd1, W_g1, b_g1, W_g2, b_g2, W_f1, W_f2, W_s1, W_s2, W_o0, b_o0, W_o1):
        import jax, jax.numpy as jnp
        import numpy as np
        import math
        N, E = (2500, 25000)
        MUL = 128
        D = MUL + 3 * MUL
        EDGE_ATTR = 32
        HID = 32
        LOG2 = math.log(2.0)

        def ssp(x):
            return jax.nn.softplus(x) - LOG2

        def split_irreps(x):
            return (x[:, :MUL], x[:, MUL:].reshape(x.shape[0], MUL, 3))

        def merge_irreps(x0, x1):
            return jnp.concatenate([x0, x1.reshape(x1.shape[0], MUL * 3)], axis=-1)

        def irrep_linear(x, W0, b0, W1):
            x0, x1 = split_irreps(x)
            y0 = x0 @ W0 + b0
            y1 = jnp.einsum('nuc,uv->nvc', x1, W1)
            return merge_irreps(y0, y1)
        edge_dst, edge_src = (edge_index[0], edge_index[1])
        old_x = x
        pre = irrep_linear(x, W_pre0, b_pre0, W_pre1)
        p0, p1 = split_irreps(pre)
        pd0 = p0[edge_dst]
        ip1 = jnp.einsum('eum,eum->eu', p1[edge_dst], p1[edge_src]) / 3.0
        s0 = jnp.concatenate([pd0, pd0, ip1], axis=-1)
        x0, x1 = split_irreps(x)
        n1 = jnp.sqrt(jnp.sum(x1 * x1, axis=-1) / 3.0)
        g = jax.nn.silu(jnp.concatenate([x0, n1], -1) @ W_g1 + b_g1) @ W_g2 + b_g2
        xg = merge_irreps(g[:, :MUL], x1 * g[:, MUL:, None])
        x = irrep_linear(xg, W_nd0, b_nd0, W_nd1)
        self_x = x
        w = ssp(edge_attr @ W_f1) @ W_f2 * (ssp(s0 @ W_s1) @ W_s2)
        w1, w2, w3, w4 = jnp.split(w, 4, axis=-1)
        x0e, x1e = split_irreps(x[edge_src])
        sh0, sh1 = (edge_sh[:, 0], edge_sh[:, 1:4])
        out0 = w1 * x0e * sh0[:, None] + w4 * (jnp.einsum('eum,em->eu', x1e, sh1) / jnp.sqrt(3.0))
        out1 = w2[:, :, None] * x0e[:, :, None] * sh1[:, None, :] + w3[:, :, None] * x1e * sh0[:, None, None]
        edge_feat = merge_irreps(out0, out1)
        out = jax.ops.segment_sum(edge_feat, edge_dst, num_segments=old_x.shape[0])
        out = out + self_x
        out = irrep_linear(out, W_o0, b_o0, W_o1)
        return out + old_x

    def _L0_mix_ref(x, w_qkv, ln_gamma, ln_beta, w_out, b_out):
        import jax, jax.numpy as jnp
        import numpy as np
        B, N, DIM = (2, 512, 512)
        HEADS, DIM_HEAD = (8, 64)
        INNER = HEADS * DIM_HEAD
        SCALE = DIM_HEAD ** (-0.5)
        LN_EPS = 1e-05

        def _layernorm(x, gamma, beta):
            mu = jnp.mean(x, axis=-1, keepdims=True)
            var = jnp.mean(jnp.square(x - mu), axis=-1, keepdims=True)
            return (x - mu) * jax.lax.rsqrt(var + LN_EPS) * gamma + beta
        b, n, _ = x.shape
        qkv = x @ w_qkv
        q, k, v = jnp.split(qkv, 3, axis=-1)

        def to_heads(t):
            return t.reshape(b, n, HEADS, DIM_HEAD).transpose(0, 2, 1, 3)
        q, k, v = (to_heads(q), to_heads(k), to_heads(v))
        dots = jnp.einsum('bhid,bhjd->bhij', q, k) * SCALE
        attn = jax.nn.relu(dots)
        out = jnp.einsum('bhij,bhjd->bhid', attn, v)
        out = out.transpose(0, 2, 1, 3).reshape(b, n, INNER)
        out = _layernorm(out, ln_gamma, ln_beta)
        return out @ w_out + b_out

    def _L0_ffn_ref(x, gate_w, w1, w3, w2, sw1, sw3, sw2):
        import jax, jax.numpy as jnp
        import numpy as np
        E = 64
        K = 2
        D = 512
        H = 256
        NSH = 2
        ROUTE_SCALE = 2.5
        CAP = 1024
        STD = 0.02
        bs, slen, d = x.shape
        xf = x.reshape(-1, d)
        logits = xf @ gate_w.T
        scores = jax.nn.sigmoid(logits.astype(jnp.float32))
        top_scores, top_idx = jax.lax.top_k(scores, K)
        top_scores = top_scores / (top_scores.sum(-1, keepdims=True) + 1e-20)
        top_scores = top_scores * ROUTE_SCALE
        flat_e = top_idx.reshape(-1)
        x_pairs = jnp.repeat(xf, K, axis=0)
        oh = jax.nn.one_hot(flat_e, E, dtype=jnp.int32)
        pos = jnp.take_along_axis(jnp.cumsum(oh, axis=0), flat_e[:, None], axis=1)[:, 0] - 1
        buf = jnp.zeros((E, CAP, d), dtype=xf.dtype).at[flat_e, pos].set(x_pairs, mode='drop')
        h = jax.nn.silu(jnp.einsum('ecd,edh->ech', buf, w1)) * jnp.einsum('ecd,edh->ech', buf, w3)
        y = jnp.einsum('ech,ehd->ecd', h, w2)
        valid = (pos < CAP)[:, None]
        y_pairs = jnp.where(valid, y[flat_e, jnp.minimum(pos, CAP - 1)], 0.0)
        routed = (y_pairs.reshape(-1, K, d) * top_scores[..., None].astype(xf.dtype)).sum(axis=1)
        shared = jax.nn.silu(xf @ sw1) * (xf @ sw3) @ sw2
        return (shared + routed).reshape(bs, slen, d)

    def _L1_gnn_ref(x, edge_index, W, b):
        import jax, jax.numpy as jnp
        import numpy as np
        N_NODES = 6250
        N_EDGES = 50000
        IN_DIM = 512
        OUT_DIM = 512
        n = x.shape[0]
        loops = jnp.arange(n, dtype=edge_index.dtype)
        row = jnp.concatenate([edge_index[0], loops])
        col = jnp.concatenate([edge_index[1], loops])
        deg = jax.ops.segment_sum(jnp.ones(row.shape[0], dtype=x.dtype), row, num_segments=n)
        dis = jax.lax.rsqrt(deg)
        norm = dis[row] * dis[col]
        h = x @ W.T + b
        out = jax.ops.segment_sum(norm[:, None] * h[row], col, num_segments=n)
        return jax.nn.relu(out)

    def _L1_mix_ref(x, Wq, Wk, Wv, Wo, bo, proj):
        import jax, jax.numpy as jnp
        import numpy as np
        HEADS = 8
        DIM_HEAD = 64
        EPS = 0.0001

        def softmax_kernel(data, proj, is_query):
            data_normalizer = data.shape[-1] ** (-0.25)
            ratio = proj.shape[0] ** (-0.5)
            data_dash = jnp.einsum('bhnd,md->bhnm', data_normalizer * data, proj)
            diag = (data * data).sum(-1) * 0.5 * data_normalizer ** 2
            diag = diag[..., None]
            if is_query:
                stab = jnp.max(data_dash, axis=-1, keepdims=True)
            else:
                stab = jnp.max(data_dash)
            return ratio * (jnp.exp(data_dash - diag - stab) + EPS)

        def linear_attention(q, k, v):
            k_cumsum = k.sum(axis=-2)
            d_inv = 1.0 / jnp.einsum('bhnm,bhm->bhn', q, k_cumsum)
            context = jnp.einsum('bhnm,bhne->bhme', k, v)
            return jnp.einsum('bhme,bhnm,bhn->bhne', context, q, d_inv)
        b, n, dim = x.shape
        h, dh = (HEADS, DIM_HEAD)
        q = (x @ Wq).reshape(b, n, h, dh).transpose(0, 2, 1, 3)
        k = (x @ Wk).reshape(b, n, h, dh).transpose(0, 2, 1, 3)
        v = (x @ Wv).reshape(b, n, h, dh).transpose(0, 2, 1, 3)
        qp = softmax_kernel(q, proj, is_query=True)
        kp = softmax_kernel(k, proj, is_query=False)
        out = linear_attention(qp, kp, v)
        out = out.transpose(0, 2, 1, 3).reshape(b, n, h * dh)
        return out @ Wo + bo

    def _L1_ffn_ref(x, switch_w, switch_b, expert_w, expert_b):
        import jax, jax.numpy as jnp
        import numpy as np
        CAPACITY_FACTOR = 1.2
        B, S, D = x.shape
        E = switch_w.shape[0]
        N = B * S
        xf = x.reshape(N, D)
        logits = xf @ switch_w.T + switch_b
        probs = jax.nn.softmax(logits, axis=-1)
        route_probs = jnp.max(probs, axis=-1)
        routes = jnp.argmax(probs, axis=-1)
        oh = jax.nn.one_hot(routes, E, dtype=jnp.int32)
        pos = jnp.take_along_axis(jnp.cumsum(oh, axis=0), routes[:, None], axis=1)[:, 0] - 1
        capacity = int(CAPACITY_FACTOR * N / E)
        keep = pos < capacity
        buf = jnp.zeros((E, capacity, D), dtype=xf.dtype).at[routes, pos].set(xf)
        y = jnp.einsum('ecd,efd->ecf', buf, expert_w) + expert_b[:, None, :]
        gathered = y[routes, jnp.minimum(pos, capacity - 1)]
        out = jnp.where(keep[:, None], gathered, xf) * route_probs[:, None]
        return out.reshape(B, S, D)
    edge_index = jnp.stack([src, dst])
    xn = _layernorm(x, axis=-1)
    x = x + _L0_gnn_ref(xn, edge_attr_4, edge_attr_32, edge_index, L0_gnn_W_pre0, L0_gnn_b_pre0, L0_gnn_W_pre1, L0_gnn_W_nd0, L0_gnn_b_nd0, L0_gnn_W_nd1, L0_gnn_W_g1, L0_gnn_b_g1, L0_gnn_W_g2, L0_gnn_b_g2, L0_gnn_W_f1, L0_gnn_W_f2, L0_gnn_W_s1, L0_gnn_W_s2, L0_gnn_W_o0, L0_gnn_b_o0, L0_gnn_W_o1) + _L0_mix_ref(xn[None], L0_mix_w_qkv, L0_mix_ln_gamma, L0_mix_ln_beta, L0_mix_w_out, L0_mix_b_out)[0]
    x = x + _L0_ffn_ref(_layernorm(x, axis=-1)[None], L0_ffn_gate_w, L0_ffn_w1, L0_ffn_w3, L0_ffn_w2, L0_ffn_sw1, L0_ffn_sw3, L0_ffn_sw2)[0]
    xn = _layernorm(x, axis=-1)
    x = x + _L1_gnn_ref(xn, edge_index, L1_gnn_W, L1_gnn_b) + _L1_mix_ref(xn[None], L1_mix_Wq, L1_mix_Wk, L1_mix_Wv, L1_mix_Wo, L1_mix_bo, L1_mix_proj)[0]
    x = x + _L1_ffn_ref(_layernorm(x, axis=-1)[None], L1_ffn_switch_w, L1_ffn_switch_b, L1_ffn_expert_w, L1_ffn_expert_b)[0]
    return x

_drawn_inputs = setup_inputs


def setup_inputs(seed=0):
    import zlib

    import numpy as np

    out = dict(_drawn_inputs(seed))
    spreads = {'L0_gnn_b_pre0': (0.0, 0.325),
     'L0_gnn_b_nd0': (0.0, 0.1),
     'L0_gnn_b_g1': (0.0, 0.1),
     'L0_gnn_b_g2': (0.0, 0.1),
     'L0_gnn_b_o0': (0.0, 0.333),
     'L0_mix_ln_gamma': (1.0, 0.2),
     'L0_mix_ln_beta': (0.0, 0.1),
     'L0_mix_b_out': (0.0, 0.1),
     'L1_mix_bo': (0.0, 0.1),
     'L1_ffn_switch_b': (0.0, 0.427),
     'L1_ffn_expert_b': (0.0, 0.8)}
    factors = {'L0_ffn_sw1': 2.807,
     'L0_ffn_sw3': 2.732,
     'L0_ffn_sw2': 2.725,
     'L1_gnn_b': 22.396,
     'L1_mix_Wq': 8.0,
     'L1_mix_Wk': 8.0,
     'L1_mix_proj': 8.0}
    for name, (base, spread) in spreads.items():
        noise = np.random.default_rng([zlib.crc32(name.encode()), seed]).standard_normal(out[name].shape)
        drawn = base * np.exp(spread * noise) if base else spread * noise
        out[name] = jnp.asarray(drawn.astype(out[name].dtype))
    for name, factor in factors.items():
        out[name] = (out[name] * factor).astype(out[name].dtype)
    return out
```

```python
from contextlib import ExitStack

import concourse.bass as bass
from concourse import mybir

F32 = mybir.dt.float32
BF16 = mybir.dt.bfloat16
F16 = mybir.dt.float16
I32 = mybir.dt.int32
ALU = mybir.AluOpType
ACT = mybir.ActivationFunctionType
AX = mybir.AxisListType

N, D = 1250, 512
P, TILES = 125, 10
KD = D // 128
MUL = 128
E = 41250
CH, CHUNKS = 250, 5
LN_EPS = 1e-5
EXP_LN = "natural_log_exp_and_others"


SOFT = ("padded", "edges_in", "scattered", "d_in", "s_in", "emptied", "x_in", "m_in", "fetched")


class Shop:

    def __init__(self, nc, ctx, tag):
        self.nc, self.ctx, self.tag, self.sems, self.hard = nc, ctx, tag, [], []

    def sb(self, name, shape, dt=F32):
        return self.ctx.enter_context(self.nc.sbuf_tensor(f"{self.tag}_{name}", shape, dt))

    def ps(self, name, shape, dt=F32):
        return self.ctx.enter_context(self.nc.psum_tensor(f"{self.tag}_{name}", shape, dt))

    def sem(self, name):
        if not self.sems:
            self.ctx.callback(self.clear)
        self.sems.append(self.nc.alloc_semaphore(f"{self.tag}_{name}"))
        if not name.startswith(SOFT):
            self.hard.append(self.sems[-1])
        return self.sems[-1]

    def clear(self):
        with self.nc.Block() as block:
            @block.gpsimd
            def _(pool):
                for sem in self.sems:
                    pool.sem_clear(sem)
        for sem in self.hard:
            self.nc.release_semaphore(sem)


def row(ap, parts):
    return ap.rearrange("(o n) -> o n", o=1).to_broadcast([parts, ap.shape[0]])


def tiles_of(ap):
    return ap.rearrange("(t p) c -> p t c", p=P)


def irrep_rows(w):
    return w[0:MUL, :], w[MUL:D, :].rearrange("(u m) c -> u m c", m=3)


def stage_constants(nc, k):
    with ExitStack() as ctx:
        s = Shop(nc, ctx, "const")
        filled, made = s.sem("filled"), s.sem("made")
        with nc.Block() as block:
            @block.gpsimd
            def _(pool):
                pool.memset(k.ident[:, :], 0.0).then_inc(filled, 1)
                pool.memset(k.before[:, :], 1.0).then_inc(filled, 1)
                pool.memset(k.ones[:, :], 1.0).then_inc(filled, 1)
                pool.memset(k.half[:, :], 0.5).then_inc(filled, 1)
                pool.iota(k.iota_f[:, :], pattern=[[1, 128]], base=0, channel_multiplier=0,
                          allow_small_or_imprecise_dtypes=True).then_inc(filled, 1)
                pool.iota(k.iota_h[:, :], pattern=[[1, N]], base=0, channel_multiplier=0,
                          allow_small_or_imprecise_dtypes=True).then_inc(filled, 1)
                pool.iota(k.part_f[:, :], pattern=[[0, 1]], base=0, channel_multiplier=1,
                          allow_small_or_imprecise_dtypes=True).then_inc(filled, 1)
                pool.wait_ge(filled, 7)
                pool.affine_select(out=k.ident[:, :], in_=k.ident[:, :], compare_op=ALU.not_equal, fill=1.0,
                                   base=0, pattern=[[-1, 128]], channel_multiplier=1).then_inc(made, 1)
                pool.affine_select(out=k.before[:, :], in_=k.before[:, :], compare_op=ALU.is_gt, fill=0.0,
                                   base=0, pattern=[[1, 128]], channel_multiplier=-1).then_inc(made, 1)
                pool.wait_ge(made, 2)


def stage_norm(nc, k, tag, x_dram, x, xn, xT, irreps, xn_dram=None, residual_dram=None, affine=None):
    with ExitStack() as ctx:
        s = Shop(nc, ctx, tag)
        stats = s.sb("stats", [P, TILES, 6])
        mean_var = s.sb("mean_var", [P, TILES, 2])
        var = s.sb("var", [P, TILES])
        inv_var = s.sb("inv_var", [P, TILES])
        rstd = s.sb("rstd", [P, TILES])
        turn = s.ps("turn", [128, 2, 512])
        scale_shift = s.sb("scale_shift", [128, 2, KD])
        loaded, measured, inverted, rooted, normed, turned, kept, saved, added, coefficients_in = (s.sem(n) for n in (
            "loaded", "measured", "inverted", "rooted", "normed", "turned", "kept", "saved", "added",
            "coefficients_in"))
        with nc.Block() as block:
            @block.sync
            def _(sp):
                if x_dram is not None:
                    sp.dma_start(x[:, :, :], tiles_of(x_dram)).then_inc(loaded, 16)
                if affine is not None:
                    for q in range(2):
                        sp.dma_start(scale_shift[:, q, :], affine[q]).then_inc(coefficients_in, 16)
                if xn_dram is not None:
                    sp.wait_ge(normed, TILES)
                    sp.dma_start(tiles_of(xn_dram), xn[:, :, :]).then_inc(saved, 16)
                    sp.wait_ge(saved, 16)

                if residual_dram is not None:
                    sp.wait_ge(added, 1)
                    sp.dma_start(tiles_of(residual_dram), x[:, :, :]).then_inc(saved, 16)
                    sp.wait_ge(saved, 16)

            @block.vector
            def _(dve):
                if x_dram is not None:
                    dve.wait_ge(loaded, 16)
                for t in range(TILES):
                    dve.bn_stats(stats[:, t, :], x[:, t, :]).then_inc(measured, 1)
                dve.wait_ge(measured, TILES)
                for t in range(TILES):
                    dve.bn_aggr(mean_var[:, t, :], stats[:, t, :]).then_inc(measured, 1)
                dve.wait_ge(measured, 2 * TILES)
                dve.tensor_scalar(var[:, :], mean_var[:, :, 1], LN_EPS, None, ALU.add).then_inc(measured, 1)
                dve.wait_ge(measured, 2 * TILES + 1)
                dve.reciprocal(inv_var[:, :], var[:, :]).then_inc(inverted, 1)
                dve.wait_ge(rooted, 1)
                for t in range(TILES):
                    dve.tensor_scalar(xn[:, t, :], x[:, t, :], mean_var[:, t, 0:1], rstd[:, t:t + 1],
                                      ALU.subtract, ALU.mult).then_inc(normed, 1)
                if residual_dram is not None:
                    dve.wait_ge(normed, TILES)
                    dve.tensor_tensor(x[:, :, :], x[:, :, :], xn[:, :, :], ALU.add).then_inc(added, 1)

            @block.scalar
            def _(act):
                act.wait_ge(inverted, 1)
                act.activation(rstd[:, :], inv_var[:, :], ACT.Sqrt).then_inc(rooted, 1)
                if affine is not None:
                    act.wait_ge(coefficients_in, 32)
                for t in range(TILES):
                    act.wait_ge(turned, t + 1)
                    if affine is not None:
                        for c in range(KD):
                            last = act.activation(xT[:, c, t * P:(t + 1) * P], turn[:, t % 2, c * P:(c + 1) * P],
                                                  ACT.Identity, scale=scale_shift[:, 0, c:c + 1],
                                                  bias=scale_shift[:, 1, c:c + 1])
                        last.then_inc(kept, 1)
                        continue
                    act.activation(xT[:, :, t * P:(t + 1) * P],
                                   turn[:, t % 2, 0:KD * P].rearrange("p (c n) -> p c n", c=KD),
                                   ACT.Copy).then_inc(kept, 1)

            @block.tensor
            def _(pe):
                for t in range(TILES):
                    pe.wait_ge(normed, t + 1)
                    if t >= 2:
                        pe.wait_ge(kept, t - 1)
                    for c in range(KD):
                        if irreps:
                            part = xn[:, t, 0:MUL] if c == 0 else xn[:, t, MUL + c - 1:D:3]
                        else:
                            part = xn[:, t, c * 128:(c + 1) * 128]
                        last = pe.transpose(turn[:, t % 2, c * P:(c + 1) * P], part, k.ident[0:P, 0:P])
                    last.then_inc(turned, 1)


def stage_node_tables(nc, k, w, xT, acc, table_d, table_s):
    with ExitStack() as ctx:
        s = Shop(nc, ctx, "nodes")
        pre0, pre1, nd0, nd1 = (s.sb(n, [128, MUL]) for n in ("pre0", "pre1", "nd0", "nd1"))
        g1, g2 = (s.sb(n, [128, 2, 2 * MUL]) for n in ("g1", "g2"))
        s1 = s.sb("s1", [128, 3, 32])
        s1_node = s.sb("s1_node", [128, 32])
        b_pre0 = s.sb("b_pre0", [128, 1])
        b_g1, b_g2 = s.sb("b_g1", [128, 2]), s.sb("b_g2", [128, 2])
        b_nd0 = s.sb("b_nd0", [P, MUL])
        p0T = s.sb("p0T", [128, N])
        normT = s.sb("normT", [128, N])
        square = s.sb("square", [128, 3, N])
        z = s.sb("z", [128, 2, N])
        gate = s.sb("gate", [128, 2, N])
        rows_d = s.sb("rows_d", [P, TILES, 416])
        bank = s.ps("bank", [128, 3, 512])
        loaded, chain, drawn, filled, kept, rooted, squared, exped, saved = (
            s.sem(n) for n in ("loaded", "chain", "drawn", "filled", "kept", "rooted", "squared", "exped", "saved"))
        loads = [(pre0[:, :], w["L0_gnn_W_pre0"]), (pre1[:, :], w["L0_gnn_W_pre1"]),
                 (nd0[:, :], w["L0_gnn_W_nd0"]), (nd1[:, :], w["L0_gnn_W_nd1"]),
                 (g1[:, :, :], w["L0_gnn_W_g1"].rearrange("(c p) n -> p c n", p=128)),
                 (g2[:, :, :], w["L0_gnn_W_g2"].rearrange("(c p) n -> p c n", p=128)),
                 (s1[:, :, :], w["L0_gnn_W_s1"].rearrange("(c p) n -> p c n", p=128)),
                 (b_pre0[:, :], w["L0_gnn_b_pre0"]), (b_g1[:, :], w["L0_gnn_b_g1"]),
                 (b_g2[:, :], w["L0_gnn_b_g2"]), (b_nd0[:, :], row(w["L0_gnn_b_nd0"], P))]
        HIDDEN, GATE, ROWS = CHUNKS, 3 * CHUNKS, 5 * CHUNKS
        with nc.Block() as block:
            @block.sync
            def _(sp):
                for out, in_ in loads:
                    sp.dma_start(out, in_).then_inc(loaded, 16)
                sp.wait_ge(kept, ROWS + 2 * TILES)
                sp.dma_start(tiles_of(table_d), rows_d[:, :, :]).then_inc(saved, 16)
                sp.dma_start(tiles_of(table_s)[:, :, 0:D], acc[:, :, :]).then_inc(saved, 16)
                sp.dma_start(tiles_of(table_s)[:, :, D:D + 384], rows_d[:, :, 0:384]).then_inc(saved, 16)
                sp.wait_ge(saved, 48)

            @block.tensor
            def _(pe):
                job = 0

                def turn():
                    nonlocal job
                    if job >= 3:
                        pe.wait_ge(kept, job - 2)
                    job += 1
                    return bank[:, (job - 1) % 3, :]

                pe.wait_ge(loaded, 16 * len(loads))
                for c in range(CHUNKS):
                    cols = slice(c * CH, (c + 1) * CH)
                    pe.matmul(turn()[:, 0:CH], pre0[:, :], xT[:, 0, cols], start=True, stop=True).then_inc(filled, 1)
                pe.wait_ge(rooted, 1)
                for h in range(2):
                    for c in range(CHUNKS):
                        cols, out = slice(c * CH, (c + 1) * CH), turn()
                        pe.matmul(out[:, 0:CH], g1[:, 0, h * 128:(h + 1) * 128], xT[:, 0, cols], start=True, stop=False)
                        pe.matmul(out[:, 0:CH], g1[:, 1, h * 128:(h + 1) * 128], normT[:, cols],
                                  start=False, stop=True).then_inc(filled, 1)
                pe.wait_ge(drawn, 1)
                for h in range(2):
                    for c in range(CHUNKS):
                        cols, out = slice(c * CH, (c + 1) * CH), turn()
                        for q in range(2):
                            last = pe.matmul(out[:, 0:CH], g2[:, q, h * 128:(h + 1) * 128], z[:, q, cols],
                                             start=(q == 0), stop=(q == 1))
                        last.then_inc(filled, 1)
                pe.wait_ge(drawn, 2)
                for t in range(TILES):
                    cols, out = slice(t * P, (t + 1) * P), turn()
                    for m in range(3):
                        pe.matmul(out[0:P, m * MUL:(m + 1) * MUL], xT[:, 1 + m, cols], pre1[:, :],
                                  start=True, stop=True)
                    pe.matmul(out[0:P, 384:416], p0T[:, cols], s1_node[:, :], start=True, stop=True).then_inc(filled, 1)
                    out = turn()
                    pe.matmul(out[0:P, 0:MUL], gate[:, 0, cols], nd0[:, :], start=True, stop=True)
                    for m in range(3):
                        last = pe.matmul(out[0:P, (1 + m) * MUL:(2 + m) * MUL], square[:, m, cols], nd1[:, :],
                                         start=True, stop=True)
                    last.then_inc(filled, 1)

            @block.scalar
            def _(act):
                act.wait_ge(squared, 1)
                act.activation(normT[:, :], square[:, 0, :], ACT.Sqrt, scale=1.0 / 3.0).then_inc(rooted, 1)
                act.wait_ge(kept, GATE)
                act.activation(gate[:, :, :], z[:, :, :], ACT.Exp, scale=-1.0).then_inc(exped, 1)

            @block.vector
            def _(dve):
                n = 0

                def link(ins):
                    nonlocal n
                    n += 1
                    ins.then_inc(chain, 1)
                    dve.wait_ge(chain, n)

                for m in range(3):
                    last = dve.tensor_tensor(square[:, m, :], xT[:, 1 + m, :], xT[:, 1 + m, :], ALU.mult)
                link(last)
                link(dve.tensor_tensor(square[:, 0, :], square[:, 0, :], square[:, 1, :], ALU.add))
                dve.tensor_tensor(square[:, 0, :], square[:, 0, :], square[:, 2, :], ALU.add).then_inc(squared, 1)
                dve.wait_ge(loaded, 16 * len(loads))
                for c in range(CHUNKS):
                    dve.wait_ge(filled, c + 1)
                    dve.tensor_scalar(p0T[:, c * CH:(c + 1) * CH], bank[:, c % 3, 0:CH], b_pre0[:, 0:1], None,
                                      ALU.add).then_inc(kept, 1)
                for h in range(2):
                    for c in range(CHUNKS):
                        j = HIDDEN + h * CHUNKS + c
                        dve.wait_ge(filled, j + 1)
                        dve.tensor_scalar(z[:, h, c * CH:(c + 1) * CH], bank[:, j % 3, 0:CH], b_g1[:, h:h + 1], None,
                                          ALU.add).then_inc(kept, 1)
                dve.wait_ge(exped, 1)
                link(dve.tensor_scalar(gate[:, :, :], gate[:, :, :], 1.0, None, ALU.add))
                link(dve.reciprocal(gate[:, :, :], gate[:, :, :]))
                dve.tensor_tensor(z[:, :, :], z[:, :, :], gate[:, :, :], ALU.mult).then_inc(drawn, 1)
                dve.wait_ge(drawn, 1)
                for h in range(2):
                    for c in range(CHUNKS):
                        j = GATE + h * CHUNKS + c
                        dve.wait_ge(filled, j + 1)
                        dve.tensor_scalar(gate[:, h, c * CH:(c + 1) * CH], bank[:, j % 3, 0:CH], b_g2[:, h:h + 1],
                                          None, ALU.add).then_inc(kept, 1)
                dve.tensor_scalar(k.s1_pair[:, :], s1[:, 2, :], 1.0 / 3.0, None, ALU.mult).then_inc(squared, 1)
                dve.wait_ge(squared, 2)
                dve.wait_ge(rooted, 1)
                dve.wait_ge(kept, ROWS)
                dve.tensor_tensor(s1_node[:, :], s1[:, 0, :], s1[:, 1, :], ALU.add).then_inc(squared, 1)
                dve.wait_ge(squared, 3)
                for m in range(3):
                    last = dve.tensor_tensor(square[:, m, :], xT[:, 1 + m, :], gate[:, 1, :], ALU.mult)
                last.then_inc(drawn, 1)
                for t in range(TILES):
                    j = ROWS + 2 * t
                    dve.wait_ge(filled, j + 1)
                    dve.tensor_copy(rows_d[:, t, :], bank[0:P, j % 3, 0:416]).then_inc(kept, 1)
                    dve.wait_ge(filled, j + 2)
                    dve.tensor_copy(acc[:, t, MUL:D], bank[0:P, (j + 1) % 3, MUL:D])
                    dve.tensor_tensor(acc[:, t, 0:MUL], bank[0:P, (j + 1) % 3, 0:MUL], b_nd0[:, :],
                                      ALU.add).then_inc(kept, 1)


GROUP = 512
GTILES = GROUP // 128
EF = E // P
GROUPS = (E + TILES * (GROUP - 1)) // GROUP
REC = 40
ECH, ECHUNKS = 33, EF // 33


def stage_edge_places(nc, k, src, dst, meta, slots):
    with ExitStack() as ctx:
        s = Shop(nc, ctx, "places")
        ids = s.sb("ids", [P, 2, EF], I32)
        fields = s.sb("fields", [P, EF, 4])
        d = s.sb("d", [P, EF])
        ones = s.sb("ones", [P, EF])
        inside = s.sb("inside", [P, TILES, EF])
        rank = s.sb("rank", [P, TILES, EF])
        totals = s.sb("totals", [P, TILES])
        small = s.sb("small", [128, 6, TILES])
        whole = s.sb("whole", [128, 2, TILES], I32)
        place = s.sb("place", [P, EF])
        term = s.sb("term", [P, EF])
        slot = s.sb("slot", [P, EF], I32)
        block_f = s.sb("block_f", [1, GROUPS])
        sums = s.ps("sums", [128, 2, 512])
        loaded, counted, summed, chain, done, saved = (
            s.sem(n) for n in ("loaded", "counted", "summed", "chain", "done", "saved"))
        with nc.Block() as block:
            @block.sync
            def _(sp):
                sp.dma_start(ids[:, 0, :], src.rearrange("(p f) -> p f", f=EF)).then_inc(loaded, 16)
                sp.dma_start(ids[:, 1, :], dst.rearrange("(p f) -> p f", f=EF)).then_inc(loaded, 16)
                sp.wait_ge(done, 1)
                sp.dma_start(meta.rearrange("(p f) c -> p f c", f=EF), fields[:, :, :]).then_inc(saved, 16)
                sp.dma_start(slots.rearrange("(p f) -> p f", f=EF), slot[:, :]).then_inc(saved, 16)
                sp.wait_ge(saved, 32)

            @block.tensor
            def _(pe):
                pe.wait_ge(counted, 1)
                pe.matmul(sums[0:P, 0, 0:TILES], k.before[0:P, 0:P], totals[:, :], start=True, stop=True)
                pe.matmul(sums[:, 1, 0:TILES], k.ones[0:P, :], totals[:, :], start=True, stop=True).then_inc(summed, 1)

            @block.vector
            def _(dve):
                n = 0

                def link(ins):
                    nonlocal n
                    n += 1
                    ins.then_inc(chain, 1)
                    dve.wait_ge(chain, n)

                dve.memset(ones[:, :], 1.0)
                dve.memset(fields[:, :, 3], 0.0)
                dve.wait_ge(loaded, 32)
                link(dve.tensor_copy(d[:, :], ids[:, 0, :]))
                dve.tensor_copy(fields[:, :, 0], d[:, :])
                dve.tensor_copy(fields[:, :, 1], ids[:, 1, :])
                for b in range(TILES):
                    last = dve.tensor_scalar(rank[:, b, :], d[:, :], float(b * P), None, ALU.is_ge)
                link(last)
                for b in range(TILES):
                    last = dve.scalar_tensor_tensor(inside[:, b, :], d[:, :], float((b + 1) * P), rank[:, b, :],
                                                    ALU.is_lt, ALU.mult)
                link(last)
                for b in range(TILES):
                    last = dve.tensor_tensor_scan(rank[:, b, :], ones[:, :], inside[:, b, :], 0.0, ALU.mult, ALU.add)
                link(last)
                dve.tensor_copy(totals[:, :], rank[:, :, EF - 1]).then_inc(counted, 1)
                for b in range(TILES):
                    link(dve.scalar_tensor_tensor(d[:, :], inside[:, b, :], float(-P * b), d[:, :],
                                                  ALU.mult, ALU.add))
                link(dve.tensor_copy(fields[:, :, 2], d[:, :]))
                dve.wait_ge(summed, 1)
                link(dve.tensor_scalar(whole[:, 0, :], sums[:, 1, 0:TILES], float(GROUP - 1), None, ALU.add))
                link(dve.tensor_single_scalar(whole[:, 1, :], whole[:, 0, :], GROUP.bit_length() - 1,
                                              ALU.logical_shift_right))
                link(dve.tensor_copy(small[:, 0, :], whole[:, 1, :]))
                link(dve.tensor_tensor_scan(small[:, 1, :], k.ones[:, 0:TILES], small[:, 0, :], 0.0,
                                            ALU.mult, ALU.add))
                link(dve.tensor_tensor(small[:, 2, :], small[:, 1, :], small[:, 0, :], ALU.subtract))
                link(dve.scalar_tensor_tensor(small[0:P, 3, :], small[0:P, 2, :], float(GROUP), sums[0:P, 0, 0:TILES],
                                              ALU.mult, ALU.add))
                link(dve.memset(place[:, :], -1.0))
                for b in range(TILES):
                    link(dve.scalar_tensor_tensor(term[:, :], rank[:, b, :], small[0:P, 3, b:b + 1], inside[:, b, :],
                                                  ALU.add, ALU.mult))
                    link(dve.tensor_tensor(place[:, :], place[:, :], term[:, :], ALU.add))
                link(dve.tensor_copy(slot[:, :], place[:, :]))
                link(dve.memset(block_f[:, :], 0.0))
                for b in range(1, TILES):
                    link(dve.scalar_tensor_tensor(block_f[:, :], k.iota_f[0:1, 0:GROUPS], small[0:1, 2, b:b + 1],
                                                  block_f[:, :], ALU.is_ge, ALU.add))
                dve.tensor_copy(k.block_of[:, :], block_f[:, :]).then_inc(done, 1)

HEADS, DH = 8, 64
HALF = N // 2
FIRST, SECOND = 3 * P, 2 * P
UNITS = 4


def stage_relu_attention(nc, k, w, xT, attended, attended_dram, meta, slots, records):
    scale = DH ** -0.5
    w_first, w_rest = irrep_rows(w["L0_mix_w_qkv"])
    with ExitStack() as ctx:
        s = Shop(nc, ctx, "attn")
        wv = s.sb("wv", [128, KD, D])
        wqk = s.sb("wqk", [128, 2, KD, 128])
        v = s.sb("v", [P, TILES, D])
        qkT = s.sb("qkT", [128, 2, N])
        probs = s.sb("probs", [P, 2, TILES, HALF])
        rec = s.sb("rec", [P, 2, ECH, REC])
        met = s.sb("met", [P, 2, ECH, 4])
        plc = s.sb("plc", [P, 2, ECH], I32)
        pad = s.sb("pad", [128, 36, REC])
        dots = s.ps("dots", [128, 2, 2, 512])
        proj = s.ps("proj", [128, 2, 512])
        outp = s.ps("outp", [128, 2, 512])
        (v_loaded, w_loaded, v_filled, v_kept, qk_used, proj_filled, proj_kept, dots_filled, first_kept, second_kept,
         out_filled, out_kept, saved, pad_set, padded, edges_in0, edges_in1, merged, scattered0, scattered1) = (s.sem(n) for n in (
             "v_loaded", "w_loaded", "v_filled", "v_kept", "qk_used", "proj_filled", "proj_kept", "dots_filled",
             "first_kept", "second_kept", "out_filled", "out_kept", "saved", "pad_set", "padded", "edges_in0", "edges_in1",
             "merged", "scattered0", "scattered1"))
        edges_in, scattered = (edges_in0, edges_in1), (scattered0, scattered1)
        edges3 = w["edges"].rearrange("(p f) c -> p f c", f=EF)
        meta3 = meta.rearrange("(p f) c -> p f c", f=EF)
        slots2 = slots.rearrange("(p f) -> p f", f=EF)
        DOTS = UNITS * TILES
        with nc.Block() as block:
            @block.sync
            def _(sp):
                sp.dma_start(wv[:, 0, :], w_first[:, 2 * D:3 * D]).then_inc(v_loaded, 16)
                for m in range(3):
                    sp.dma_start(wv[:, 1 + m, :], w_rest[:, m, 2 * D:3 * D]).then_inc(v_loaded, 16)
                with sp.Fori(0, HEADS // 2) as i:
                    sp.wait_ge(qk_used, i + 1)
                    for q in range(2):
                        cols = bass.ds(i * 128 + q * D, 128)
                        sp.dma_start(wqk[:, q, 0, :], w_first[:, cols]).then_inc(w_loaded, 16)
                        for m in range(3):
                            sp.dma_start(wqk[:, q, 1 + m, :], w_rest[:, m, cols]).then_inc(w_loaded, 16)
                sp.wait_ge(out_kept, HEADS * 2 + 2)
                sp.dma_start(tiles_of(attended_dram), attended[:, :, :]).then_inc(saved, 16)
                sp.wait_ge(saved, 16)

            @block.tensor
            def _(pe):
                pe.sem_inc(qk_used, 1)
                pe.wait_ge(v_loaded, 64)
                for t in range(TILES):
                    if t >= 2:
                        pe.wait_ge(v_kept, t - 1)
                    for c in range(KD):
                        last = pe.matmul(proj[0:P, t % 2, :], xT[:, c, t * P:(t + 1) * P], wv[:, c, :],
                                         start=(c == 0), stop=(c == KD - 1))
                    last.then_inc(v_filled, 1)
                pe.wait_ge(v_kept, TILES)
                with pe.Fori(0, HEADS // 2) as i:
                    pe.wait_ge(w_loaded, i * 128 + 128)
                    for q in range(2):
                        for c in range(CHUNKS):
                            n = q * CHUNKS + c
                            pe.wait_ge(proj_kept, i * (2 * CHUNKS) + (n + 1))
                            for r in range(KD):
                                last = pe.matmul(proj[:, n % 2, 0:CH], wqk[:, q, r, :], xT[:, r, c * CH:(c + 1) * CH],
                                                 start=(r == 0), stop=(r == KD - 1))
                            last.then_inc(proj_filled, 1)
                    pe.wait_ge(proj_kept, i * (2 * CHUNKS) + 2 * CHUNKS + 2)
                    pe.sem_inc(qk_used, 1)

                    def scores(u):
                        rows, base = slice(DH * (u // 2), DH * (u // 2 + 1)), HALF * (u % 2)
                        for j in range(TILES):
                            n = u * TILES + j
                            pe.wait_ge(first_kept, i * DOTS + (n + 1))
                            pe.wait_ge(second_kept, i * DOTS + (n + 1))
                            keys = qkT[rows, 1, j * P:(j + 1) * P]
                            pe.matmul(dots[0:P, n % 2, 0, 0:FIRST], keys, qkT[rows, 0, base:base + FIRST],
                                      start=True, stop=True)
                            pe.matmul(dots[0:P, n % 2, 1, 0:SECOND], keys, qkT[rows, 0, base + FIRST:base + HALF],
                                      start=True, stop=True).then_inc(dots_filled, 1)

                    def values(u):
                        pe.wait_ge(first_kept, i * DOTS + ((u + 1) * TILES + 2))
                        pe.wait_ge(second_kept, i * DOTS + ((u + 1) * TILES + 2))
                        pe.wait_ge(out_kept, i * UNITS + (u + 1))
                        for a in range(5):
                            for j in range(TILES):
                                last = pe.matmul(outp[0:P, u % 2, a * DH:(a + 1) * DH],
                                                 probs[:, u % 2, j, a * P:(a + 1) * P],
                                                 v[:, j, bass.ds(i * 128 + DH * (u // 2), DH)],
                                                 start=(j == 0), stop=(j == TILES - 1))
                        last.then_inc(out_filled, 1)

                    for u in range(UNITS):
                        scores(u)
                        if u >= 1:
                            values(u - 1)
                    values(UNITS - 1)

            @block.scalar
            def _(act):
                act.sem_inc(proj_kept, 2)
                act.sem_inc(first_kept, 2)
                for t in range(TILES):
                    act.wait_ge(v_filled, t + 1)
                    act.activation(v[:, t, :], proj[0:P, t % 2, :], ACT.Copy).then_inc(v_kept, 1)
                with act.Fori(0, HEADS // 2) as i:
                    act.wait_ge(out_filled, i * UNITS + 2)
                    for q in range(2):
                        for c in range(CHUNKS):
                            n = q * CHUNKS + c
                            act.wait_ge(proj_filled, i * (2 * CHUNKS) + (n + 1))
                            act.activation(qkT[:, q, c * CH:(c + 1) * CH], proj[:, n % 2, 0:CH],
                                           ACT.Copy).then_inc(proj_kept, 1)
                    for u in range(UNITS):
                        act.wait_ge(out_filled, i * UNITS + (u + 1))
                        for j in range(TILES):
                            n = u * TILES + j
                            act.wait_ge(dots_filled, i * DOTS + (n + 1))
                            act.activation(probs[:, u % 2, j, 0:FIRST], dots[0:P, n % 2, 0, 0:FIRST], ACT.Relu,
                                           scale=scale).then_inc(first_kept, 1)

            @block.vector
            def _(dve):
                dve.sem_inc(second_kept, 2)
                dve.sem_inc(out_kept, 2)
                dve.sem_inc(out_filled, 2)
                with dve.Fori(0, HEADS // 2) as i:
                    def take(u):
                        dve.wait_ge(out_filled, i * UNITS + (u + 3))
                        h = i * 128 + DH * (u // 2)
                        dve.tensor_copy(attended[:, 5 * (u % 2):5 * (u % 2) + 5, bass.ds(h, DH)],
                                        outp[0:P, u % 2, 0:5 * DH].rearrange("p (a d) -> p a d", a=5)
                                        ).then_inc(out_kept, 1)

                    for u in range(UNITS):
                        dve.wait_ge(out_filled, i * UNITS + (u + 1))
                        for j in range(TILES):
                            n = u * TILES + j
                            dve.wait_ge(dots_filled, i * DOTS + (n + 1))
                            dve.tensor_scalar(probs[:, u % 2, j, FIRST:HALF], dots[0:P, n % 2, 1, 0:SECOND],
                                              0.0, scale, ALU.max, ALU.mult).then_inc(second_kept, 1)
                        if u >= 1:
                            take(u - 1)
                    take(UNITS - 1)

            @block.gpsimd
            def _(pool):
                pool.memset(pad[:, :, :], 0.0).then_inc(pad_set, 1)
                pool.wait_ge(pad_set, 1)
                pool.memset(pad[:, :, 38], -1.0).then_inc(pad_set, 1)
                pool.wait_ge(pad_set, 2)
                per = GROUPS * GROUP // 128
                places = records.rearrange("(p f) c -> p f c", f=per)
                for q in range(per // 36):
                    pool.dma_start(places[:, q * 36:(q + 1) * 36, :], pad[:, :, :]).then_inc(padded, 16)
                pool.wait_ge(padded, 16 * (per // 36))
                for c in range(ECHUNKS):
                    b, n = c % 2, c // 2
                    if n >= 1:
                        pool.wait_ge(scattered[b], 16 * ECH * n)
                    for out_, in_ in ((rec[:, b, :, :], edges3), (met[:, b, :, :], meta3), (plc[:, b, :], slots2)):
                        pool.dma_start(out_, in_[:, c * ECH:(c + 1) * ECH]).then_inc(edges_in[b], 16)
                    pool.wait_ge(edges_in[b], 48 * (n + 1))
                    pool.tensor_copy(rec[:, b, :, 36:40], met[:, b, :, :]).then_inc(merged, 1)
                    pool.wait_ge(merged, c + 1)
                    for f in range(ECH):
                        pool.indirect_dma_start(out=records, out_offset=bass.IndirectOffsetOnAxis(
                            ap=plc[:, b, f:f + 1], axis=0), in_=rec[:, b, f, :], in_offset=None).then_inc(scattered[b], 16)
                pool.wait_ge(scattered[0], 16 * ECH * ((ECHUNKS + 1) // 2))
                pool.wait_ge(scattered[1], 16 * ECH * (ECHUNKS // 2))

RING = 3
WD, WS = 384 + 32, 4 * MUL + 384


def stage_edges(nc, k, w, table_d, table_s, records, acc, pairs):
    with ExitStack() as ctx:
        s = Shop(nc, ctx, "edge")
        from_drivers = s.sb("from_drivers", [128, 64])
        from_inner = s.sb("from_inner", [128, 64])
        out_w = s.sb("out_w", [128, 2, D])
        rec = s.sb("rec", [128, RING, GTILES, REC])
        ids = s.sb("ids", [128, RING, GTILES, 2], I32)
        at_d = s.sb("at_d", [128, RING, GTILES, WD])
        at_s = s.sb("at_s", [128, RING, GTILES, WS])
        prod = s.sb("prod", [128, 3, MUL])
        half_sum = s.sb("half_sum", [128, MUL])
        inner = s.sb("inner", [128, RING, GTILES, MUL])
        drivers = s.sb("drivers", [128, GTILES, 64])
        driversT = s.sb("driversT", [128, GROUP])
        innerT = s.sb("innerT", [128, GROUP])
        mag = s.sb("mag", [64, GROUP])
        expd = s.sb("expd", [64, GROUP])
        logd = s.sb("logd", [64, GROUP])
        hidden = s.sb("hidden", [128, RING, GROUP])
        wa_sb = s.sb("wa_sb", [128, 2, D])
        ww = s.sb("ww", [128, 2, D])
        s_scaled = s.sb("s_scaled", [128, 2, D])
        dot = s.sb("dot", [128, 2, 3, MUL])
        vec = s.sb("vec", [128, 2, MUL])
        vec_sh = s.sb("vec_sh", [128, 3, MUL])
        last_part = s.sb("last_part", [128, MUL])
        msg = s.sb("msg", [128, 2, D])
        spread = s.sb("spread", [128, 2, P])
        one_d = s.sb("one_d", [128, 2, P], BF16)
        one_s = s.sb("one_s", [128, 2, N], BF16)
        turn = s.ps("turn", [128, 512])
        pre = s.ps("pre", [64, 512])
        wa = s.ps("wa", [128, 512])
        wb = s.ps("wb", [128, 512])
        sums = s.ps("sums", [128, 512])
        joins = s.ps("joins", [128, 3 * 512])
        (w_in, cleared, scaled, rec_free, ids_set, multiplied, added, inner_set, drivers_set, drivers_turned,
         drivers_kept, inner_turned, inner_kept, pre_filled, mag_set, exp_set, log_set, hidden_set, wa_filled,
         wb_filled, wa_kept, prescaled, dotted, ww_set, vec_set, vec_scaled, parts_set, msg_set, one_set, joined,
         gathered_free, sums_filled, sums_kept, acc_set, pool_passed, pe_passed) = (s.sem(n) for n in (
             "w_in", "cleared", "scaled", "rec_free", "ids_set", "multiplied", "added", "inner_set",
             "drivers_set", "drivers_turned", "drivers_kept", "inner_turned", "inner_kept", "pre_filled",
             "mag_set", "exp_set", "log_set", "hidden_set", "wa_filled", "wb_filled", "wa_kept", "prescaled",
             "dotted", "ww_set", "vec_set", "vec_scaled", "parts_set", "msg_set", "one_set", "joined",
             "gathered_free", "sums_filled", "sums_kept", "acc_set", "pool_passed", "pe_passed"))
        rec_in = [s.sem(f"rec_in{r}") for r in range(RING)]
        d_in = [[s.sem(f"d_in{r}{j}") for j in range(GTILES)] for r in range(RING)]
        s_in = [[s.sem(f"s_in{r}{j}") for j in range(GTILES)] for r in range(RING)]
        G = GTILES
        assert GROUPS % RING == 0

        def groups(eng, group):
            group(0, 0, 0, True, False)
            with eng.Fori(0, GROUPS // RING - 1) as i:
                for u in range(RING):
                    group(i * RING + (u + 1), (u + 1) % RING, i + (u + 1) // RING, False, False)
            for g in range(GROUPS - RING + 1, GROUPS):
                group(g, g % RING, g // RING, False, g == LAST)

        def after(r, i):
            return (r + 1) % RING, i + (r + 1) // RING

        LAST = GROUPS - 1
        with nc.Block() as block:
            @block.sync
            def _(sp):
                sp.wait_ge(cleared, 4)
                sp.dma_start(from_drivers[0:32, 0:32], w["L0_gnn_W_f1"]).then_inc(w_in, 16)
                sp.dma_start(out_w[0:32, 0, :], w["L0_gnn_W_f2"]).then_inc(w_in, 16)
                sp.dma_start(out_w[32:64, 1, :], w["L0_gnn_W_s2"]).then_inc(w_in, 16)
                with sp.Fori(0, GROUPS // RING) as i:
                    for r in range(RING):
                        sp.wait_ge(rec_free, i * RING + (r + 1))
                        sp.dma_start(rec[:, r, :, :].rearrange("p j c -> p (j c)"),
                                     records.rearrange("(g p j) c -> g p (j c)", p=128, j=G)[bass.ds(i * RING + r, 1)]
                                     .rearrange("g p c -> (g p) c")).then_inc(rec_in[r], 16)

            @block.gpsimd
            def _(pool):
                def inner_product(g, r, i, j):
                    T = g * G + j
                    pool.wait_ge(d_in[r][j], i * 16 + 16)
                    pool.wait_ge(s_in[r][j], i * 16 + 16)
                    pool.tensor_tensor(prod[:, :, :].rearrange("p m u -> p (m u)"), at_d[:, r, j, 0:384],
                                       at_s[:, r, j, 512:896], ALU.mult).then_inc(multiplied, 1)
                    pool.wait_ge(multiplied, T + 1)
                    pool.tensor_tensor(half_sum[:, :], prod[:, 0, :], prod[:, 1, :], ALU.add).then_inc(added, 1)
                    pool.wait_ge(added, T + 1)
                    pool.tensor_tensor(inner[:, r, j, :], half_sum[:, :], prod[:, 2, :], ALU.add).then_inc(inner_set, 1)
                    pool.wait_ge(inner_set, T + 1)

                with pool.Fori(0, GROUPS // RING) as i:
                    for r in range(RING):
                        g = i * RING + r
                        pool.wait_ge(rec_in[r], i * 16 + 16)
                        pool.wait_ge(gathered_free, g + 1)
                        pool.sem_inc(pool_passed, 1)
                        pool.tensor_copy(ids[:, r, :, :], rec[:, r, :, 36:38]).then_inc(ids_set, 1)
                        pool.wait_ge(ids_set, g + 1)
                        pool.sem_inc(pool_passed, 1)
                        for j in range(G):
                            pool.indirect_dma_start(
                                out=at_d[:, r, j, :], out_offset=None, in_=table_d,
                                in_offset=bass.IndirectOffsetOnAxis(ap=ids[:, r, j, 0:1], axis=0)).then_inc(d_in[r][j], 16)
                            pool.indirect_dma_start(
                                out=at_s[:, r, j, :], out_offset=None, in_=table_s,
                                in_offset=bass.IndirectOffsetOnAxis(ap=ids[:, r, j, 1:2], axis=0)).then_inc(s_in[r][j], 16)
                        for j in range(G):
                            inner_product(g, r, i, j)

            @block.tensor
            def _(pe):
                pe.sem_inc(joined, 2)
                pe.sem_inc(sums_filled, 2)
                pe.wait_ge(w_in, 48)
                pe.wait_ge(scaled, 1)
                pe.wait_ge(cleared, 8)

                def turns(g, r):
                    pe.wait_ge(inner_set, g * G + G)
                    for j in range(G):
                        done = pe.transpose(turn[:, j * 128:(j + 1) * 128], inner[:, r, j, :], k.ident[:, :])
                    done.then_inc(inner_turned, 1)
                    pe.wait_ge(drivers_set, g + 1)
                    pe.sem_inc(pe_passed, 1)
                    for j in range(G):
                        done = pe.transpose(pre[0:64, j * 128:(j + 1) * 128], drivers[:, j, :], k.ident[:, :])
                    done.then_inc(drivers_turned, 1)

                def hidden_products(g):
                    pe.wait_ge(drivers_kept, g + 1)
                    pe.matmul(pre[:, :], from_drivers[:, :], driversT[:, :], start=True, stop=False)
                    pe.wait_ge(inner_kept, g + 1)
                    pe.matmul(pre[:, :], from_inner[:, :], innerT[:, :], start=False, stop=True).then_inc(pre_filled, 1)

                def weights(g, r, j):
                    T, cols = g * G + j, slice(j * 128, (j + 1) * 128)
                    if j == 0:
                        pe.wait_ge(hidden_set, g + 1)
                    pe.wait_ge(wa_kept, T + 1)
                    pe.matmul(wa[:, :], hidden[:, r, cols], out_w[:, 0, :], start=True, stop=True).then_inc(wa_filled, 1)
                    pe.wait_ge(ww_set, T + 1)
                    pe.matmul(wb[:, :], hidden[:, r, cols], out_w[:, 1, :], start=True, stop=True).then_inc(wb_filled, 1)

                def sum_up(g, j):
                    T = g * G + j
                    if j == 0:
                        pe.wait_ge(sums_kept, g + 1)
                    pe.wait_ge(one_set, T + 1)
                    for c in range(0, N, 512):
                        last = pe.matmul(joins[0:P, c:min(c + 512, N)], one_d[:, j % 2, :],
                                         one_s[:, j % 2, c:min(c + 512, N)], start=(j == 0), stop=(j == G - 1))
                    last.then_inc(joined, 1)
                    pe.wait_ge(msg_set, T + 1)
                    pe.matmul(sums[0:P, :], spread[:, j % 2, :], msg[:, j % 2, :], start=(j == 0),
                              stop=(j == G - 1)).then_inc(sums_filled, 1)

                def group(g, r, i, first, last):
                    r2, _ = after(r, i)
                    for j in range(G):
                        if j + 1 < G:
                            weights(g, r, j + 1)
                        elif not last:
                            weights(g + 1, r2, 0)
                        if j == 0 and not last:
                            turns(g + 1, r2)
                        if j == 1 and not last:
                            hidden_products(g + 1)
                        sum_up(g, j)

                turns(0, 0)
                hidden_products(0)
                weights(0, 0, 0)
                groups(pe, group)

            @block.scalar
            def _(act):
                act.preload_act_table_set(EXP_LN)
                act.sem_inc(wa_kept, 1)

                def take_drivers(r, i):
                    act.wait_ge(rec_in[r], i * 16 + 16)
                    act.activation(drivers[:, :, 0:32], rec[:, r, :, 0:32], ACT.Copy)
                    for j in range(G):
                        act.wait_ge(d_in[r][j], i * 16 + 16)
                    act.activation(drivers[:, :, 32:64], at_d[:, r, :, 384:416], ACT.Copy).then_inc(drivers_set, 1)

                def keep_turned(g):
                    act.wait_ge(inner_turned, g + 1)
                    act.activation(innerT[:, :], turn[:, :], ACT.Copy).then_inc(inner_kept, 1)
                    act.wait_ge(drivers_turned, g + 1)
                    act.activation(driversT[0:64, :], pre[:, :], ACT.Copy).then_inc(drivers_kept, 1)

                def soften(g):
                    act.wait_ge(pre_filled, g + 1)
                    act.activation(mag[:, :], pre[:, :], ACT.Abs).then_inc(mag_set, 1)
                    act.wait_ge(mag_set, g + 1)
                    act.activation(expd[:, :], mag[:, :], ACT.Exp, scale=-1.0).then_inc(exp_set, 1)
                    act.wait_ge(exp_set, g + 1)
                    act.activation(logd[:, :], expd[:, :], ACT.Ln, scale=0.5, bias=k.half[0:64, 0:1]).then_inc(log_set, 1)

                def prescale(g, r, i, j):
                    act.wait_ge(s_in[r][j], i * 16 + 16)
                    act.activation(s_scaled[:, j % 2, :], at_s[:, r, j, 0:D], ACT.Copy, scale=rec[:, r, j, 32:33])
                    act.activation(dot[:, j % 2, 0, :], at_s[:, r, j, MUL:2 * MUL], ACT.Copy,
                                   scale=rec[:, r, j, 33:34]).then_inc(prescaled, 1)
                    act.wait_ge(wa_filled, g * G + (j + 1))
                    act.activation(wa_sb[:, j % 2, :], wa[:, :], ACT.Copy).then_inc(wa_kept, 1)

                def scale_vectors(g, r, j):
                    act.wait_ge(vec_set, g * G + (j + 1))
                    for m in range(3):
                        last = act.activation(vec_sh[:, m, :], vec[:, j % 2, :], ACT.Copy, scale=rec[:, r, j, 33 + m:34 + m])
                    last.then_inc(vec_scaled, 1)

                def group(g, r, i, first, last):
                    r2, i2 = after(r, i)
                    for j in range(G):
                        if j == 0 and not last:
                            take_drivers(r2, i2)
                        scale_vectors(g, r, j)
                        if j + 1 < G:
                            prescale(g, r, i, j + 1)
                        elif not last:
                            prescale(g + 1, r2, i2, 0)
                        if j == 0 and not last:
                            keep_turned(g + 1)
                        if j == 1 and not last:
                            soften(g + 1)

                take_drivers(0, 0)
                keep_turned(0)
                soften(0)
                prescale(0, 0, 0, 0)
                groups(act, group)

            @block.vector
            def _(dve):
                for out_, value in ((from_drivers, 0.0), (out_w, 0.0), (from_inner, 0.0), (driversT, 0.0)):
                    dve.memset(out_[:], value).then_inc(cleared, 1)
                dve.memset(hidden[:, :, :], 0.0).then_inc(cleared, 1)
                dve.memset(pairs[:, :, :], 0.0).then_inc(acc_set, 1)
                dve.wait_ge(cleared, 4)
                dve.tensor_copy(from_drivers[32:64, 32:64], k.ident[32:64, 32:64]).then_inc(cleared, 1)
                dve.tensor_copy(from_inner[:, 32:64], k.s1_pair[:, :]).then_inc(cleared, 1)
                dve.wait_ge(w_in, 48)
                dve.tensor_scalar(out_w[32:64, 1, 384:512], out_w[32:64, 1, 384:512], 3.0 ** -0.5, None,
                                  ALU.mult).then_inc(scaled, 1)
                dve.sem_inc(cleared, 1)
                dve.sem_inc(rec_free, RING)
                dve.sem_inc(gathered_free, RING)
                dve.sem_inc(ww_set, 1)
                dve.sem_inc(sums_kept, 1)

                def soften(g, r):
                    dve.wait_ge(log_set, g + 1)
                    dve.scalar_tensor_tensor(hidden[0:64, r, :], pre[:, :], 0.0, logd[:, :], ALU.max,
                                             ALU.add).then_inc(hidden_set, 1)

                def ones(g, r, j):
                    T, b, dl = g * G + j, j % 2, rec[:, r, j, 38:39]
                    dve.wait_ge(joined, T + 1)
                    dve.tensor_scalar(one_d[:, b, :], k.iota_h[:, 0:P], dl, None, ALU.is_equal)
                    dve.tensor_scalar(one_s[:, b, :], k.iota_h[:, :], rec[:, r, j, 37:38], None,
                                      ALU.is_equal).then_inc(one_set, 1)
                    dve.wait_ge(sums_filled, T + 1)
                    dve.tensor_scalar(spread[:, b, :], k.iota_f[:, 0:P], dl, None, ALU.is_equal)

                def evict(g):
                    block_no = dve.value_load(k.block_of[0:1, bass.ds(g, 1)], min_val=0, max_val=TILES - 1)
                    dve.wait_ge(sums_filled, g * G + (G + 2))
                    dve.wait_ge(acc_set, g + 1)
                    a = acc[:, bass.ds(block_no, 1), :].rearrange("p t c -> p (t c)")
                    q = pairs[:, bass.ds(block_no, 1), :].rearrange("p t c -> p (t c)")
                    dve.tensor_tensor(a, a, sums[0:P, :], ALU.add)
                    dve.tensor_tensor(q, q, joins[0:P, 0:N], ALU.add).then_inc(acc_set, 1)
                    dve.wait_ge(acc_set, g + 2)
                    dve.sem_inc(sums_kept, 1)

                def group(g, r, i, first, last):
                    for j in range(G):
                        T, b = g * G + j, j % 2
                        ones(g, r, j)
                        dve.wait_ge(prescaled, T + 1)
                        for m in range(1, 3):
                            dve.scalar_tensor_tensor(dot[:, b, m, :], at_s[:, r, j, (1 + m) * MUL:(2 + m) * MUL],
                                                     rec[:, r, j, 33 + m:34 + m], dot[:, b, m - 1, :],
                                                     ALU.mult, ALU.add).then_inc(dotted, 1)
                            if m == 1:
                                dve.wait_ge(dotted, 2 * T + 1)
                        dve.wait_ge(wa_kept, T + 2)
                        dve.wait_ge(wb_filled, T + 1)
                        dve.tensor_tensor(ww[:, b, :], wb[:, :], wa_sb[:, b, :], ALU.mult).then_inc(ww_set, 1)
                        if j == 0 and not first:
                            evict(g - 1)
                        dve.wait_ge(ww_set, T + 2)
                        dve.tensor_tensor(vec[:, b, :], ww[:, b, MUL:2 * MUL], at_s[:, r, j, 0:MUL],
                                          ALU.mult).then_inc(vec_set, 1)
                        dve.wait_ge(dotted, 2 * T + 2)
                        dve.tensor_tensor(last_part[:, :], ww[:, b, 384:512], dot[:, b, 2, :], ALU.mult)
                        dve.tensor_tensor(msg[:, b, 0:MUL], ww[:, b, 0:MUL], s_scaled[:, b, 0:MUL],
                                          ALU.mult).then_inc(parts_set, 1)
                        dve.tensor_tensor(msg[:, b, MUL:D].rearrange("p (m u) -> p m u", m=3),
                                          s_scaled[:, b, MUL:D].rearrange("p (m u) -> p m u", m=3),
                                          ww[:, b, 256:384].unsqueeze(1).to_broadcast([128, 3, MUL]),
                                          ALU.mult).then_inc(parts_set, 1)
                        dve.wait_ge(parts_set, 2 * T + 1)
                        dve.tensor_tensor(msg[:, b, 0:MUL], msg[:, b, 0:MUL], last_part[:, :], ALU.add)
                        dve.wait_ge(parts_set, 2 * T + 2)
                        dve.wait_ge(vec_scaled, T + 1)
                        dve.tensor_tensor(msg[:, b, MUL:D], msg[:, b, MUL:D], vec_sh[:, :, :].rearrange("p m u -> p (m u)"),
                                          ALU.add).then_inc(msg_set, 1)
                        if j == 2 and not last:
                            soften(g + 1, (r + 1) % RING)
                    dve.wait_ge(msg_set, g * G + G)
                    dve.sem_inc(rec_free, 1)
                    dve.sem_inc(gathered_free, 1)

                soften(0, 0)
                groups(dve, group)
                evict(LAST)


def stage_irreps_out(nc, k, w, acc, x, x_dram):
    with ExitStack() as ctx:
        s = Shop(nc, ctx, "irout")
        o0, o1 = s.sb("o0", [128, MUL]), s.sb("o1", [128, MUL])
        b_o0 = s.sb("b_o0", [P, MUL])
        accT = s.sb("accT", [128, 2, KD, P])
        turn = s.ps("turn", [128, 2, 512])
        outp = s.ps("outp", [128, 2, 512])
        loaded, turned, kept, filled, added, biased = (
            s.sem(n) for n in ("loaded", "turned", "kept", "filled", "added", "biased"))
        with nc.Block() as block:
            @block.sync
            def _(sp):
                sp.dma_start(x[:, :, :], tiles_of(x_dram)).then_inc(loaded, 16)
                sp.dma_start(o0[:, :], w["L0_gnn_W_o0"]).then_inc(loaded, 16)
                sp.dma_start(o1[:, :], w["L0_gnn_W_o1"]).then_inc(loaded, 16)
                sp.dma_start(b_o0[:, :], row(w["L0_gnn_b_o0"], P)).then_inc(loaded, 16)

            @block.tensor
            def _(pe):
                def turn_tile(t):
                    if t >= 2:
                        pe.wait_ge(kept, t - 1)
                    for c in range(KD):
                        last = pe.transpose(turn[:, t % 2, c * P:(c + 1) * P], acc[:, t, c * 128:(c + 1) * 128],
                                            k.ident[0:P, 0:P])
                    last.then_inc(turned, 1)

                turn_tile(0)
                pe.wait_ge(loaded, 64)
                for t in range(TILES):
                    if t + 1 < TILES:
                        turn_tile(t + 1)
                    pe.wait_ge(kept, t + 1)
                    if t >= 2:
                        pe.wait_ge(added, t - 1)
                    for c in range(KD):
                        last = pe.matmul(outp[0:P, t % 2, c * MUL:(c + 1) * MUL], accT[:, t % 2, c, :],
                                         o0[:, :] if c == 0 else o1[:, :], start=True, stop=True)
                    last.then_inc(filled, 1)

            @block.scalar
            def _(act):
                for t in range(TILES):
                    act.wait_ge(turned, t + 1)
                    if t >= 2:
                        act.wait_ge(filled, t - 1)
                    act.activation(accT[:, t % 2, :, :], turn[:, t % 2, 0:KD * P].rearrange("p (c n) -> p c n", c=KD),
                                   ACT.Copy).then_inc(kept, 1)

            @block.vector
            def _(dve):
                dve.wait_ge(loaded, 64)
                for t in range(TILES):
                    dve.wait_ge(filled, t + 1)
                    dve.tensor_tensor(x[:, t, 0:MUL], x[:, t, 0:MUL], outp[0:P, t % 2, 0:MUL], ALU.add)
                    v = x[:, t, MUL:D].rearrange("p (u m) -> p m u", m=3)
                    dve.tensor_tensor(v, v, outp[0:P, t % 2, MUL:D].rearrange("p (m u) -> p m u", m=3),
                                      ALU.add).then_inc(added, 1)
                dve.wait_ge(added, TILES)
                for t in range(TILES):
                    dve.tensor_tensor(x[:, t, 0:MUL], x[:, t, 0:MUL], b_o0[:, :], ALU.add).then_inc(biased, 1)
                dve.wait_ge(biased, TILES)


def stage_linear(nc, k, tag, aT, weight, bias, x):
    with ExitStack() as ctx:
        s = Shop(nc, ctx, tag)
        wt = s.sb("wt", [128, KD, D])
        b = s.sb("b", [P, D])
        outp = s.ps("outp", [128, 2, 512])
        loaded, filled, added, biased = (s.sem(n) for n in ("loaded", "filled", "added", "biased"))
        with nc.Block() as block:
            @block.sync
            def _(sp):
                sp.dma_start(wt[:, :, :], weight.rearrange("(c p) n -> p c n", p=128)).then_inc(loaded, 16)
                if bias is not None:
                    sp.dma_start(b[:, :], row(bias, P)).then_inc(loaded, 16)

            @block.tensor
            def _(pe):
                pe.wait_ge(loaded, 16 if bias is None else 32)
                for t in range(TILES):
                    if t >= 2:
                        pe.wait_ge(added, t - 1)
                    for c in range(KD):
                        last = pe.matmul(outp[0:P, t % 2, :], aT[:, c, t * P:(t + 1) * P], wt[:, c, :],
                                         start=(c == 0), stop=(c == KD - 1))
                    last.then_inc(filled, 1)

            @block.vector
            def _(dve):
                for t in range(TILES):
                    dve.wait_ge(filled, t + 1)
                    dve.tensor_tensor(x[:, t, :], x[:, t, :], outp[0:P, t % 2, :], ALU.add).then_inc(added, 1)
                    if bias is not None:
                        dve.wait_ge(added, t + 1)
                        dve.tensor_tensor(x[:, t, :], x[:, t, :], b[:, :], ALU.add).then_inc(biased, 1)


def stage_shared_hidden(nc, k, w, xT, hT):
    with ExitStack() as ctx:
        s = Shop(nc, ctx, "shared")
        w1, w3 = s.sb("w1", [128, KD, D]), s.sb("w3", [128, KD, D])
        e = s.sb("e", [128, 2, CH])
        pair = s.ps("pair", [128, 2, 512])
        loaded, filled, exped, chain, used = (s.sem(n) for n in ("loaded", "filled", "exped", "chain", "used"))
        jobs = [(q, c) for q in range(KD) for c in range(CHUNKS)]
        with nc.Block() as block:
            @block.sync
            def _(sp):
                sp.dma_start(w1[:, :, :], w["L0_ffn_sw1"].rearrange("(c p) n -> p c n", p=128)).then_inc(loaded, 16)
                sp.dma_start(w3[:, :, :], w["L0_ffn_sw3"].rearrange("(c p) n -> p c n", p=128)).then_inc(loaded, 16)

            @block.tensor
            def _(pe):
                pe.wait_ge(loaded, 32)
                for n, (q, c) in enumerate(jobs):
                    if n >= 2:
                        pe.wait_ge(used, n - 1)
                    for h, wt in enumerate((w1, w3)):
                        for r in range(KD):
                            last = pe.matmul(pair[:, n % 2, h * CH:(h + 1) * CH], wt[:, r, q * 128:(q + 1) * 128],
                                             xT[:, r, c * CH:(c + 1) * CH], start=(r == 0), stop=(r == KD - 1))
                    last.then_inc(filled, 1)

            @block.scalar
            def _(act):
                act.preload_act_table_set(EXP_LN)
                for n in range(len(jobs)):
                    act.wait_ge(filled, n + 1)
                    if n >= 2:
                        act.wait_ge(used, n - 1)
                    act.activation(e[:, n % 2, :], pair[:, n % 2, 0:CH], ACT.Exp, scale=-1.0).then_inc(exped, 1)

            @block.vector
            def _(dve):
                m = 0

                def link(ins):
                    nonlocal m
                    m += 1
                    ins.then_inc(chain, 1)
                    dve.wait_ge(chain, m)

                for n, (q, c) in enumerate(jobs):
                    dve.wait_ge(exped, n + 1)
                    g, out = e[:, n % 2, :], hT[:, q, c * CH:(c + 1) * CH]
                    link(dve.tensor_scalar(g, g, 1.0, None, ALU.add))
                    link(dve.reciprocal(g, g))
                    link(dve.tensor_tensor(out, pair[:, n % 2, 0:CH], g, ALU.mult))
                    dve.tensor_tensor(out, pair[:, n % 2, CH:2 * CH], out, ALU.mult).then_inc(used, 1)


EXPERTS, HID, CAP = 64, 256, 1024
STILES = 84
MRING = 4
assert STILES >= (2 * N + EXPERTS * 127) // 128 and STILES % MRING == 0


def stage_route(nc, k, w, xT, slots, weights, weight_rows, token_rows, tokens_dram):
    W = TILES * EXPERTS
    with ExitStack() as ctx:
        s = Shop(nc, ctx, "route")
        gate = s.sb("gate", [128, KD, EXPERTS])
        logits = s.sb("logits", [P, TILES, EXPERTS])
        best = s.sb("best", [P, TILES, 8])
        best_at = s.sb("best_at", [P, TILES, 8], mybir.dt.uint32)
        best_f = s.sb("best_f", [P, TILES, 2])
        hot = s.sb("hot", [P, 2, TILES, EXPERTS])
        count = s.sb("count", [P, TILES, EXPERTS])
        before = s.sb("before", [P, TILES + 1, EXPERTS])
        place = s.sb("place", [P, TILES, EXPERTS])
        rank = s.sb("rank", [P, TILES, EXPERTS])
        term = s.sb("term", [P, TILES, EXPERTS])
        whole = s.sb("whole", [128, 2, EXPERTS], I32)
        small = s.sb("small", [128, 3, EXPERTS])
        compare = s.sb("compare", [128, STILES, EXPERTS])
        of_tile = s.sb("of_tile", [128, 2, STILES])
        slot_f = s.sb("slot_f", [P, TILES, 2])
        pos_f = s.sb("pos_f", [P, TILES, 2])
        sig = s.sb("sig", [P, TILES, 2])
        sig_sum = s.sb("sig_sum", [P, TILES])
        token = s.sb("token", [P, TILES])
        none = s.sb("none", [STILES, 128])
        listed = s.sb("listed", [STILES, 128])
        lg = s.ps("lg", [128, 2, 512])
        rk = s.ps("rk", [128, 2, 512])
        tot = s.ps("tot", [128, 512])
        (loaded, scored, chain, counted, ranked, exp_asked, exped, placed, zeroed, emptied, scattered, listed_in, turned,
         written, numbered) = (s.sem(n) for n in (
             "loaded", "scored", "chain", "counted", "ranked", "exp_asked", "exped", "placed", "zeroed", "emptied",
             "scattered", "listed_in", "turned", "written", "numbered"))
        with nc.Block() as block:
            @block.sync
            def _(sp):
                sp.dma_start(gate[:, :, :], w["L0_ffn_gate_w"].rearrange("(c p) n -> p c n", p=128)).then_inc(loaded, 16)
                sp.wait_ge(scattered, 16 * 2 * TILES)
                sp.dma_start(listed[:, :], tokens_dram.rearrange("(i p) o -> i (p o)", p=128)).then_inc(listed_in, 16)

            @block.gpsimd
            def _(pool):
                pool.memset(none[:, :], 0.0).then_inc(zeroed, 1)
                pool.iota(token[:, :], pattern=[[P, TILES]], base=0, channel_multiplier=1,
                          allow_small_or_imprecise_dtypes=True).then_inc(numbered, 1)
                pool.wait_ge(zeroed, 1)
                pool.wait_ge(numbered, 1)
                pool.dma_start(tokens_dram.rearrange("(i p) o -> i (p o)", p=128), none[:, :]).then_inc(emptied, 16)
                pool.wait_ge(emptied, 16)
                pool.wait_ge(placed, 1)
                for t in range(TILES):
                    for q in range(2):
                        pool.indirect_dma_start(out=tokens_dram, out_offset=bass.IndirectOffsetOnAxis(
                            ap=slots[:, t, q:q + 1], axis=0), in_=token[:, t:t + 1], in_offset=None).then_inc(scattered, 16)
                pool.wait_ge(scattered, 16 * 2 * TILES)

            @block.tensor
            def _(pe):
                pe.wait_ge(loaded, 16)
                for t in range(TILES):
                    for c in range(KD):
                        last = pe.matmul(lg[0:P, t // 5, (t % 5) * EXPERTS:(t % 5 + 1) * EXPERTS],
                                         xT[:, c, t * P:(t + 1) * P], gate[:, c, :], start=(c == 0), stop=(c == KD - 1))
                last.then_inc(scored, 1)
                pe.wait_ge(counted, 1)
                for h in range(2):
                    out = rk[0:P, h, 0:5 * EXPERTS]
                    pe.matmul(out, k.before[0:P, 0:P], count[:, 5 * h:5 * h + 5, :].rearrange("p t e -> p (t e)"),
                              start=True, stop=False)
                    pe.matmul(out, k.ones[0:P, 0:P], before[:, 5 * h:5 * h + 5, :].rearrange("p t e -> p (t e)"),
                              start=False, stop=True)
                pe.matmul(tot[:, 0:EXPERTS], k.ones[0:P, :], before[:, TILES, :], start=True, stop=True).then_inc(ranked, 1)
                pe.wait_ge(listed_in, 16)
                pe.transpose(tot[:, 128:128 + STILES], listed[:, :], k.ident[0:STILES, 0:STILES]).then_inc(turned, 1)

            @block.scalar
            def _(act):
                act.wait_ge(exp_asked, 1)
                act.activation(sig[:, :, :], best[:, :, 0:2], ACT.Exp, scale=-1.0).then_inc(exped, 1)

            @block.vector
            def _(dve):
                n = 0

                def link(ins):
                    nonlocal n
                    n += 1
                    ins.then_inc(chain, 1)
                    dve.wait_ge(chain, n)

                dve.wait_ge(scored, 1)
                for h in range(2):
                    last = dve.tensor_copy(logits[:, 5 * h:5 * h + 5, :].rearrange("p t e -> p (t e)"),
                                           lg[0:P, h, 0:5 * EXPERTS])
                link(last)
                for t in range(TILES):
                    last = dve.max(best[:, t, :], logits[:, t, :])
                link(last)
                for t in range(TILES):
                    last = dve.max_index(best_at[:, t, :], best[:, t, :], logits[:, t, :])
                last.then_inc(exp_asked, 1)
                dve.wait_ge(exp_asked, 1)
                link(dve.tensor_copy(best_f[:, :, :], best_at[:, :, 0:2]))
                for t in range(TILES):
                    for q in range(2):
                        last = dve.tensor_scalar(hot[:, q, t, :], k.iota_f[0:P, 0:EXPERTS], best_f[:, t, q:q + 1], None,
                                                 ALU.is_equal)
                link(last)
                link(dve.tensor_tensor(count[:, :, :], hot[:, 0, :, :], hot[:, 1, :, :], ALU.add))
                link(dve.memset(before[:, 0, :], 0.0))
                for t in range(TILES):
                    link(dve.tensor_tensor(before[:, t + 1, :], before[:, t, :], count[:, t, :], ALU.add))
                dve.sem_inc(counted, 1)
                dve.wait_ge(exped, 1)
                link(dve.tensor_scalar(sig[:, :, :], sig[:, :, :], 1.0, None, ALU.add))
                link(dve.reciprocal(sig[:, :, :], sig[:, :, :]))
                link(dve.tensor_tensor(sig_sum[:, :], sig[:, :, 0], sig[:, :, 1], ALU.add))
                link(dve.tensor_scalar(sig_sum[:, :], sig_sum[:, :], 1e-20, None, ALU.add))
                link(dve.reciprocal(sig_sum[:, :], sig_sum[:, :]))
                link(dve.tensor_tensor(sig[:, :, :], sig[:, :, :], sig_sum[:, :].unsqueeze(2).to_broadcast([P, TILES, 2]),
                                       ALU.mult))
                dve.wait_ge(ranked, 1)
                link(dve.tensor_scalar(whole[:, 0, :], tot[:, 0:EXPERTS], 127.0, None, ALU.add))
                link(dve.tensor_single_scalar(whole[:, 1, :], whole[:, 0, :], 7, ALU.logical_shift_right))
                link(dve.tensor_copy(small[:, 0, :], whole[:, 1, :]))
                link(dve.tensor_tensor_scan(small[:, 1, :], k.ones[:, 0:EXPERTS], small[:, 0, :], 0.0, ALU.mult, ALU.add))
                link(dve.tensor_tensor(small[:, 2, :], small[:, 1, :], small[:, 0, :], ALU.subtract))
                for h in range(2):
                    last = dve.tensor_copy(rank[:, 5 * h:5 * h + 5, :].rearrange("p t e -> p (t e)"), rk[0:P, h, 0:5 * EXPERTS])
                link(last)
                link(dve.scalar_tensor_tensor(place[:, :, :], small[0:P, 2, :].unsqueeze(1).to_broadcast([P, TILES, EXPERTS]),
                                              128.0, rank[:, :, :], ALU.mult, ALU.add))
                for q in range(2):
                    link(dve.tensor_tensor(term[:, :, :], hot[:, q, :, :], place[:, :, :], ALU.mult))
                    link(dve.tensor_reduce(slot_f[:, :, q], term[:, :, :], AX.X, ALU.add))
                    link(dve.tensor_tensor(term[:, :, :], hot[:, q, :, :], rank[:, :, :], ALU.mult))
                    link(dve.tensor_reduce(pos_f[:, :, q], term[:, :, :], AX.X, ALU.add))
                dve.tensor_copy(slots[:, :, :], slot_f[:, :, :]).then_inc(placed, 1)
                link(dve.tensor_scalar(pos_f[:, :, :], pos_f[:, :, :], float(CAP), 2.5, ALU.is_lt, ALU.mult))
                link(dve.tensor_tensor(weights[:, :, :], sig[:, :, :], pos_f[:, :, :], ALU.mult))
                link(dve.tensor_tensor(compare[:, :, :], k.iota_f[:, 0:STILES].unsqueeze(2).to_broadcast([128, STILES, EXPERTS]),
                                       small[:, 2, :].unsqueeze(1).to_broadcast([128, STILES, EXPERTS]), ALU.is_ge))
                link(dve.tensor_reduce(of_tile[:, 0, :], compare[:, :, :], AX.X, ALU.add))
                link(dve.tensor_scalar(of_tile[:, 0, :], of_tile[:, 0, :], 128.0, k.part_f[:, 0:1], ALU.mult, ALU.add))
                link(dve.tensor_scalar(of_tile[:, 1, :], k.iota_f[:, 0:STILES], small[:, 1, EXPERTS - 1:EXPERTS],
                                       float(EXPERTS * 128), ALU.is_ge, ALU.mult))
                link(dve.tensor_tensor(of_tile[:, 0, :], of_tile[:, 0, :], of_tile[:, 1, :], ALU.add))
                link(dve.tensor_scalar(weight_rows[:, :], of_tile[:, 0, :], -128.0, None, ALU.add))
                dve.wait_ge(turned, 1)
                link(dve.tensor_copy(token_rows[:, :], tot[:, 128:128 + STILES]))


def stage_experts(nc, k, w, weight_rows, token_rows, xn_dram, y_dram):
    HC = HID // 128
    mats = (w["L0_ffn_w1"].rearrange("e (p c) h -> (e p) (c h)", p=128),
            w["L0_ffn_w3"].rearrange("e (p c) h -> (e p) (c h)", p=128),
            w["L0_ffn_w2"].rearrange("e (p c) d -> (e p) (c d)", p=128))
    R = MRING
    with ExitStack() as ctx:
        s = Shop(nc, ctx, "experts")
        rows = s.sb("rows", [128, R, 2], I32)
        mat = s.sb("mat", [128, R, 3, 1024])
        xg = s.sb("xg", [128, R, D])
        xgT = s.sb("xgT", [128, 2, KD, 128])
        e = s.sb("e", [128, 2, HID])
        hT = s.sb("hT", [128, 2, HID])
        y = s.sb("y", [128, 2, D])
        turn = s.ps("turn", [128, 2, 512])
        hid = s.ps("hid", [128, 2, 512])
        outp = s.ps("outp", [128, 2, 512])
        (rows_set, turned, turn_kept, filled, exped, plus_one, inverted, gated, hidden_set, out_filled,
         y_set, pool_passed) = (s.sem(n) for n in (
             "rows_set", "turned", "turn_kept", "filled", "exped", "plus_one", "inverted",
             "gated", "hidden_set", "out_filled", "y_set", "pool_passed"))
        x_in = [s.sem(f"x_in{r}") for r in range(R)]
        m_in = [[s.sem(f"m_in{r}{q}") for q in range(3)] for r in range(R)]
        y_out = [s.sem(f"y_out{b}") for b in range(2)]

        def turns(eng, step):
            with eng.Fori(0, STILES // R - 1) as i:
                for u in range(R):
                    step(i * R + u, u, i, True, True)
            i = STILES // R - 1
            for u in range(R):
                step(i * R + u, u, i, u < R - 1, False)

        with nc.Block() as block:
            @block.gpsimd
            def _(pool):
                with pool.Fori(0, STILES // R) as i:
                    for r in range(R):
                        pool.wait_ge(rows_set, i * R + (r + 1))
                        pool.sem_inc(pool_passed, 1)
                        pool.indirect_dma_start(out=xg[:, r, :], out_offset=None, in_=xn_dram,
                                                in_offset=bass.IndirectOffsetOnAxis(ap=rows[:, r, 0:1], axis=0)
                                                ).then_inc(x_in[r], 16)
                        for q in range(3):
                            pool.indirect_dma_start(out=mat[:, r, q, :], out_offset=None, in_=mats[q],
                                                    in_offset=bass.IndirectOffsetOnAxis(ap=rows[:, r, 1:2], axis=0),
                                                    bounds_check=EXPERTS * 128 - 1, oob_is_err=False
                                                    ).then_inc(m_in[r][q], 16)

            @block.sync
            def _(sp):
                out = y_dram.rearrange("(i p) d -> p i d", p=128)
                with sp.Fori(0, STILES // 2) as i:
                    for b in range(2):
                        sp.wait_ge(y_set, i * 2 + (b + 3))
                        sp.dma_start(out[:, bass.ds(i * 2 + b, 1), :].rearrange("p i d -> p (i d)"),
                                     y[:, b, :]).then_inc(y_out[b], 16)
                for b in range(2):
                    sp.wait_ge(y_out[b], 16 * (STILES // 2) + 16)

            @block.tensor
            def _(pe):
                def hidden(n, r, i):
                    b, lap = r % 2, i * 16 + 16
                    pe.wait_ge(x_in[r], lap)
                    pe.wait_ge(turn_kept, n + 1)
                    for c in range(KD):
                        last = pe.transpose(turn[:, b, c * 128:(c + 1) * 128], xg[:, r, c:D:KD], k.ident[:, :])
                    last.then_inc(turned, 1)
                    pe.wait_ge(turn_kept, n + 3)
                    pe.wait_ge(hidden_set, n + 1)
                    for q in range(2):
                        pe.wait_ge(m_in[r][q], lap)
                        for h in range(HC):
                            for c in range(KD):
                                last = pe.matmul(hid[:, b, q * HID + h * 128:q * HID + (h + 1) * 128],
                                                 mat[:, r, q, c * HID + h:(c + 1) * HID:HC], xgT[:, b, c, :],
                                                 start=(c == 0), stop=(c == KD - 1))
                    last.then_inc(filled, 1)

                def step(n, u, i, more, ahead):
                    if more:
                        hidden(n + 1, (u + 1) % R, i + (u + 1) // R)
                    b = u % 2
                    pe.wait_ge(hidden_set, n + 3)
                    pe.wait_ge(y_set, n + 1)
                    pe.wait_ge(m_in[u][2], i * 16 + 16)
                    for h in range(HC):
                        last = pe.matmul(outp[:, b, :], hT[:, b, h * 128:(h + 1) * 128],
                                         mat[:, u, 2, h * D:(h + 1) * D], start=(h == 0), stop=(h == HC - 1))
                    last.then_inc(out_filled, 1)

                hidden(0, 0, 0)
                turns(pe, step)

            @block.scalar
            def _(act):
                act.sem_inc(turn_kept, 2)
                act.sem_inc(y_set, 2)
                for b in range(2):
                    act.sem_inc(y_out[b], 16)
                act.preload_act_table_set(EXP_LN)

                def hidden(n, b):
                    act.wait_ge(turned, n + 1)
                    act.activation(xgT[:, b, :, :].rearrange("p c n -> p (c n)"), turn[:, b, :],
                                   ACT.Copy).then_inc(turn_kept, 1)
                    act.wait_ge(filled, n + 1)
                    act.activation(e[:, b, :], hid[:, b, 0:HID], ACT.Exp, scale=-1.0).then_inc(exped, 1)

                def step(n, u, i, more, ahead):
                    if more:
                        hidden(n + 1, (u + 1) % 2)
                    act.wait_ge(out_filled, n + 1)
                    act.wait_ge(y_out[u % 2], i * (16 * R // 2) + 16 * (u // 2 + 1))
                    act.activation(y[:, u % 2, :], outp[:, u % 2, :], ACT.Copy).then_inc(y_set, 1)

                hidden(0, 0)
                turns(act, step)

            @block.vector
            def _(dve):
                dve.sem_inc(hidden_set, 2)

                def ids(n, r):
                    dve.tensor_copy(rows[:, r, 0:1], token_rows[:, bass.ds(n, 1)])
                    dve.tensor_copy(rows[:, r, 1:2], weight_rows[:, bass.ds(n, 1)]).then_inc(rows_set, 1)

                def hidden(n, b):
                    dve.wait_ge(exped, n + 1)
                    dve.tensor_scalar(e[:, b, :], e[:, b, :], 1.0, None, ALU.add).then_inc(plus_one, 1)
                    dve.wait_ge(plus_one, n + 1)
                    dve.reciprocal(e[:, b, :], e[:, b, :]).then_inc(inverted, 1)
                    dve.wait_ge(inverted, n + 1)
                    dve.tensor_tensor(e[:, b, :], hid[:, b, 0:HID], e[:, b, :], ALU.mult).then_inc(gated, 1)
                    dve.wait_ge(gated, n + 1)
                    dve.tensor_tensor(hT[:, b, :], hid[:, b, HID:2 * HID], e[:, b, :], ALU.mult).then_inc(hidden_set, 1)

                def step(n, u, i, more, ahead):
                    if more:
                        hidden(n + 1, (u + 1) % 2)
                    dve.wait_ge(out_filled, n + 1)
                    if ahead:
                        ids(n + R, u)

                for r in range(R):
                    ids(r, r)
                hidden(0, 0)
                turns(dve, step)


def stage_combine(nc, k, x, slots, weights, y_dram):
    with ExitStack() as ctx:
        s = Shop(nc, ctx, "combine")
        got = s.sb("got", [P, TILES, 2, D])
        fetched, added = s.sem("fetched"), s.sem("added")
        with nc.Block() as block:
            @block.gpsimd
            def _(pool):
                for t in range(TILES):
                    for q in range(2):
                        pool.indirect_dma_start(out=got[:, t, q, :], out_offset=None, in_=y_dram,
                                                in_offset=bass.IndirectOffsetOnAxis(ap=slots[:, t, q:q + 1], axis=0)
                                                ).then_inc(fetched, 16)

            @block.vector
            def _(dve):
                dve.wait_ge(fetched, 16 * 2 * TILES)
                for q in range(2):
                    for t in range(TILES):
                        dve.scalar_tensor_tensor(x[:, t, :], got[:, t, q, :], weights[:, t, q:q + 1], x[:, t, :],
                                                 ALU.mult, ALU.add).then_inc(added, 1)
                    dve.wait_ge(added, TILES * (q + 1))


def stage_graph_convolution(nc, k, w, xT, pairs, x):
    with ExitStack() as ctx:
        s = Shop(nc, ctx, "conv")
        wt = s.sb("wt", [128, KD, D])
        bias = s.sb("bias", [P, D])
        h = s.sb("h", [P, TILES, D])
        deg = s.sb("deg", [P, TILES])
        inv = s.sb("inv", [P, TILES])
        dis = s.sb("dis", [P, TILES])
        tmp = s.sb("tmp", [P, 2, D])
        outp = s.ps("outp", [128, 2, 512])
        loaded, chain, inverted, rooted, filled, kept = (
            s.sem(n) for n in ("loaded", "chain", "inverted", "rooted", "filled", "kept"))
        with nc.Block() as block:
            @block.sync
            def _(sp):
                sp.dma_start(wt[:, :, :], w["L1_gnn_W"].rearrange("(c p) n -> p c n", p=128)).then_inc(loaded, 16)
                sp.dma_start(bias[:, :], row(w["L1_gnn_b"], P)).then_inc(loaded, 16)

            @block.tensor
            def _(pe):
                pe.wait_ge(loaded, 32)
                for t in range(TILES):
                    if t >= 2:
                        pe.wait_ge(kept, t - 1)
                    for c in range(KD):
                        last = pe.matmul(outp[0:P, t % 2, :], xT[:, c, t * P:(t + 1) * P], wt[:, c, :],
                                         start=(c == 0), stop=(c == KD - 1))
                    last.then_inc(filled, 1)
                pe.wait_ge(kept, TILES)
                for t in range(TILES):
                    if t >= 2:
                        pe.wait_ge(kept, TILES + t - 1)
                    for r in range(TILES):
                        last = pe.matmul(outp[0:P, t % 2, :], pairs[:, r, t * P:(t + 1) * P], h[:, r, :],
                                         start=(r == 0), stop=(r == TILES - 1))
                    last.then_inc(filled, 1)

            @block.scalar
            def _(act):
                act.wait_ge(inverted, 1)
                act.activation(dis[:, :], inv[:, :], ACT.Sqrt).then_inc(rooted, 1)

            @block.vector
            def _(dve):
                n = 0

                def link(ins):
                    nonlocal n
                    n += 1
                    ins.then_inc(chain, 1)
                    dve.wait_ge(chain, n)

                for t in range(TILES):
                    last = dve.tensor_reduce(deg[:, t:t + 1], pairs[:, t, :], AX.X, ALU.add)
                link(last)
                link(dve.tensor_scalar(deg[:, :], deg[:, :], 1.0, None, ALU.add))
                dve.reciprocal(inv[:, :], deg[:, :]).then_inc(inverted, 1)
                dve.wait_ge(rooted, 1)
                dve.wait_ge(loaded, 32)
                for t in range(TILES):
                    dve.wait_ge(filled, t + 1)
                    link(dve.tensor_tensor(h[:, t, :], outp[0:P, t % 2, :], bias[:, :], ALU.add))
                    dve.tensor_scalar(h[:, t, :], h[:, t, :], dis[:, t:t + 1], None, ALU.mult).then_inc(kept, 1)
                dve.wait_ge(kept, TILES)
                for t in range(TILES):
                    dve.wait_ge(filled, TILES + t + 1)
                    link(dve.tensor_tensor(tmp[:, t % 2, :], outp[0:P, t % 2, :], h[:, t, :], ALU.add))
                    link(dve.tensor_scalar(tmp[:, t % 2, :], tmp[:, t % 2, :], dis[:, t:t + 1], 0.0, ALU.mult, ALU.max))
                    dve.tensor_tensor(x[:, t, :], x[:, t, :], tmp[:, t % 2, :], ALU.add).then_inc(kept, 1)


FEATURES, EPS = 266, 1e-4
FCH = ((0, 89), (89, 178), (178, 266))
VW = DH + 1


def project_pair(pe, bank, kept, filled, base, wt, xT):
    for c in range(CHUNKS):
        pe.wait_ge(kept, base + (c + 1))
        for r in range(KD):
            last = pe.matmul(bank[:, (c + 0) % 2, 0:CH], wt[:, r, :], xT[:, r, c * CH:(c + 1) * CH],
                             start=(r == 0), stop=(r == KD - 1))
        last.then_inc(filled, 1)


def stage_key_maximum(nc, k, w, xT, v, kT_all, top):
    with ExitStack() as ctx:
        s = Shop(nc, ctx, "keymax")
        wv, wk = s.sb("wv", [128, KD, D]), s.sb("wk", [128, KD, D])
        projT = s.sb("projT", [128, FEATURES])
        most = s.sb("most", [P, HEADS * TILES])
        one = s.sb("one", [128, 4])
        flat = s.sb("flat", [1, 128])
        bank = s.ps("bank", [128, 2, 512])
        feat = s.ps("feat", [128, 4, 512])
        tail = s.ps("tail", [128, 512])
        (loaded, v_filled, v_kept, filled, kept, feat_filled, feat_read, chain, asked, answered) = (s.sem(n) for n in (
            "loaded", "v_filled", "v_kept", "filled", "kept", "feat_filled", "feat_read", "chain", "asked", "answered"))
        with nc.Block() as block:
            @block.sync
            def _(sp):
                sp.dma_start(wv[:, :, :], w["L1_mix_Wv"].rearrange("(c p) n -> p c n", p=128)).then_inc(loaded, 16)
                sp.dma_start(wk[:, :, :], w["L1_mix_Wk"].rearrange("(c p) n -> p c n", p=128)).then_inc(loaded, 16)
                for h in range(2):
                    sp.dma_start(projT[h * DH:(h + 1) * DH, :], w["L1_mix_proj"]).then_inc(loaded, 16)

            @block.tensor
            def _(pe):
                pe.wait_ge(loaded, 64)
                for t in range(TILES):
                    if t >= 2:
                        pe.wait_ge(v_kept, t - 1)
                    for c in range(KD):
                        last = pe.matmul(bank[0:P, t % 2, :], xT[:, c, t * P:(t + 1) * P], wv[:, c, :],
                                         start=(c == 0), stop=(c == KD - 1))
                    last.then_inc(v_filled, 1)
                pe.wait_ge(v_kept, TILES)
                for p in range(HEADS // 2):
                    for c in range(CHUNKS):
                        n = p * CHUNKS + c
                        if n >= 2:
                            pe.wait_ge(kept, n - 1)
                        for r in range(KD):
                            last = pe.matmul(bank[:, n % 2, 0:CH], wk[:, r, p * 128:(p + 1) * 128],
                                             xT[:, r, c * CH:(c + 1) * CH], start=(r == 0), stop=(r == KD - 1))
                        last.then_inc(filled, 1)
                for p in range(HEADS // 2):
                    pe.wait_ge(kept, CHUNKS * (p + 1))
                    for h in range(2):
                        for t in range(TILES):
                            n = (p * 2 + h) * TILES + t
                            if n >= 4:
                                pe.wait_ge(feat_read, n - 3)
                            pe.matmul(feat[0:P, n % 4, 0:FEATURES], kT_all[h * DH:(h + 1) * DH, p, t * P:(t + 1) * P],
                                      projT[h * DH:(h + 1) * DH, :], start=True, stop=True).then_inc(feat_filled, 1)
                pe.wait_ge(asked, 1)
                pe.transpose(tail[0:1, 0:P], one[0:P, 0:1], k.ident[0:P, 0:P]).then_inc(answered, 1)
                pe.wait_ge(asked, 2)
                pe.matmul(tail[:, 256:257], k.ones[0:1, :], one[0:1, 1:2], start=True, stop=True).then_inc(answered, 1)

            @block.scalar
            def _(act):
                for t in range(TILES):
                    act.wait_ge(v_filled, t + 1)
                    act.activation(v[:, t, :, 0:DH], bank[0:P, t % 2, :].rearrange("p (h d) -> p h d", h=HEADS),
                                   ACT.Copy).then_inc(v_kept, 1)
                for p in range(HEADS // 2):
                    for c in range(CHUNKS):
                        n = p * CHUNKS + c
                        act.wait_ge(filled, n + 1)
                        act.activation(kT_all[:, p, c * CH:(c + 1) * CH], bank[:, n % 2, 0:CH], ACT.Copy).then_inc(kept, 1)

            @block.vector
            def _(dve):
                dve.memset(v[:, :, :, DH], 1.0).then_inc(chain, 1)
                for n in range(HEADS * TILES):
                    dve.wait_ge(feat_filled, n + 1)
                    dve.tensor_reduce(most[:, n:n + 1], feat[0:P, n % 4, 0:FEATURES], AX.X, ALU.max).then_inc(feat_read, 1)
                dve.wait_ge(feat_read, HEADS * TILES)
                dve.tensor_reduce(one[0:P, 0:1], most[:, :], AX.X, ALU.max).then_inc(asked, 1)
                dve.wait_ge(answered, 1)
                dve.tensor_reduce(one[0:1, 1:2], tail[0:1, 0:P], AX.X, ALU.max).then_inc(asked, 1)
                dve.wait_ge(answered, 2)
                dve.tensor_copy(top[:, :], tail[:, 256:257]).then_inc(chain, 1)
                dve.wait_ge(chain, 2)


def stage_random_features(nc, k, w, xT, v, kT_all, top, attended):
    norm = DH ** -0.25
    ratio = FEATURES ** -0.5
    with ExitStack() as ctx:
        s = Shop(nc, ctx, "feat")
        wq = s.sb("wq", [128, KD, 128])
        projT = s.sb("projT", [128, FEATURES])
        qkT = s.sb("qkT", [128, 2, N])
        square = s.sb("square", [128, 2, N])
        diag = s.sb("diag", [P, 2, TILES, 2])
        halves = s.sb("halves", [128, 2])
        kbias = s.sb("kbias", [P, TILES, 2])
        qbias = s.sb("qbias", [P, 2, TILES])
        most = s.sb("most", [P, 2, TILES])
        expd = s.sb("expd", [P, 3, FEATURES])
        mapped = s.sb("mapped", [P, 3, FEATURES])
        context = s.sb("context", [128, 2, 3, VW])
        turned_sb = s.sb("turned_sb", [128, 2, 3, P])
        inv = s.sb("inv", [P, 2])
        top_n = s.sb("top_n", [128, 1])
        bank = s.ps("bank", [128, 2, 512])
        feat = s.ps("feat", [128, 2, 512])
        ctxp = s.ps("ctxp", [128, 512])
        turn = s.ps("turn", [128, 2, 512])
        outp = s.ps("outp", [128, 512])
        (w_in, proj_in, filled, kept, squared, diag_filled, diag_set, feat_filled, peaked, bias_set, exped, mapped_set,
         mapped_used, ctx_filled, ctx_kept, turn_filled, turn_kept, out_filled, out_kept, inverted, top_set,
         diag_read) = (s.sem(n) for n in (
             "w_in", "proj_in", "filled", "kept", "squared", "diag_filled", "diag_set", "feat_filled", "peaked",
             "bias_set", "exped", "mapped_set", "mapped_used", "ctx_filled", "ctx_kept", "turn_filled", "turn_kept",
             "out_filled", "out_kept", "inverted", "top_set", "diag_read"))
        wq_dram = w["L1_mix_Wq"].rearrange("(c p) n -> p c n", p=128)
        JOBS = 4 * TILES
        with nc.Block() as block:
            @block.sync
            def _(sp):
                for h in range(2):
                    sp.dma_start(projT[h * DH:(h + 1) * DH, :], w["L1_mix_proj"]).then_inc(proj_in, 16)
                with sp.Fori(0, HEADS // 2) as i:
                    sp.wait_ge(out_filled, i * (2 * TILES) + 2)
                    sp.dma_start(wq[:, :, :], wq_dram[:, :, bass.ds(i * 128, 128)]).then_inc(w_in, 16)

            @block.tensor
            def _(pe):
                pe.wait_ge(proj_in, 32)
                pe.wait_ge(top_set, 5)
                pe.sem_inc(mapped_used, 3)
                pe.sem_inc(out_filled, 2)
                with pe.Fori(0, HEADS // 2) as i:
                    pe.wait_ge(w_in, i * 16 + 16)
                    project_pair(pe, bank, kept, filled, i * (CHUNKS + 1), wq, xT)
                    pe.wait_ge(squared, i + 1)
                    pe.wait_ge(out_kept, i * (2 * TILES) + 1)
                    for q in range(2):
                        for t in range(TILES):
                            c = 128 + (q * TILES + t) * 2
                            last = pe.matmul(outp[0:P, c:c + 2], square[:, q, t * P:(t + 1) * P], halves[:, :],
                                             start=True, stop=True)
                    last.then_inc(diag_filled, 1)

                    def features(n):
                        h, q, t = n // (2 * TILES), 1 - (n // TILES) % 2, n % TILES
                        pe.wait_ge(exped, i * JOBS + (n + 1))
                        pe.matmul(feat[0:P, n % 2, 0:FEATURES], qkT[h * DH:(h + 1) * DH, q, t * P:(t + 1) * P],
                                  projT[h * DH:(h + 1) * DH, :], start=True, stop=True).then_inc(feat_filled, 1)

                    def use(n):
                        h, q, t = n // (2 * TILES), 1 - (n // TILES) % 2, n % TILES
                        m = h * TILES + t
                        pe.wait_ge(mapped_set, i * JOBS + (n + 4))
                        if q == 1:
                            if t == 0:
                                pe.wait_ge(ctx_kept, i * 2 + (h + 1))
                            for c, (a, b) in enumerate(FCH):
                                last = pe.matmul(ctxp[0:b - a, c * VW:(c + 1) * VW], mapped[:, n % 3, a:b],
                                                 v[:, t, bass.ds(i * 2 + h, 1), :].rearrange("p h d -> p (h d)"),
                                                 start=(t == 0 and c == 0), stop=(t == TILES - 1 and c == 2),
                                                 skip_group_check=True)
                            last.then_inc(mapped_used, 1)
                            return
                        pe.wait_ge(turn_kept, i * (2 * TILES) + (m + 1))
                        for c, (a, b) in enumerate(FCH):
                            last = pe.transpose(turn[0:b - a, m % 2, c * P:(c + 1) * P], mapped[:, n % 3, a:b],
                                                k.ident[0:P, 0:P])
                        last.then_inc(mapped_used, 1)

                    def weigh(m):
                        h = m // TILES
                        pe.wait_ge(turn_kept, i * (2 * TILES) + (m + 3))
                        if m % TILES == 0:
                            pe.wait_ge(ctx_kept, i * 2 + (h + 2))
                        pe.wait_ge(out_kept, i * (2 * TILES) + (m + 1))
                        for c, (a, b) in enumerate(FCH):
                            last = pe.matmul(outp[0:P, 0:VW], turned_sb[0:b - a, m % 2, c, :],
                                             context[0:b - a, h, c, :], start=(c == 0), stop=(c == 2))
                        last.then_inc(out_filled, 1)

                    features(0)
                    for n in range(JOBS):
                        if n + 1 < JOBS:
                            features(n + 1)
                        use(n)
                        q, m = 1 - (n // TILES) % 2, (n // (2 * TILES)) * TILES + n % TILES
                        if q == 0 and m % TILES >= 1:
                            weigh(m - 1)
                        if q == 0 and m % TILES == TILES - 1:
                            weigh(m)

            @block.scalar
            def _(act):
                act.preload_act_table_set(EXP_LN)
                act.sem_inc(kept, 2)
                act.sem_inc(exped, 2)
                act.sem_inc(turn_kept, 2)
                act.sem_inc(ctx_kept, 1)
                with act.Fori(0, HEADS // 2) as i:
                    act.wait_ge(out_filled, i * (2 * TILES) + 2)
                    for c in range(CHUNKS):
                        act.wait_ge(filled, i * CHUNKS + (c + 1))
                        act.activation(qkT[:, 0, c * CH:(c + 1) * CH], bank[:, c % 2, 0:CH], ACT.Copy).then_inc(kept, 1)
                    act.activation(qkT[:, 1, :], kT_all[:, bass.ds(i, 1), :].rearrange("p o n -> p (o n)"),
                                   ACT.Copy).then_inc(kept, 1)
                    act.wait_ge(kept, i * (CHUNKS + 1) + (CHUNKS + 3))
                    act.activation(square[:, :, :], qkT[:, :, :], ACT.Square).then_inc(squared, 1)

                    def keep_turned(m):
                        act.wait_ge(mapped_used, i * JOBS + ((m // TILES) * 2 * TILES + TILES + m % TILES + 4))
                        act.wait_ge(out_filled, i * (2 * TILES) + (m + 1))
                        for c, (a, b) in enumerate(FCH):
                            last = act.activation(turned_sb[0:b - a, m % 2, c, :], turn[0:b - a, m % 2, c * P:(c + 1) * P],
                                                  ACT.Copy)
                        last.then_inc(turn_kept, 1)

                    for n in range(JOBS):
                        h, q, t = n // (2 * TILES), 1 - (n // TILES) % 2, n % TILES
                        act.wait_ge(feat_filled, i * JOBS + (n + 1))
                        if q == 1:
                            act.wait_ge(diag_set, i + 1)
                            bias = kbias[:, t, h:h + 1]
                        else:
                            act.wait_ge(bias_set, i * (2 * TILES) + (h * TILES + t + 1))
                            bias = qbias[:, h, t:t + 1]
                        act.wait_ge(mapped_set, i * JOBS + (n + 1))
                        act.activation(expd[:, n % 3, :], feat[0:P, n % 2, 0:FEATURES], ACT.Exp, scale=norm,
                                       bias=bias).then_inc(exped, 1)
                        if q == 0 and t == 0:
                            act.wait_ge(mapped_used, i * JOBS + (n + 3))
                            for c, (a, b) in enumerate(FCH):
                                last = act.activation(context[0:b - a, h, c, :], ctxp[0:b - a, c * VW:(c + 1) * VW], ACT.Copy)
                            last.then_inc(ctx_kept, 1)
                        if q == 0 and t >= 1:
                            keep_turned(h * TILES + t - 1)
                        if q == 0 and t == TILES - 1:
                            keep_turned(h * TILES + t)

            @block.vector
            def _(dve):
                dve.sem_inc(out_kept, 1)
                dve.sem_inc(mapped_set, 3)
                dve.tensor_scalar(top_n[:, :], top[:, :], norm, None, ALU.mult).then_inc(top_set, 1)
                for h in range(2):
                    dve.memset(halves[h * DH:(h + 1) * DH, h:h + 1], 1.0).then_inc(top_set, 1)
                    dve.memset(halves[h * DH:(h + 1) * DH, 1 - h:2 - h], 0.0).then_inc(top_set, 1)
                dve.wait_ge(top_set, 5)
                with dve.Fori(0, HEADS // 2) as i:
                    dve.wait_ge(diag_filled, i + 1)
                    dve.tensor_scalar(diag[:, :, :, :].rearrange("p q t h -> p (q t h)"), outp[0:P, 128:128 + 4 * TILES],
                                      0.5 * norm * norm, None, ALU.mult).then_inc(diag_read, 1)
                    dve.wait_ge(diag_read, i + 1)
                    dve.tensor_scalar(kbias[:, :, :], diag[:, 1, :, :], top_n[0:P, 0:1], -1.0, ALU.add,
                                      ALU.mult).then_inc(diag_set, 1)

                    def take(m):
                        h, t = m // TILES, m % TILES
                        dve.wait_ge(out_filled, i * (2 * TILES) + (m + 3))
                        dve.reciprocal(inv[:, m % 2:m % 2 + 1], outp[0:P, DH:DH + 1]).then_inc(inverted, 1)
                        dve.wait_ge(inverted, i * (2 * TILES) + (m + 1))
                        dve.tensor_scalar(attended[:, t, bass.ds(i * 128 + h * DH, DH)], outp[0:P, 0:DH],
                                          inv[:, m % 2:m % 2 + 1], None, ALU.mult).then_inc(out_kept, 1)

                    def peak(n):
                        h, t = n // (2 * TILES), n % TILES
                        m = h * TILES + t
                        dve.wait_ge(feat_filled, i * JOBS + (n + 1))
                        dve.tensor_reduce(most[:, h, t:t + 1], feat[0:P, n % 2, 0:FEATURES], AX.X, ALU.max).then_inc(peaked, 1)
                        dve.wait_ge(peaked, i * (4 * TILES) + (2 * m + 1))
                        dve.tensor_scalar(most[:, h, t:t + 1], most[:, h, t:t + 1], norm, None, ALU.mult).then_inc(peaked, 1)
                        dve.wait_ge(peaked, i * (4 * TILES) + (2 * m + 2))
                        dve.tensor_scalar(qbias[:, h, t:t + 1], most[:, h, t:t + 1], diag[:, 0, t, h:h + 1], -1.0,
                                          ALU.add, ALU.mult).then_inc(bias_set, 1)

                    for n in range(JOBS):
                        q, m = 1 - (n // TILES) % 2, (n // (2 * TILES)) * TILES + n % TILES
                        if q == 0:
                            peak(n)
                        dve.wait_ge(exped, i * JOBS + (n + 3))
                        dve.wait_ge(mapped_used, i * JOBS + (n + 1))
                        dve.tensor_scalar(mapped[:, n % 3, :], expd[:, n % 3, :], EPS, ratio, ALU.add,
                                          ALU.mult).then_inc(mapped_set, 1)
                        if q == 0 and m % TILES >= 1:
                            take(m - 1)
                        if q == 0 and m % TILES == TILES - 1:
                            take(m)


SWITCH, SCAP = 16, int(1.2 * N / 16)


def stage_switch_route(nc, k, w, xT, gather_slots, share, keep, token_rows, tokens_dram):
    W = TILES * SWITCH
    with ExitStack() as ctx:
        s = Shop(nc, ctx, "switch")
        gate = s.sb("gate", [128, KD, SWITCH])
        bias = s.sb("bias", [P, SWITCH])
        logits = s.sb("logits", [P, TILES, SWITCH])
        shifted = s.sb("shifted", [P, TILES, SWITCH])
        best = s.sb("best", [P, TILES, 8])
        best_at = s.sb("best_at", [P, TILES, 8], mybir.dt.uint32)
        best_f = s.sb("best_f", [P, TILES])
        hot = s.sb("hot", [P, TILES, SWITCH])
        before = s.sb("before", [P, TILES, SWITCH])
        rank = s.sb("rank", [P, TILES, SWITCH])
        pos = s.sb("pos", [P, TILES])
        near = s.sb("near", [P, TILES])
        place = s.sb("place", [P, 3, TILES])
        put = s.sb("put", [P, TILES], I32)
        total = s.sb("total", [P, TILES])
        token = s.sb("token", [P, TILES])
        none = s.sb("none", [SWITCH, 128])
        listed = s.sb("listed", [SWITCH, 128])
        lg = s.ps("lg", [128, 512])
        rk = s.ps("rk", [128, 512])
        (loaded, scored, chain, counted, ranked, exp_asked, exped, placed, zeroed, emptied, scattered, listed_in, turned,
         numbered) = (s.sem(n) for n in (
             "loaded", "scored", "chain", "counted", "ranked", "exp_asked", "exped", "placed", "zeroed", "emptied",
             "scattered", "listed_in", "turned", "numbered"))
        with nc.Block() as block:
            @block.sync
            def _(sp):
                sp.dma_start(gate[:, :, :], w["L1_ffn_switch_w"].rearrange("(c p) n -> p c n", p=128)).then_inc(loaded, 16)
                sp.dma_start(bias[:, :], row(w["L1_ffn_switch_b"], P)).then_inc(loaded, 16)
                sp.wait_ge(scattered, 16 * TILES)
                sp.dma_start(listed[:, :], tokens_dram.rearrange("(i p) o -> i (p o)", p=128)).then_inc(listed_in, 16)

            @block.gpsimd
            def _(pool):
                pool.memset(none[:, :], 0.0).then_inc(zeroed, 1)
                pool.iota(token[:, :], pattern=[[P, TILES]], base=0, channel_multiplier=1,
                          allow_small_or_imprecise_dtypes=True).then_inc(numbered, 1)
                pool.wait_ge(zeroed, 1)
                pool.wait_ge(numbered, 1)
                pool.dma_start(tokens_dram.rearrange("(i p) o -> i (p o)", p=128), none[:, :]).then_inc(emptied, 16)
                pool.wait_ge(emptied, 16)
                pool.wait_ge(placed, 1)
                for t in range(TILES):
                    pool.indirect_dma_start(out=tokens_dram, out_offset=bass.IndirectOffsetOnAxis(
                        ap=put[:, t:t + 1], axis=0), in_=token[:, t:t + 1], in_offset=None,
                        bounds_check=SWITCH * 128 - 1, oob_is_err=False).then_inc(scattered, 16)
                pool.wait_ge(scattered, 16 * TILES)

            @block.tensor
            def _(pe):
                pe.wait_ge(loaded, 32)
                for t in range(TILES):
                    for c in range(KD):
                        last = pe.matmul(lg[0:P, t * SWITCH:(t + 1) * SWITCH], xT[:, c, t * P:(t + 1) * P], gate[:, c, :],
                                         start=(c == 0), stop=(c == KD - 1))
                last.then_inc(scored, 1)
                pe.wait_ge(counted, 1)
                pe.matmul(rk[0:P, 0:W], k.before[0:P, 0:P], hot[:, :, :].rearrange("p t e -> p (t e)"),
                          start=True, stop=False)
                pe.matmul(rk[0:P, 0:W], k.ones[0:P, 0:P], before[:, :, :].rearrange("p t e -> p (t e)"),
                          start=False, stop=True).then_inc(ranked, 1)
                pe.wait_ge(listed_in, 16)
                pe.transpose(rk[:, 256:256 + SWITCH], listed[:, :], k.ident[0:SWITCH, 0:SWITCH]).then_inc(turned, 1)

            @block.scalar
            def _(act):
                act.wait_ge(exp_asked, 1)
                act.activation(shifted[:, :, :], shifted[:, :, :], ACT.Exp).then_inc(exped, 1)

            @block.vector
            def _(dve):
                n = 0

                def link(ins):
                    nonlocal n
                    n += 1
                    ins.then_inc(chain, 1)
                    dve.wait_ge(chain, n)

                dve.wait_ge(scored, 1)
                link(dve.tensor_tensor(logits[:, :, :], lg[0:P, 0:W].rearrange("p (t e) -> p t e", t=TILES),
                                       bias[:, :].unsqueeze(1).to_broadcast([P, TILES, SWITCH]), ALU.add))
                for t in range(TILES):
                    last = dve.max(best[:, t, :], logits[:, t, :])
                link(last)
                for t in range(TILES):
                    last = dve.max_index(best_at[:, t, :], best[:, t, :], logits[:, t, :])
                link(last)
                dve.tensor_tensor(shifted[:, :, :], logits[:, :, :], best[:, :, 0:1].to_broadcast([P, TILES, SWITCH]),
                                  ALU.subtract).then_inc(exp_asked, 1)
                link(dve.tensor_copy(best_f[:, :], best_at[:, :, 0]))
                for t in range(TILES):
                    last = dve.tensor_scalar(hot[:, t, :], k.iota_f[0:P, 0:SWITCH], best_f[:, t:t + 1], None, ALU.is_equal)
                link(last)
                link(dve.memset(before[:, 0, :], 0.0))
                for t in range(TILES - 1):
                    link(dve.tensor_tensor(before[:, t + 1, :], before[:, t, :], hot[:, t, :], ALU.add))
                dve.sem_inc(counted, 1)
                dve.wait_ge(exped, 1)
                link(dve.tensor_reduce(total[:, :], shifted[:, :, :], AX.X, ALU.add))
                link(dve.reciprocal(share[:, :], total[:, :]))
                dve.wait_ge(ranked, 1)
                link(dve.tensor_tensor(rank[:, :, :], rk[0:P, 0:W].rearrange("p (t e) -> p t e", t=TILES), hot[:, :, :],
                                       ALU.mult))
                link(dve.tensor_reduce(pos[:, :], rank[:, :, :], AX.X, ALU.add))
                link(dve.tensor_scalar(keep[:, :], pos[:, :], float(SCAP), None, ALU.is_lt))
                link(dve.tensor_scalar(near[:, :], pos[:, :], float(SCAP - 1), None, ALU.min))
                link(dve.scalar_tensor_tensor(place[:, 0, :], best_f[:, :], 128.0, near[:, :], ALU.mult, ALU.add))
                link(dve.tensor_copy(gather_slots[:, :], place[:, 0, :]))
                link(dve.tensor_scalar(place[:, 1, :], keep[:, :], -float(SWITCH * 128), float(SWITCH * 128), ALU.mult, ALU.add))
                link(dve.tensor_tensor(place[:, 2, :], place[:, 0, :], place[:, 1, :], ALU.add))
                dve.tensor_copy(put[:, :], place[:, 2, :]).then_inc(placed, 1)
                dve.wait_ge(turned, 1)
                link(dve.tensor_copy(token_rows[:, :], rk[:, 256:256 + SWITCH]))


def stage_switch_experts(nc, k, w, token_rows, xn_dram, y_dram):
    with ExitStack() as ctx:
        s = Shop(nc, ctx, "swexp")
        wt = s.sb("wt", [128, 3, KD, D])
        bias = s.sb("bias", [128, 3, D])
        xg = s.sb("xg", [128, SWITCH, D])
        xgT = s.sb("xgT", [128, 2, KD, 128])
        y = s.sb("y", [128, 2, D])
        turn = s.ps("turn", [128, 2, 512])
        outp = s.ps("outp", [128, 2, 512])
        turned, turn_kept, out_filled, y_set = (s.sem(n) for n in ("turned", "turn_kept", "out_filled", "y_set"))
        y_out = [s.sem(f"y_out{b}") for b in range(2)]
        x_in = [s.sem(f"x_in{r}") for r in range(SWITCH)]
        w_in = [s.sem(f"w_in{r}") for r in range(3)]
        with nc.Block() as block:
            @block.sync
            def _(sp):
                for e in range(SWITCH):
                    if e >= 3:
                        sp.wait_ge(y_set, e - 2)
                    sp.dma_start(wt[:, e % 3, :, :], w["L1_ffn_expert_w"][e].rearrange("(c p) n -> p c n", p=128)
                                 ).then_inc(w_in[e % 3], 16)
                    sp.dma_start(bias[:, e % 3, :], row(w["L1_ffn_expert_b"][e], 128)).then_inc(w_in[e % 3], 16)

            @block.gpsimd
            def _(pool):
                for e in range(SWITCH):
                    pool.indirect_dma_start(out=xg[:, e, :], out_offset=None, in_=xn_dram,
                                            in_offset=bass.IndirectOffsetOnAxis(ap=token_rows[:, e:e + 1], axis=0)
                                            ).then_inc(x_in[e], 16)

            @block.tensor
            def _(pe):
                for e in range(SWITCH):
                    pe.wait_ge(x_in[e], 16)
                    if e >= 2:
                        pe.wait_ge(turn_kept, e - 1)
                    for c in range(KD):
                        last = pe.transpose(turn[:, e % 2, c * 128:(c + 1) * 128], xg[:, e, c * 128:(c + 1) * 128],
                                            k.ident[:, :])
                    last.then_inc(turned, 1)
                    pe.wait_ge(turn_kept, e + 1)
                    pe.wait_ge(w_in[e % 3], 32 * (e // 3 + 1))
                    if e >= 2:
                        pe.wait_ge(y_set, e - 1)
                    for c in range(KD):
                        last = pe.matmul(outp[:, e % 2, :], xgT[:, e % 2, c, :], wt[:, e % 3, c, :],
                                         start=(c == 0), stop=(c == KD - 1))
                    last.then_inc(out_filled, 1)

            @block.scalar
            def _(act):
                for e in range(SWITCH):
                    act.wait_ge(turned, e + 1)
                    act.activation(xgT[:, e % 2, :, :].rearrange("p c n -> p (c n)"), turn[:, e % 2, :],
                                   ACT.Copy).then_inc(turn_kept, 1)
                    act.wait_ge(y_set, e + 1)
                    act.dma_start(y_dram[e * 128:(e + 1) * 128, :], y[:, e % 2, :]).then_inc(y_out[e % 2], 16)
                for b in range(2):
                    act.wait_ge(y_out[b], 16 * (SWITCH // 2))

            @block.vector
            def _(dve):
                for e in range(SWITCH):
                    dve.wait_ge(out_filled, e + 1)
                    dve.wait_ge(w_in[e % 3], 32 * (e // 3 + 1))
                    if e >= 2:
                        dve.wait_ge(y_out[e % 2], 16 * (e // 2))
                    dve.tensor_tensor(y[:, e % 2, :], outp[:, e % 2, :], bias[:, e % 3, :], ALU.add).then_inc(y_set, 1)


def stage_switch_combine(nc, k, x, xn, gather_slots, share, keep, y_dram, out):
    with ExitStack() as ctx:
        s = Shop(nc, ctx, "swcomb")
        got = s.sb("got", [P, TILES, D])
        fetched, chain, saved = s.sem("fetched"), s.sem("chain"), s.sem("saved")
        kept = s.sb("kept", [P, TILES], I32)
        final = s.sem("final")
        with nc.Block() as block:
            @block.gpsimd
            def _(pool):
                for t in range(TILES):
                    pool.indirect_dma_start(out=got[:, t, :], out_offset=None, in_=y_dram,
                                            in_offset=bass.IndirectOffsetOnAxis(ap=gather_slots[:, t:t + 1], axis=0)
                                            ).then_inc(fetched, 16)

            @block.vector
            def _(dve):
                dve.tensor_copy(kept[:, :], keep[:, :]).then_inc(chain, 1)
                dve.wait_ge(chain, 1)
                dve.wait_ge(fetched, 16 * TILES)
                for t in range(TILES):
                    dve.copy_predicated(xn[:, t, :], kept[:, t:t + 1].to_broadcast([P, D]), got[:, t, :]).then_inc(chain, 1)
                dve.wait_ge(chain, 1 + TILES)
                for t in range(TILES):
                    dve.scalar_tensor_tensor(x[:, t, :], xn[:, t, :], share[:, t:t + 1], x[:, t, :],
                                             ALU.mult, ALU.add).then_inc(final, 1)

            @block.sync
            def _(sp):
                sp.wait_ge(final, TILES)
                sp.dma_start(tiles_of(out), x[:, :, :]).then_inc(saved, 16)
                sp.wait_ge(saved, 16)


class Kept:
    pass


def program(nc, w, out):
    k = Kept()

    def dram(name, shape, dt=F32):
        return nc.dram_tensor(name, shape, dt, kind="Internal").ap()

    table_d, table_s = dram("table_d", (N, WD)), dram("table_s", (N, WS))
    meta, slots = dram("meta", (E, 4)), dram("slots", (E,), I32)
    records = dram("records", (GROUPS * GROUP, REC))
    x_dram, att_dram = dram("x_dram", (N, D)), dram("att_dram", (N, D))
    xn1_dram, xn3_dram = dram("xn1_dram", (N, D)), dram("xn3_dram", (N, D))
    tokens1, tokens3 = dram("tokens1", (STILES * 128, 1)), dram("tokens3", (SWITCH * 128, 1))
    y1_dram, y3_dram = dram("y1_dram", (STILES * 128, D)), dram("y3_dram", (SWITCH * 128, D))
    with ExitStack() as whole:
        s = Shop(nc, whole, "k")
        k.ident, k.before, k.ones, k.iota_f = (s.sb(n, [128, 128]) for n in ("ident", "before", "ones", "iota_f"))
        k.half = s.sb("half", [128, 1])
        k.part_f = s.sb("part_f", [128, 1])
        k.iota_h = s.sb("iota_h", [128, N], F16)
        k.s1_pair = s.sb("s1_pair", [128, 32])
        k.block_of = s.sb("block_of", [1, GROUPS], I32)
        stage_constants(nc, k)
        acc = s.sb("acc", [P, TILES, D])
        with ExitStack() as turned:
            xT = Shop(nc, turned, "turned").sb("xT", [128, KD, N])
            with ExitStack() as rows:
                x = Shop(nc, rows, "rows").sb("x", [P, TILES, D])
                stage_norm(nc, k, "norm0", w["x"], x, acc, xT, True, residual_dram=x_dram)
                stage_node_tables(nc, k, w, xT, acc, table_d, table_s)
            stage_edge_places(nc, k, w["src"], w["dst"], meta, slots)
            with ExitStack() as rows:
                attended = Shop(nc, rows, "mixed").sb("attended", [P, TILES, D])
                stage_relu_attention(nc, k, w, xT, attended, att_dram, meta, slots, records)
        with ExitStack() as joined:
            pairs = Shop(nc, joined, "joined").sb("pairs", [P, TILES, N])
            stage_edges(nc, k, w, table_d, table_s, records, acc, pairs)
            with ExitStack() as late:
                s3 = Shop(nc, late, "late")
                x, xT = s3.sb("x1", [P, TILES, D]), s3.sb("xT1", [128, KD, N])
                stage_irreps_out(nc, k, w, acc, x, x_dram)
                stage_norm(nc, k, "mixnorm", att_dram, acc, acc, xT, False,
                           affine=(w["L0_mix_ln_gamma"], w["L0_mix_ln_beta"]))
                stage_linear(nc, k, "mixout", xT, w["L0_mix_w_out"], w["L0_mix_b_out"], x)
                with ExitStack() as ffn:
                    s4 = Shop(nc, ffn, "ffn")
                    slots2, shares = s4.sb("slots2", [P, TILES, 2], I32), s4.sb("shares", [P, TILES, 2])
                    weight_rows = s4.sb("weight_rows", [128, STILES], I32)
                    token_rows = s4.sb("token_rows", [128, STILES], I32)
                    stage_norm(nc, k, "norm1", None, x, acc, xT, False, xn_dram=xn1_dram)
                    stage_route(nc, k, w, xT, slots2, shares, weight_rows, token_rows, tokens1)
                    with ExitStack() as hid:
                        hT = Shop(nc, hid, "hid").sb("hT", [128, KD, N])
                        stage_shared_hidden(nc, k, w, xT, hT)
                        stage_linear(nc, k, "sharedout", hT, w["L0_ffn_sw2"], None, x)
                    stage_experts(nc, k, w, weight_rows, token_rows, xn1_dram, y1_dram)
                    stage_combine(nc, k, x, slots2, shares, y1_dram)
                stage_norm(nc, k, "norm2", None, x, acc, xT, False)
                stage_graph_convolution(nc, k, w, xT, pairs, x)
                save(nc, s3, x, x_dram)
        with ExitStack() as last:
            s3 = Shop(nc, last, "last")
            xT = s3.sb("xT2", [128, KD, N])
            with ExitStack() as feat:
                s4 = Shop(nc, feat, "perf")
                v = s4.sb("v", [P, TILES, HEADS, VW])
                kT_all = s4.sb("kT_all", [128, HEADS // 2, N])
                top = s4.sb("top", [128, 1])
                turn_again(nc, k, "again", acc, xT)
                stage_key_maximum(nc, k, w, xT, v, kT_all, top)
                stage_random_features(nc, k, w, xT, v, kT_all, top, acc)
            x = s3.sb("x2", [P, TILES, D])
            turn_again(nc, k, "mixed1", acc, xT, x, x_dram)
            stage_linear(nc, k, "featout", xT, w["L1_mix_Wo"], w["L1_mix_bo"], x)
            s4 = Shop(nc, last, "sw")
            gather_slots, token_rows = s4.sb("gather_slots", [P, TILES], I32), s4.sb("token_rows3", [128, SWITCH], I32)
            share, keep = s4.sb("share", [P, TILES]), s4.sb("keep", [P, TILES])
            stage_norm(nc, k, "norm3", None, x, acc, xT, False, xn_dram=xn3_dram)
            stage_switch_route(nc, k, w, xT, gather_slots, share, keep, token_rows, tokens3)
            stage_switch_experts(nc, k, w, token_rows, xn3_dram, y3_dram)
            stage_switch_combine(nc, k, x, acc, gather_slots, share, keep, y3_dram, out)


def save(nc, shop, x, x_dram):
    saved = shop.sem("x_saved")
    with nc.Block() as block:
        @block.sync
        def _(sp):
            sp.dma_start(tiles_of(x_dram), x[:, :, :]).then_inc(saved, 16)
            sp.wait_ge(saved, 16)


def turn_again(nc, k, tag, a, aT, x=None, x_dram=None):
    with ExitStack() as ctx:
        s = Shop(nc, ctx, tag)
        turn = s.ps("turn", [128, 2, 512])
        turned, kept, loaded = s.sem("turned"), s.sem("kept"), s.sem("loaded")
        with nc.Block() as block:
            @block.sync
            def _(sp):
                if x is not None:
                    sp.dma_start(x[:, :, :], tiles_of(x_dram)).then_inc(loaded, 16)
                    sp.wait_ge(loaded, 16)

            @block.tensor
            def _(pe):
                for t in range(TILES):
                    if t >= 2:
                        pe.wait_ge(kept, t - 1)
                    for c in range(KD):
                        last = pe.transpose(turn[:, t % 2, c * P:(c + 1) * P], a[:, t, c * 128:(c + 1) * 128],
                                            k.ident[0:P, 0:P])
                    last.then_inc(turned, 1)

            @block.scalar
            def _(act):
                for t in range(TILES):
                    act.wait_ge(turned, t + 1)
                    act.activation(aT[:, :, t * P:(t + 1) * P],
                                   turn[:, t % 2, 0:KD * P].rearrange("p (c n) -> p c n", c=KD), ACT.Copy).then_inc(kept, 1)


def laid_out(inputs):
    import numpy as _np
    a = {n: _np.asarray(v) for n, v in inputs.items()}

    def columns(v):
        return v.reshape(-1, 128).T

    for n in ("L0_gnn_b_pre0", "L0_gnn_b_g1", "L0_gnn_b_g2", "L0_mix_ln_gamma", "L0_mix_ln_beta"):
        a[n] = columns(a[n])
    for n in ("L0_ffn_gate_w", "L1_gnn_W", "L1_mix_proj", "L1_ffn_switch_w"):
        a[n] = a[n].T
    a["L1_ffn_expert_w"] = a["L1_ffn_expert_w"].transpose(0, 2, 1)
    a["edges"] = _np.concatenate([a.pop("edge_attr_32"), a.pop("edge_attr_4"),
                                  _np.zeros((a["src"].shape[0], 4), _np.float32)], axis=1)
    return {n: _np.ascontiguousarray(v) for n, v in a.items()}


def kernel(**inputs):
    import concourse.bacc as _bacc
    from concourse import mybir as _mybir
    from concourse.bass_utils import run_bass_kernel_spmd as _run

    nc = _bacc.Bacc("TRN2", target_bir_lowering=False, num_devices=1)
    arrays, w = {}, {}
    for name, a in laid_out(inputs).items():
        arrays[f"in_{name}_dram"] = a
        w[name] = nc.dram_tensor(f"in_{name}_dram", a.shape, _mybir.dt.from_np(a.dtype), kind="ExternalInput").ap()
    out = nc.dram_tensor("out_0_dram", (N, D), F32, kind="ExternalOutput").ap()
    program(nc, w, out)
    r = _run(nc, [arrays], core_ids=[0])
    return r.results[0]["out_0_dram"]
```

```python
from contextlib import ExitStack

import concourse.bass as bass
from concourse import mybir

F32 = mybir.dt.float32
BF16 = mybir.dt.bfloat16
F16 = mybir.dt.float16
I32 = mybir.dt.int32
ALU = mybir.AluOpType
ACT = mybir.ActivationFunctionType
AX = mybir.AxisListType

N, D = 1250, 512
P, TILES = 125, 10
KD = D // 128
MUL = 128
E = 41250
CH, CHUNKS = 250, 5
LN_EPS = 1e-5
EXP_LN = "natural_log_exp_and_others"


SOFT = ("padded", "edges_in", "scattered", "d_in", "s_in", "emptied", "x_in", "m_in", "fetched")

SEMAPHORES = 150


class Shop:

    in_use, spent = 0, []

    def __init__(self, nc, ctx, tag):
        self.nc, self.ctx, self.tag = nc, ctx, tag

    def sb(self, name, shape, dt=F32):
        return self.ctx.enter_context(self.nc.sbuf_tensor(f"{self.tag}_{name}", shape, dt))

    def ps(self, name, shape, dt=F32):
        return self.ctx.enter_context(self.nc.psum_tensor(f"{self.tag}_{name}", shape, dt))

    def sem(self, name):
        if Shop.in_use == SEMAPHORES:
            Shop.clear_spent(self.nc)
        Shop.in_use += 1
        sem = self.nc.alloc_semaphore(f"{self.tag}_{name}")
        if not name.startswith(SOFT):
            self.ctx.callback(Shop.spent.append, sem)
        return sem

    @staticmethod
    def clear_spent(nc):
        with nc.Block() as block:
            @block.gpsimd
            def _(pool):
                for sem in Shop.spent:
                    pool.sem_clear(sem)
        for sem in Shop.spent:
            nc.release_semaphore(sem)
        Shop.in_use -= len(Shop.spent)
        Shop.spent.clear()


def row(ap, parts):
    return ap.rearrange("(o n) -> o n", o=1).to_broadcast([parts, ap.shape[0]])


def tiles_of(ap):
    return ap.rearrange("(t p) c -> p t c", p=P)


def irrep_rows(w):
    return w[0:MUL, :], w[MUL:D, :].rearrange("(u m) c -> u m c", m=3)


def stage_constants(nc, k):
    with ExitStack() as ctx:
        s = Shop(nc, ctx, "const")
        filled, made = s.sem("filled"), s.sem("made")
        with nc.Block() as block:
            @block.gpsimd
            def _(pool):
                pool.memset(k.ident[:, :], 0.0).then_inc(filled, 1)
                pool.memset(k.before[:, :], 1.0).then_inc(filled, 1)
                pool.memset(k.ones[:, :], 1.0).then_inc(filled, 1)
                pool.memset(k.half[:, :], 0.5).then_inc(filled, 1)
                pool.iota(k.iota_f[:, :], pattern=[[1, 128]], base=0, channel_multiplier=0,
                          allow_small_or_imprecise_dtypes=True).then_inc(filled, 1)
                pool.iota(k.iota_h[:, :], pattern=[[1, N]], base=0, channel_multiplier=0,
                          allow_small_or_imprecise_dtypes=True).then_inc(filled, 1)
                pool.iota(k.part_f[:, :], pattern=[[0, 1]], base=0, channel_multiplier=1,
                          allow_small_or_imprecise_dtypes=True).then_inc(filled, 1)
                pool.wait_ge(filled, 7)
                pool.affine_select(out=k.ident[:, :], in_=k.ident[:, :], compare_op=ALU.not_equal, fill=1.0,
                                   base=0, pattern=[[-1, 128]], channel_multiplier=1).then_inc(made, 1)
                pool.affine_select(out=k.before[:, :], in_=k.before[:, :], compare_op=ALU.is_gt, fill=0.0,
                                   base=0, pattern=[[1, 128]], channel_multiplier=-1).then_inc(made, 1)
                pool.wait_ge(made, 2)


def stage_norm(nc, k, tag, x_dram, x, xn, xT, irreps, xn_dram=None, residual_dram=None, affine=None, scatter=None, ahead=()):
    with ExitStack() as ctx:
        s = Shop(nc, ctx, tag)
        stats = s.sb("stats", [P, TILES, 6])
        mean_var = s.sb("mean_var", [P, TILES, 2])
        var = s.sb("var", [P, TILES])
        inv_var = s.sb("inv_var", [P, TILES])
        rstd = s.sb("rstd", [P, TILES])
        turn = s.ps("turn", [128, 2, 512])
        scale_shift = s.sb("scale_shift", [128, 2, KD])
        loaded = [s.sem(f"loaded{n}") for n in range(TILES // 2)]
        measured, inverted, rooted, normed, turned, kept, saved, added, coefficients_in = (s.sem(n) for n in (
            "measured", "inverted", "rooted", "normed", "turned", "kept", "saved", "added",
            "coefficients_in"))
        with nc.Block() as block:
            @block.sync
            def _(sp):
                if x_dram is not None:
                    for t in range(0, TILES, 2):
                        sp.dma_start(x[:, t:t + 2, :], tiles_of(x_dram)[:, t:t + 2, :]).then_inc(loaded[t // 2], 16)
                if affine is not None:
                    for q in range(2):
                        sp.dma_start(scale_shift[:, q, :], affine[q]).then_inc(coefficients_in, 16)
                for weights, sources in ahead:
                    weights.load(sp, sources)
                if xn_dram is not None:
                    for t in range(0, TILES, 2):
                        sp.wait_ge(normed, t + 2)
                        sp.dma_start(tiles_of(xn_dram)[:, t:t + 2, :], xn[:, t:t + 2, :]).then_inc(saved, 16)
                    sp.wait_ge(saved, 16 * (TILES // 2))

                if residual_dram is not None:
                    sp.wait_ge(added, 1)
                    sp.dma_start(tiles_of(residual_dram), x[:, :, :]).then_inc(saved, 16)
                    sp.wait_ge(saved, 16)

            @block.vector
            def _(dve):
                for t in range(TILES):
                    if x_dram is not None and t % 2 == 0:
                        dve.wait_ge(loaded[t // 2], 16)
                    dve.bn_stats(stats[:, t, :], x[:, t, :]).then_inc(measured, 1)
                dve.wait_ge(measured, TILES)
                for t in range(TILES):
                    dve.bn_aggr(mean_var[:, t, :], stats[:, t, :]).then_inc(measured, 1)
                dve.wait_ge(measured, 2 * TILES)
                dve.tensor_scalar(var[:, :], mean_var[:, :, 1], LN_EPS, None, ALU.add).then_inc(measured, 1)
                dve.wait_ge(measured, 2 * TILES + 1)
                dve.reciprocal(inv_var[:, :], var[:, :]).then_inc(inverted, 1)
                dve.wait_ge(rooted, 1)
                for t in range(TILES):
                    dve.tensor_scalar(xn[:, t, :], x[:, t, :], mean_var[:, t, 0:1], rstd[:, t:t + 1],
                                      ALU.subtract, ALU.mult).then_inc(normed, 1)
                if residual_dram is not None:
                    dve.wait_ge(normed, TILES)
                    dve.tensor_tensor(x[:, :, :], x[:, :, :], xn[:, :, :], ALU.add).then_inc(added, 1)

            @block.scalar
            def _(act):
                act.wait_ge(inverted, 1)
                act.activation(rstd[:, :], inv_var[:, :], ACT.Sqrt).then_inc(rooted, 1)
                if affine is not None:
                    act.wait_ge(coefficients_in, 32)
                for t in range(TILES):
                    act.wait_ge(turned, t + 1)
                    if affine is not None:
                        for c in range(KD):
                            last = act.activation(xT[:, c, t * P:(t + 1) * P], turn[:, t % 2, c * P:(c + 1) * P],
                                                  ACT.Identity, scale=scale_shift[:, 0, c:c + 1],
                                                  bias=scale_shift[:, 1, c:c + 1])
                        last.then_inc(kept, 1)
                        continue
                    act.activation(xT[:, :, t * P:(t + 1) * P],
                                   turn[:, t % 2, 0:KD * P].rearrange("p (c n) -> p c n", c=KD),
                                   ACT.Copy).then_inc(kept, 1)

            @block.gpsimd
            def _(pool):
                if scatter is not None:
                    scatter.start(pool)

            @block.tensor
            def _(pe):
                for t in range(TILES):
                    pe.wait_ge(normed, t + 1)
                    if t >= 2:
                        pe.wait_ge(kept, t - 1)
                    for c in range(KD):
                        if irreps:
                            part = xn[:, t, 0:MUL] if c == 0 else xn[:, t, MUL + c - 1:D:3]
                        else:
                            part = xn[:, t, c * 128:(c + 1) * 128]
                        last = pe.transpose(turn[:, t % 2, c * P:(c + 1) * P], part, k.ident[0:P, 0:P])
                    last.then_inc(turned, 1)


def stage_node_tables(nc, k, w, xT, acc, table_d, table_s, scatter):
    with ExitStack() as ctx:
        s = Shop(nc, ctx, "nodes")
        pre0, pre1, nd0, nd1 = (s.sb(n, [128, MUL]) for n in ("pre0", "pre1", "nd0", "nd1"))
        g1, g2 = (s.sb(n, [128, 2, 2 * MUL]) for n in ("g1", "g2"))
        s1 = s.sb("s1", [128, 3, 32])
        s1_node = s.sb("s1_node", [128, 32])
        b_pre0 = s.sb("b_pre0", [128, 1])
        b_g1, b_g2 = s.sb("b_g1", [128, 2]), s.sb("b_g2", [128, 2])
        b_nd0 = s.sb("b_nd0", [P, MUL])
        p0T = s.sb("p0T", [128, N])
        normT = s.sb("normT", [128, N])
        square = s.sb("square", [128, 3, N])
        z = s.sb("z", [128, 2, N])
        gate = s.sb("gate", [128, 2, N])
        rows_d = s.sb("rows_d", [P, TILES, 416])
        bank = s.ps("bank", [128, 3, 512])
        loaded, chain, drawn, filled, kept, rooted, squared, exped, saved = (
            s.sem(n) for n in ("loaded", "chain", "drawn", "filled", "kept", "rooted", "squared", "exped", "saved"))
        loads = [(pre0[:, :], w["L0_gnn_W_pre0"]), (pre1[:, :], w["L0_gnn_W_pre1"]),
                 (nd0[:, :], w["L0_gnn_W_nd0"]), (nd1[:, :], w["L0_gnn_W_nd1"]),
                 (g1[:, :, :], w["L0_gnn_W_g1"].rearrange("(c p) n -> p c n", p=128)),
                 (g2[:, :, :], w["L0_gnn_W_g2"].rearrange("(c p) n -> p c n", p=128)),
                 (s1[:, :, :], w["L0_gnn_W_s1"].rearrange("(c p) n -> p c n", p=128)),
                 (b_pre0[:, :], w["L0_gnn_b_pre0"]), (b_g1[:, :], w["L0_gnn_b_g1"]),
                 (b_g2[:, :], w["L0_gnn_b_g2"]), (b_nd0[:, :], row(w["L0_gnn_b_nd0"], P))]
        HIDDEN, GATE, ROWS = CHUNKS, 3 * CHUNKS, 5 * CHUNKS
        with nc.Block() as block:
            @block.sync
            def _(sp):
                for out, in_ in loads:
                    sp.dma_start(out, in_).then_inc(loaded, 16)
                for t in range(0, TILES, 2):
                    two = slice(t, t + 2)
                    sp.wait_ge(kept, ROWS + 2 * (t + 2))
                    sp.dma_start(tiles_of(table_d)[:, two, :], rows_d[:, two, :]).then_inc(saved, 16)
                    sp.dma_start(tiles_of(table_s)[:, two, 0:D], acc[:, two, :]).then_inc(saved, 16)
                    sp.dma_start(tiles_of(table_s)[:, two, D:D + 384], rows_d[:, two, 0:384]).then_inc(saved, 16)
                sp.wait_ge(saved, 48 * (TILES // 2))

            @block.gpsimd
            def _(pool):
                scatter.chunks(pool, 0, 1)

            @block.tensor
            def _(pe):
                job = 0

                def turn():
                    nonlocal job
                    if job >= 3:
                        pe.wait_ge(kept, job - 2)
                    job += 1
                    return bank[:, (job - 1) % 3, :]

                pe.wait_ge(loaded, 16 * len(loads))
                for c in range(CHUNKS):
                    cols = slice(c * CH, (c + 1) * CH)
                    pe.matmul(turn()[:, 0:CH], pre0[:, :], xT[:, 0, cols], start=True, stop=True).then_inc(filled, 1)
                pe.wait_ge(rooted, 1)
                for h in range(2):
                    for c in range(CHUNKS):
                        cols, out = slice(c * CH, (c + 1) * CH), turn()
                        pe.matmul(out[:, 0:CH], g1[:, 0, h * 128:(h + 1) * 128], xT[:, 0, cols], start=True, stop=False)
                        pe.matmul(out[:, 0:CH], g1[:, 1, h * 128:(h + 1) * 128], normT[:, cols],
                                  start=False, stop=True).then_inc(filled, 1)
                for h in range(2):
                    for c in range(CHUNKS):
                        if h == 0:
                            pe.wait_ge(drawn, c + 1)
                        cols, out = slice(c * CH, (c + 1) * CH), turn()
                        for q in range(2):
                            last = pe.matmul(out[:, 0:CH], g2[:, q, h * 128:(h + 1) * 128], z[:, q, cols],
                                             start=(q == 0), stop=(q == 1))
                        last.then_inc(filled, 1)
                pe.wait_ge(drawn, CHUNKS + 1)
                for t in range(TILES):
                    cols, out = slice(t * P, (t + 1) * P), turn()
                    for m in range(3):
                        pe.matmul(out[0:P, m * MUL:(m + 1) * MUL], xT[:, 1 + m, cols], pre1[:, :],
                                  start=True, stop=True)
                    pe.matmul(out[0:P, 384:416], p0T[:, cols], s1_node[:, :], start=True, stop=True).then_inc(filled, 1)
                    out = turn()
                    pe.matmul(out[0:P, 0:MUL], gate[:, 0, cols], nd0[:, :], start=True, stop=True)
                    for m in range(3):
                        last = pe.matmul(out[0:P, (1 + m) * MUL:(2 + m) * MUL], square[:, m, cols], nd1[:, :],
                                         start=True, stop=True)
                    last.then_inc(filled, 1)

            @block.scalar
            def _(act):
                act.wait_ge(squared, 1)
                act.activation(normT[:, :], square[:, 0, :], ACT.Sqrt, scale=1.0 / 3.0).then_inc(rooted, 1)
                act.wait_ge(kept, GATE)
                for c in range(CHUNKS):
                    cols = slice(c * CH, (c + 1) * CH)
                    act.activation(gate[:, :, cols], z[:, :, cols], ACT.Exp, scale=-1.0).then_inc(exped, 1)
                for h in range(2):
                    for c in range(CHUNKS):
                        j = GATE + h * CHUNKS + c
                        act.wait_ge(filled, j + 1)
                        act.activation(gate[:, h, c * CH:(c + 1) * CH], bank[:, j % 3, 0:CH], ACT.Identity,
                                       bias=b_g2[:, h:h + 1]).then_inc(kept, 1)

            @block.vector
            def _(dve):
                n = 0

                def link(ins):
                    nonlocal n
                    n += 1
                    ins.then_inc(chain, 1)
                    dve.wait_ge(chain, n)

                for m in range(3):
                    last = dve.tensor_tensor(square[:, m, :], xT[:, 1 + m, :], xT[:, 1 + m, :], ALU.mult)
                link(last)
                link(dve.tensor_tensor(square[:, 0, :], square[:, 0, :], square[:, 1, :], ALU.add))
                dve.tensor_tensor(square[:, 0, :], square[:, 0, :], square[:, 2, :], ALU.add).then_inc(squared, 1)
                dve.wait_ge(loaded, 16 * len(loads))
                for c in range(CHUNKS):
                    dve.wait_ge(filled, c + 1)
                    dve.tensor_scalar(p0T[:, c * CH:(c + 1) * CH], bank[:, c % 3, 0:CH], b_pre0[:, 0:1], None,
                                      ALU.add).then_inc(kept, 1)
                for h in range(2):
                    for c in range(CHUNKS):
                        j = HIDDEN + h * CHUNKS + c
                        dve.wait_ge(filled, j + 1)
                        dve.tensor_scalar(z[:, h, c * CH:(c + 1) * CH], bank[:, j % 3, 0:CH], b_g1[:, h:h + 1], None,
                                          ALU.add).then_inc(kept, 1)
                for c in range(CHUNKS):
                    g, zc = (a[:, :, c * CH:(c + 1) * CH] for a in (gate, z))
                    dve.wait_ge(exped, c + 1)
                    link(dve.tensor_scalar(g, g, 1.0, None, ALU.add))
                    link(dve.reciprocal(g, g))
                    dve.tensor_tensor(zc, zc, g, ALU.mult).then_inc(drawn, 1)
                dve.tensor_scalar(k.s1_pair[:, :], s1[:, 2, :], 1.0 / 3.0, None, ALU.mult).then_inc(squared, 1)
                dve.wait_ge(squared, 2)
                dve.wait_ge(rooted, 1)
                dve.wait_ge(kept, ROWS)
                dve.tensor_tensor(s1_node[:, :], s1[:, 0, :], s1[:, 1, :], ALU.add).then_inc(squared, 1)
                dve.wait_ge(squared, 3)
                for m in range(3):
                    last = dve.tensor_tensor(square[:, m, :], xT[:, 1 + m, :], gate[:, 1, :], ALU.mult)
                last.then_inc(drawn, 1)
                for t in range(TILES):
                    j = ROWS + 2 * t
                    dve.wait_ge(filled, j + 1)
                    dve.tensor_copy(rows_d[:, t, :], bank[0:P, j % 3, 0:416]).then_inc(kept, 1)
                    dve.wait_ge(filled, j + 2)
                    dve.tensor_copy(acc[:, t, MUL:D], bank[0:P, (j + 1) % 3, MUL:D])
                    dve.tensor_tensor(acc[:, t, 0:MUL], bank[0:P, (j + 1) % 3, 0:MUL], b_nd0[:, :],
                                      ALU.add).then_inc(kept, 1)


GROUP = 512
GTILES = GROUP // 128
EF = E // P
GROUPS = (E + TILES * (GROUP - 1)) // GROUP
REC = 40
ECH, ECHUNKS = 33, EF // 33


def stage_edge_places(nc, k, src, dst, meta, slots):
    with ExitStack() as ctx:
        s = Shop(nc, ctx, "places")
        ids = s.sb("ids", [P, 2, EF], I32)
        fields = s.sb("fields", [P, EF, 4])
        d = s.sb("d", [P, EF])
        ones = s.sb("ones", [P, EF])
        inside = s.sb("inside", [P, TILES, EF])
        rank = s.sb("rank", [P, TILES, EF])
        totals = s.sb("totals", [P, TILES])
        small = s.sb("small", [128, 6, TILES])
        whole = s.sb("whole", [128, 2, TILES], I32)
        place = s.sb("place", [P, EF])
        term = s.sb("term", [P, EF])
        slot = s.sb("slot", [P, EF], I32)
        block_f = s.sb("block_f", [1, GROUPS])
        sums = s.ps("sums", [128, 2, 512])
        loaded, counted, summed, chain, done, saved = (
            s.sem(n) for n in ("loaded", "counted", "summed", "chain", "done", "saved"))
        with nc.Block() as block:
            @block.sync
            def _(sp):
                sp.dma_start(ids[:, 0, :], src.rearrange("(p f) -> p f", f=EF)).then_inc(loaded, 16)
                sp.dma_start(ids[:, 1, :], dst.rearrange("(p f) -> p f", f=EF)).then_inc(loaded, 16)
                sp.wait_ge(done, 1)
                sp.dma_start(meta.rearrange("(p f) c -> p f c", f=EF), fields[:, :, :]).then_inc(saved, 16)
                sp.dma_start(slots.rearrange("(p f) -> p f", f=EF), slot[:, :]).then_inc(saved, 16)
                sp.wait_ge(saved, 32)

            @block.tensor
            def _(pe):
                pe.wait_ge(counted, 1)
                pe.matmul(sums[0:P, 0, 0:TILES], k.before[0:P, 0:P], totals[:, :], start=True, stop=True)
                pe.matmul(sums[:, 1, 0:TILES], k.ones[0:P, :], totals[:, :], start=True, stop=True).then_inc(summed, 1)

            @block.vector
            def _(dve):
                n = 0

                def link(ins):
                    nonlocal n
                    n += 1
                    ins.then_inc(chain, 1)
                    dve.wait_ge(chain, n)

                dve.memset(ones[:, :], 1.0)
                dve.memset(fields[:, :, 3], 0.0)
                dve.wait_ge(loaded, 32)
                link(dve.tensor_copy(d[:, :], ids[:, 0, :]))
                dve.tensor_copy(fields[:, :, 0], d[:, :])
                dve.tensor_copy(fields[:, :, 1], ids[:, 1, :])
                for b in range(TILES):
                    last = dve.tensor_scalar(rank[:, b, :], d[:, :], float(b * P), None, ALU.is_ge)
                link(last)
                for b in range(TILES):
                    last = dve.scalar_tensor_tensor(inside[:, b, :], d[:, :], float((b + 1) * P), rank[:, b, :],
                                                    ALU.is_lt, ALU.mult)
                link(last)
                for b in range(TILES):
                    last = dve.tensor_tensor_scan(rank[:, b, :], ones[:, :], inside[:, b, :], 0.0, ALU.mult, ALU.add)
                link(last)
                dve.tensor_copy(totals[:, :], rank[:, :, EF - 1]).then_inc(counted, 1)
                for b in range(TILES):
                    link(dve.scalar_tensor_tensor(d[:, :], inside[:, b, :], float(-P * b), d[:, :],
                                                  ALU.mult, ALU.add))
                link(dve.tensor_copy(fields[:, :, 2], d[:, :]))
                dve.wait_ge(summed, 1)
                link(dve.tensor_scalar(whole[:, 0, :], sums[:, 1, 0:TILES], float(GROUP - 1), None, ALU.add))
                link(dve.tensor_single_scalar(whole[:, 1, :], whole[:, 0, :], GROUP.bit_length() - 1,
                                              ALU.logical_shift_right))
                link(dve.tensor_copy(small[:, 0, :], whole[:, 1, :]))
                link(dve.tensor_tensor_scan(small[:, 1, :], k.ones[:, 0:TILES], small[:, 0, :], 0.0,
                                            ALU.mult, ALU.add))
                link(dve.tensor_tensor(small[:, 2, :], small[:, 1, :], small[:, 0, :], ALU.subtract))
                link(dve.scalar_tensor_tensor(small[0:P, 3, :], small[0:P, 2, :], float(GROUP), sums[0:P, 0, 0:TILES],
                                              ALU.mult, ALU.add))
                link(dve.memset(place[:, :], -1.0))
                for b in range(TILES):
                    link(dve.scalar_tensor_tensor(term[:, :], rank[:, b, :], small[0:P, 3, b:b + 1], inside[:, b, :],
                                                  ALU.add, ALU.mult))
                    link(dve.tensor_tensor(place[:, :], place[:, :], term[:, :], ALU.add))
                link(dve.tensor_copy(slot[:, :], place[:, :]))
                link(dve.memset(block_f[:, :], 0.0))
                for b in range(1, TILES):
                    link(dve.scalar_tensor_tensor(block_f[:, :], k.iota_f[0:1, 0:GROUPS], small[0:1, 2, b:b + 1],
                                                  block_f[:, :], ALU.is_ge, ALU.add))
                dve.tensor_copy(k.block_of[:, :], block_f[:, :]).then_inc(done, 1)



class Ahead:

    def __init__(self, s, name, shapes):
        self.loaded = s.sem(f"{name}_loaded")
        self.tensors = [s.sb(f"{name}{n}", shape) for n, shape in enumerate(shapes)]

    def load(self, sp, sources):
        for tensor, source in zip(self.tensors, sources):
            sp.dma_start(tensor[:], source).then_inc(self.loaded, 16)


class RecordScatter:

    def __init__(self, s, w, meta, slots, records):
        self.rec = s.sb("rec", [P, 2, ECH, REC])
        self.met = s.sb("met", [P, 2, ECH, 4])
        self.plc = s.sb("plc", [P, 2, ECH], I32)
        self.pad = s.sb("pad", [128, 36, REC])
        self.pad_set, self.padded, self.merged = s.sem("pad_set"), s.sem("padded"), s.sem("merged")
        self.edges_in = [s.sem(f"edges_in{b}") for b in range(2)]
        self.scattered = [s.sem(f"scattered{b}") for b in range(2)]
        self.records = records
        self.sources = (w["edges"].rearrange("(p f) c -> p f c", f=EF), meta.rearrange("(p f) c -> p f c", f=EF),
                        slots.rearrange("(p f) -> p f", f=EF))

    def start(self, pool):
        pool.memset(self.pad[:, :, :], 0.0).then_inc(self.pad_set, 1)
        pool.wait_ge(self.pad_set, 1)
        pool.memset(self.pad[:, :, 38], -1.0).then_inc(self.pad_set, 1)
        pool.wait_ge(self.pad_set, 2)
        per = GROUPS * GROUP // 128
        places = self.records.rearrange("(p f) c -> p f c", f=per)
        for q in range(per // 36):
            pool.dma_start(places[:, q * 36:(q + 1) * 36, :], self.pad[:, :, :]).then_inc(self.padded, 16)
        pool.wait_ge(self.padded, 16 * (per // 36))

    def load(self, pool, c):
        b = c % 2
        if c >= 2:
            pool.wait_ge(self.scattered[b], 16 * ECH * (c // 2))
        for out_, in_ in zip((self.rec[:, b, :, :], self.met[:, b, :, :], self.plc[:, b, :]), self.sources):
            pool.dma_start(out_, in_[:, c * ECH:(c + 1) * ECH]).then_inc(self.edges_in[b], 16)

    def chunks(self, pool, first, last):
        for c in range(first, last):
            b = c % 2
            self.load(pool, c)
            pool.wait_ge(self.edges_in[b], 48 * (c // 2 + 1))
            pool.tensor_copy(self.rec[:, b, :, 36:40], self.met[:, b, :, :]).then_inc(self.merged, 1)
            pool.wait_ge(self.merged, c + 1)
            for f in range(ECH):
                pool.indirect_dma_start(out=self.records, out_offset=bass.IndirectOffsetOnAxis(
                    ap=self.plc[:, b, f:f + 1], axis=0), in_=self.rec[:, b, f, :], in_offset=None
                                        ).then_inc(self.scattered[b], 16)

    def finish(self, pool):
        pool.wait_ge(self.scattered[0], 16 * ECH * ((ECHUNKS + 1) // 2))
        pool.wait_ge(self.scattered[1], 16 * ECH * (ECHUNKS // 2))


HEADS, DH = 8, 64
HALF = N // 2
FIRST, SECOND = 3 * P, 2 * P
UNITS = 4


def stage_relu_attention(nc, k, w, xT, attended, attended_dram, scatter):
    scale = DH ** -0.5
    w_first, w_rest = irrep_rows(w["L0_mix_w_qkv"])
    with ExitStack() as ctx:
        s = Shop(nc, ctx, "attn")
        wv = s.sb("wv", [128, KD, D])
        wqk = s.sb("wqk", [128, 2, KD, 128])
        v = s.sb("v", [P, TILES, D])
        qT = s.sb("qT", [128, N])
        kT = s.sb("kT", [128, 2, N])
        probs = s.sb("probs", [P, 2, TILES, HALF])
        dots = s.ps("dots", [128, 2, 2, 512])
        proj = s.ps("proj", [128, 2, 512])
        outp = s.ps("outp", [128, 2, 512])
        (v_loaded, w_loaded, v_filled, v_kept, qk_used, proj_filled, proj_kept, dots_filled, first_kept, second_kept,
         out_filled, out_kept, saved, cleared) = (s.sem(n) for n in (
             "v_loaded", "w_loaded", "v_filled", "v_kept", "qk_used", "proj_filled", "proj_kept", "dots_filled",
             "first_kept", "second_kept", "out_filled", "out_kept", "saved", "cleared"))
        DOTS = UNITS * TILES
        with nc.Block() as block:
            @block.sync
            def _(sp):
                sp.dma_start(wv[:, 0, :], w_first[:, 2 * D:3 * D]).then_inc(v_loaded, 16)
                for m in range(3):
                    sp.dma_start(wv[:, 1 + m, :], w_rest[:, m, 2 * D:3 * D]).then_inc(v_loaded, 16)
                with sp.Fori(0, HEADS // 2) as i:
                    sp.wait_ge(qk_used, i + 1)
                    for q in range(2):
                        cols = bass.ds(i * 128 + q * D, 128)
                        sp.dma_start(wqk[:, q, 0, :], w_first[:, cols]).then_inc(w_loaded, 16)
                        for m in range(3):
                            sp.dma_start(wqk[:, q, 1 + m, :], w_rest[:, m, cols]).then_inc(w_loaded, 16)
                sp.wait_ge(out_kept, HEADS * 2 + 2)
                sp.dma_start(tiles_of(attended_dram), attended[:, :, :]).then_inc(saved, 16)
                sp.wait_ge(saved, 16)

            @block.tensor
            def _(pe):
                pe.sem_inc(qk_used, 1)
                pe.wait_ge(v_loaded, 64)
                for t in range(TILES):
                    if t >= 2:
                        pe.wait_ge(v_kept, t - 1)
                    for c in range(KD):
                        last = pe.matmul(proj[0:P, t % 2, :], xT[:, c, t * P:(t + 1) * P], wv[:, c, :],
                                         start=(c == 0), stop=(c == KD - 1))
                    last.then_inc(v_filled, 1)
                pe.wait_ge(v_kept, TILES)
                with pe.Fori(0, HEADS // 2) as i:
                    pe.wait_ge(w_loaded, i * 128 + 128)
                    for q in range(2):
                        for c in range(CHUNKS):
                            n = q * CHUNKS + c
                            pe.wait_ge(proj_kept, i * (2 * CHUNKS) + (n + 1))
                            for r in range(KD):
                                last = pe.matmul(proj[:, n % 2, 0:CH], wqk[:, q, r, :], xT[:, r, c * CH:(c + 1) * CH],
                                                 start=(r == 0), stop=(r == KD - 1))
                            last.then_inc(proj_filled, 1)
                    pe.wait_ge(proj_kept, i * (2 * CHUNKS) + 2 * CHUNKS + 2)
                    pe.sem_inc(qk_used, 1)

                    def scores(u):
                        h, base = u // 2, HALF * (u % 2)
                        for j in range(TILES):
                            n = u * TILES + j
                            pe.wait_ge(first_kept, i * DOTS + (n + 1))
                            pe.wait_ge(second_kept, i * DOTS + (n + 1))
                            keys = kT[:, h, j * P:(j + 1) * P]
                            pe.matmul(dots[0:P, n % 2, 0, 0:FIRST], keys, qT[:, base:base + FIRST],
                                      start=True, stop=True)
                            pe.matmul(dots[0:P, n % 2, 1, 0:SECOND], keys, qT[:, base + FIRST:base + HALF],
                                      start=True, stop=True).then_inc(dots_filled, 1)

                    def values(u):
                        pe.wait_ge(first_kept, i * DOTS + ((u + 1) * TILES + 2))
                        pe.wait_ge(second_kept, i * DOTS + ((u + 1) * TILES + 2))
                        pe.wait_ge(out_kept, i * UNITS + (u + 1))
                        for a in range(5):
                            for j in range(TILES):
                                last = pe.matmul(outp[0:P, u % 2, a * DH:(a + 1) * DH],
                                                 probs[:, u % 2, j, a * P:(a + 1) * P],
                                                 v[:, j, bass.ds(i * 128 + DH * (u // 2), DH)],
                                                 start=(j == 0), stop=(j == TILES - 1))
                        last.then_inc(out_filled, 1)

                    for u in range(UNITS):
                        scores(u)
                        if u >= 1:
                            values(u - 1)
                    values(UNITS - 1)

            @block.scalar
            def _(act):
                act.sem_inc(proj_kept, 2)
                act.sem_inc(first_kept, 2)
                for t in range(TILES):
                    act.wait_ge(v_filled, t + 1)
                    act.activation(v[:, t, :], proj[0:P, t % 2, :], ACT.Copy).then_inc(v_kept, 1)
                act.wait_ge(cleared, 1)
                with act.Fori(0, HEADS // 2) as i:
                    act.wait_ge(out_filled, i * UNITS + 2)
                    for q in range(2):
                        for c in range(CHUNKS):
                            n = q * CHUNKS + c
                            act.wait_ge(proj_filled, i * (2 * CHUNKS) + (n + 1))
                            cols = slice(c * CH, (c + 1) * CH)
                            if q == 0:
                                act.activation(qT[:, cols], proj[:, n % 2, 0:CH], ACT.Copy).then_inc(proj_kept, 1)
                                continue
                            act.activation(kT[0:DH, 0, cols], proj[0:DH, n % 2, 0:CH], ACT.Copy)
                            act.activation(kT[DH:128, 1, cols], proj[DH:128, n % 2, 0:CH], ACT.Copy).then_inc(proj_kept, 1)
                    for u in range(UNITS):
                        act.wait_ge(out_filled, i * UNITS + (u + 1))
                        for j in range(TILES):
                            n = u * TILES + j
                            act.wait_ge(dots_filled, i * DOTS + (n + 1))
                            act.activation(probs[:, u % 2, j, 0:FIRST], dots[0:P, n % 2, 0, 0:FIRST], ACT.Relu,
                                           scale=scale).then_inc(first_kept, 1)

            @block.vector
            def _(dve):
                dve.memset(kT[:, :, :], 0.0).then_inc(cleared, 1)
                dve.sem_inc(second_kept, 2)
                dve.sem_inc(out_kept, 2)
                dve.sem_inc(out_filled, 2)
                with dve.Fori(0, HEADS // 2) as i:
                    def take(u):
                        dve.wait_ge(out_filled, i * UNITS + (u + 3))
                        h = i * 128 + DH * (u // 2)
                        dve.tensor_copy(attended[:, 5 * (u % 2):5 * (u % 2) + 5, bass.ds(h, DH)],
                                        outp[0:P, u % 2, 0:5 * DH].rearrange("p (a d) -> p a d", a=5)
                                        ).then_inc(out_kept, 1)

                    for u in range(UNITS):
                        dve.wait_ge(out_filled, i * UNITS + (u + 1))
                        for j in range(TILES):
                            n = u * TILES + j
                            dve.wait_ge(dots_filled, i * DOTS + (n + 1))
                            dve.tensor_scalar(probs[:, u % 2, j, FIRST:HALF], dots[0:P, n % 2, 1, 0:SECOND],
                                              0.0, scale, ALU.max, ALU.mult).then_inc(second_kept, 1)
                        if u >= 1:
                            take(u - 1)
                    take(UNITS - 1)

            @block.gpsimd
            def _(pool):
                scatter.chunks(pool, 1, ECHUNKS)
                scatter.finish(pool)


RING = 4
WD, WS = 384 + 32, 4 * MUL + 384


assert E < 2 ** 16


def stage_edges(nc, k, w, table_d, table_s, records, acc, pairs):
    with ExitStack() as ctx:
        s = Shop(nc, ctx, "edge")
        from_drivers = s.sb("from_drivers", [128, 64])
        from_inner = s.sb("from_inner", [128, 64])
        out_w = s.sb("out_w", [128, 2, D])
        rec = s.sb("rec", [128, RING, GTILES, REC])
        ids = s.sb("ids", [128, RING, GTILES, 2], I32)
        at_d = s.sb("at_d", [128, RING, GTILES, WD])
        at_s = s.sb("at_s", [128, RING, GTILES, WS])
        prod = s.sb("prod", [128, 3, MUL])
        half_sum = s.sb("half_sum", [128, MUL])
        inner = s.sb("inner", [128, RING, GTILES, MUL])
        drivers = s.sb("drivers", [128, GTILES, 64])
        driversT = s.sb("driversT", [128, GROUP])
        innerT = s.sb("innerT", [128, GROUP])
        mag = s.sb("mag", [64, GROUP])
        expd = s.sb("expd", [64, GROUP])
        logd = s.sb("logd", [64, GROUP])
        hidden = s.sb("hidden", [128, RING, GROUP])
        wa_sb = s.sb("wa_sb", [128, 2, D])
        ww = s.sb("ww", [128, 2, D])
        s_scaled = s.sb("s_scaled", [128, 2, D])
        dot = s.sb("dot", [128, 2, 3, MUL])
        vec = s.sb("vec", [128, 2, MUL])
        vec_sh = s.sb("vec_sh", [128, 3, MUL])
        last_part = s.sb("last_part", [128, MUL])
        msg = s.sb("msg", [128, 2, D])
        spread = s.sb("spread", [128, 2, P])
        one_d = s.sb("one_d", [128, 2, P], BF16)
        one_s = s.sb("one_s", [128, 2, N], BF16)
        joins_sb = s.sb("joins_sb", [P, N], F16)
        turn = s.ps("turn", [128, 512])
        pre = s.ps("pre", [64, 512])
        wa = s.ps("wa", [128, 512])
        wb = s.ps("wb", [128, 512])
        sums = s.ps("sums", [128, 512])
        joins = s.ps("joins", [128, 3 * 512])
        (w_in, cleared, scaled, ids_set, multiplied, added, inner_set, drivers_set, drivers_turned,
         drivers_kept, inner_turned, inner_kept, pre_filled, mag_set, exp_set, log_set, hidden_set, wa_filled,
         wb_filled, wa_kept, prescaled, dot_begun, dotted, ww_set, vec_set, vec_scaled, vectors_set, parts_set, msg_set, one_set, joined,
         sums_filled, sums_kept, joins_kept, pairs_added, pool_passed, pe_passed) = (s.sem(n) for n in (
             "w_in", "cleared", "scaled", "ids_set", "multiplied", "added", "inner_set",
             "drivers_set", "drivers_turned", "drivers_kept", "inner_turned", "inner_kept", "pre_filled",
             "mag_set", "exp_set", "log_set", "hidden_set", "wa_filled", "wb_filled", "wa_kept", "prescaled", "dot_begun",
             "dotted", "ww_set", "vec_set", "vec_scaled", "vectors_set", "parts_set", "msg_set", "one_set", "joined",
             "sums_filled", "sums_kept", "joins_kept", "pairs_added", "pool_passed", "pe_passed"))
        rec_in = [s.sem(f"rec_in{r}") for r in range(RING)]
        d_in = [[s.sem(f"d_in{r}{j}") for j in range(GTILES)] for r in range(RING)]
        s_in = [[s.sem(f"s_in{r}{j}") for j in range(GTILES)] for r in range(RING)]
        G = GTILES
        TURNS = GROUPS // RING - 1

        def groups(eng, group):
            group(0, 0, 0, True, False)
            with eng.Fori(0, TURNS) as i:
                for u in range(RING):
                    group(i * RING + (u + 1), (u + 1) % RING, i + (u + 1) // RING, False, False)
            for g in range(RING * TURNS + 1, GROUPS):
                group(g, g % RING, g // RING, False, g == LAST)

        def after(r, i):
            return (r + 1) % RING, i + (r + 1) // RING

        LAST = GROUPS - 1
        CREDITS = RING * G
        with nc.Block() as block:
            @block.sync
            def _(sp):
                sp.wait_ge(cleared, 4)
                sp.dma_start(from_drivers[0:32, 0:32], w["L0_gnn_W_f1"]).then_inc(w_in, 16)
                sp.dma_start(out_w[0:32, 0, :], w["L0_gnn_W_f2"]).then_inc(w_in, 16)
                sp.dma_start(out_w[32:64, 1, :], w["L0_gnn_W_s2"]).then_inc(w_in, 16)

                def load(g, r):
                    sp.wait_ge(msg_set, g * G + G)
                    sp.dma_start(rec[:, r, :, :].rearrange("p j c -> p (j c)"),
                                 records.rearrange("(g p j) c -> g p (j c)", p=128, j=G)[bass.ds(g, 1)]
                                 .rearrange("g p c -> (g p) c")).then_inc(rec_in[r], 16)

                with sp.Fori(0, TURNS + 1) as i:
                    for r in range(RING):
                        load(i * RING + r, r)
                for g in range(RING * (TURNS + 1), GROUPS):
                    load(g, g % RING)

            @block.gpsimd
            def _(pool):
                def inner_product(g, r, i, j):
                    T = g * G + j
                    pool.wait_ge(d_in[r][j], i * 16 + 16)
                    pool.wait_ge(s_in[r][j], i * 16 + 16)
                    pool.tensor_tensor(prod[:, :, :].rearrange("p m u -> p (m u)"), at_d[:, r, j, 0:384],
                                       at_s[:, r, j, 512:896], ALU.mult).then_inc(multiplied, 1)
                    pool.wait_ge(multiplied, T + 1)
                    pool.tensor_tensor(half_sum[:, :], prod[:, 0, :], prod[:, 1, :], ALU.add).then_inc(added, 1)
                    pool.wait_ge(added, T + 1)
                    pool.tensor_tensor(inner[:, r, j, :], half_sum[:, :], prod[:, 2, :], ALU.add).then_inc(inner_set, 1)
                    pool.wait_ge(inner_set, T + 1)

                def gather(g, r, i):
                    pool.wait_ge(rec_in[r], i * 16 + 16)
                    pool.wait_ge(msg_set, g * G + G)
                    pool.sem_inc(pool_passed, 1)
                    pool.tensor_copy(ids[:, r, :, :], rec[:, r, :, 36:38]).then_inc(ids_set, 1)
                    pool.wait_ge(ids_set, g + 1)
                    pool.sem_inc(pool_passed, 1)
                    for j in range(G):
                        pool.indirect_dma_start(
                            out=at_d[:, r, j, :], out_offset=None, in_=table_d,
                            in_offset=bass.IndirectOffsetOnAxis(ap=ids[:, r, j, 0:1], axis=0)).then_inc(d_in[r][j], 16)
                        pool.indirect_dma_start(
                            out=at_s[:, r, j, :], out_offset=None, in_=table_s,
                            in_offset=bass.IndirectOffsetOnAxis(ap=ids[:, r, j, 1:2], axis=0)).then_inc(s_in[r][j], 16)
                    for j in range(G):
                        inner_product(g, r, i, j)

                with pool.Fori(0, TURNS + 1) as i:
                    for r in range(RING):
                        gather(i * RING + r, r, i)
                for g in range(RING * (TURNS + 1), GROUPS):
                    gather(g, g % RING, g // RING)

            @block.tensor
            def _(pe):
                pe.sem_inc(joined, 2)
                pe.sem_inc(sums_filled, 2)
                pe.wait_ge(w_in, 48)
                pe.wait_ge(scaled, 1)
                pe.wait_ge(cleared, 8)

                def turn_inner(g, r):
                    pe.wait_ge(inner_set, g * G + G)
                    for j in range(G):
                        done = pe.transpose(turn[:, j * 128:(j + 1) * 128], inner[:, r, j, :], k.ident[:, :])
                    done.then_inc(inner_turned, 1)

                def turn_drivers(g):
                    pe.wait_ge(drivers_set, g + 1)
                    pe.sem_inc(pe_passed, 1)
                    for j in range(G):
                        done = pe.transpose(pre[0:64, j * 128:(j + 1) * 128], drivers[:, j, :], k.ident[:, :])
                    done.then_inc(drivers_turned, 1)

                def hidden_products(g):
                    pe.wait_ge(drivers_kept, g + 1)
                    pe.matmul(pre[:, :], from_drivers[:, :], driversT[:, :], start=True, stop=False)
                    pe.wait_ge(inner_kept, g + 1)
                    pe.matmul(pre[:, :], from_inner[:, :], innerT[:, :], start=False, stop=True).then_inc(pre_filled, 1)

                def weights(g, r, j):
                    T, cols = g * G + j, slice(j * 128, (j + 1) * 128)
                    if j == 0:
                        pe.wait_ge(hidden_set, g + 1)
                    pe.wait_ge(wa_kept, T + 1)
                    pe.matmul(wa[:, :], hidden[:, r, cols], out_w[:, 0, :], start=True, stop=True).then_inc(wa_filled, 1)
                    pe.wait_ge(ww_set, T + 1)
                    pe.matmul(wb[:, :], hidden[:, r, cols], out_w[:, 1, :], start=True, stop=True).then_inc(wb_filled, 1)

                def sum_up(g, j, meanwhile):
                    T = g * G + j
                    if j == 0:
                        pe.wait_ge(joins_kept, g + 1)
                    pe.wait_ge(one_set, T + 1)
                    for c in range(0, N, 512):
                        last = pe.matmul(joins[0:P, c:min(c + 512, N)], one_d[:, j % 2, :],
                                         one_s[:, j % 2, c:min(c + 512, N)], start=(j == 0), stop=(j == G - 1))
                    last.then_inc(joined, 1)
                    meanwhile()
                    pe.wait_ge(msg_set, T + (1 + CREDITS))
                    if j == 0:
                        pe.wait_ge(sums_kept, g + 1)
                    pe.matmul(sums[0:P, :], spread[:, j % 2, :], msg[:, j % 2, :], start=(j == 0),
                              stop=(j == G - 1)).then_inc(sums_filled, 1)

                def group(g, r, i, first, last):
                    r2, _ = after(r, i)
                    for j in range(G):
                        if j + 1 < G:
                            weights(g, r, j + 1)
                        elif not last:
                            weights(g + 1, r2, 0)

                        def meanwhile():
                            if j == 0 and not last:
                                turn_inner(g + 1, r2)
                                turn_drivers(g + 1)
                            if j == 1 and not last:
                                hidden_products(g + 1)

                        sum_up(g, j, meanwhile)

                turn_inner(0, 0)
                turn_drivers(0)
                hidden_products(0)
                weights(0, 0, 0)
                groups(pe, group)

            @block.scalar
            def _(act):
                act.preload_act_table_set(EXP_LN)
                act.sem_inc(wa_kept, 1)
                act.sem_inc(joins_kept, 1)

                def take_drivers(r, i):
                    act.wait_ge(rec_in[r], i * 16 + 16)
                    act.activation(drivers[:, :, 0:32], rec[:, r, :, 0:32], ACT.Copy)
                    for j in range(G):
                        act.wait_ge(d_in[r][j], i * 16 + 16)
                    act.activation(drivers[:, :, 32:64], at_d[:, r, :, 384:416], ACT.Copy).then_inc(drivers_set, 1)

                def keep_turned(g):
                    act.wait_ge(inner_turned, g + 1)
                    act.activation(innerT[:, :], turn[:, :], ACT.Copy).then_inc(inner_kept, 1)
                    act.wait_ge(drivers_turned, g + 1)
                    act.activation(driversT[0:64, :], pre[:, :], ACT.Copy).then_inc(drivers_kept, 1)

                def magnitude(g):
                    act.wait_ge(pre_filled, g + 1)
                    act.activation(mag[:, :], pre[:, :], ACT.Abs).then_inc(mag_set, 1)

                def exponential(g):
                    act.wait_ge(mag_set, g + 1)
                    act.activation(expd[:, :], mag[:, :], ACT.Exp, scale=-1.0).then_inc(exp_set, 1)

                def logarithm(g):
                    act.wait_ge(exp_set, g + 1)
                    act.activation(logd[:, :], expd[:, :], ACT.Ln, scale=0.5, bias=k.half[0:64, 0:1]).then_inc(log_set, 1)

                def prescale(g, r, i, j):
                    act.wait_ge(s_in[r][j], i * 16 + 16)
                    act.activation(dot[:, j % 2, 0, :], at_s[:, r, j, MUL:2 * MUL], ACT.Copy,
                                   scale=rec[:, r, j, 33:34]).then_inc(dot_begun, 1)
                    act.wait_ge(wa_filled, g * G + (j + 1))
                    act.activation(wa_sb[:, j % 2, :], wa[:, :], ACT.Copy).then_inc(wa_kept, 1)
                    act.activation(s_scaled[:, j % 2, :], at_s[:, r, j, 0:D], ACT.Copy,
                                   scale=rec[:, r, j, 32:33]).then_inc(prescaled, 1)

                def spread_out(g, j):
                    act.wait_ge(one_set, g * G + (j + 1))
                    act.wait_ge(sums_filled, g * G + (j + 1))
                    act.activation(spread[:, j % 2, :], one_d[:, j % 2, :], ACT.Copy)

                def scale_vectors(g, r, j):
                    act.wait_ge(vec_set, g * G + (j + 1))
                    for m in range(3):
                        last = act.activation(vec_sh[:, m, :], vec[:, j % 2, :], ACT.Copy, scale=rec[:, r, j, 33 + m:34 + m])
                    last.then_inc(vec_scaled, 1)

                def keep_joins(g):
                    act.wait_ge(joined, g * G + (G + 2))
                    act.wait_ge(pairs_added, 2 * g + 2)
                    act.activation(joins_sb[:, :], joins[0:P, 0:N], ACT.Copy).then_inc(joins_kept, 1)

                def group(g, r, i, first, last):
                    r2, i2 = after(r, i)
                    for j in range(G):
                        if j == 0 and not first:
                            keep_joins(g - 1)
                        if j == 0 and not last:
                            take_drivers(r2, i2)
                        spread_out(g, j)
                        scale_vectors(g, r, j)
                        if j == 2 and not last:
                            exponential(g + 1)
                        if j + 1 < G:
                            prescale(g, r, i, j + 1)
                        elif not last:
                            prescale(g + 1, r2, i2, 0)
                        if j == 0 and not last:
                            keep_turned(g + 1)
                        if j == 1 and not last:
                            magnitude(g + 1)
                        if j == 2 and not last:
                            logarithm(g + 1)

                take_drivers(0, 0)
                keep_turned(0)
                magnitude(0)
                exponential(0)
                logarithm(0)
                prescale(0, 0, 0, 0)
                groups(act, group)
                keep_joins(LAST)

            @block.vector
            def _(dve):
                for out_, value in ((from_drivers, 0.0), (out_w, 0.0), (from_inner, 0.0), (driversT, 0.0)):
                    dve.memset(out_[:], value).then_inc(cleared, 1)
                dve.memset(hidden[:, :, :], 0.0).then_inc(cleared, 1)
                dve.memset(pairs[:, :, :], 0).then_inc(pairs_added, 2)
                dve.wait_ge(cleared, 4)
                dve.tensor_copy(from_drivers[32:64, 32:64], k.ident[32:64, 32:64]).then_inc(cleared, 1)
                dve.tensor_copy(from_inner[:, 32:64], k.s1_pair[:, :]).then_inc(cleared, 1)
                dve.wait_ge(w_in, 48)
                dve.tensor_scalar(out_w[32:64, 1, 384:512], out_w[32:64, 1, 384:512], 3.0 ** -0.5, None,
                                  ALU.mult).then_inc(scaled, 1)
                dve.sem_inc(cleared, 1)
                dve.sem_inc(msg_set, CREDITS)
                dve.sem_inc(ww_set, 1)
                dve.sem_inc(sums_kept, 1)

                def soften(g, r):
                    dve.wait_ge(log_set, g + 1)
                    dve.scalar_tensor_tensor(hidden[0:64, r, :], pre[:, :], 0.0, logd[:, :], ALU.max,
                                             ALU.add).then_inc(hidden_set, 1)

                def ones(g, r, i, j):
                    T, b = g * G + j, j % 2
                    if j == 0:
                        dve.wait_ge(rec_in[r], i * 16 + 16)
                    dve.wait_ge(joined, T + 1)
                    dve.tensor_scalar(one_d[:, b, :], k.iota_h[:, 0:P], rec[:, r, j, 38:39], None, ALU.is_equal)
                    dve.tensor_scalar(one_s[:, b, :], k.iota_h[:, :], rec[:, r, j, 37:38], None,
                                      ALU.is_equal).then_inc(one_set, 1)

                def block_of(g):
                    return dve.value_load(k.block_of[0:1, bass.ds(g, 1)], min_val=0, max_val=TILES - 1)

                def add_sums(g, block_no):
                    dve.wait_ge(sums_filled, g * G + (G + 2))
                    dve.wait_ge(sums_kept, g + 1)
                    a = acc[:, bass.ds(block_no, 1), :].rearrange("p t c -> p (t c)")
                    dve.tensor_tensor(a, a, sums[0:P, :], ALU.add).then_inc(sums_kept, 1)

                def add_joins(g, block_no, half):
                    cols = slice(half * (N // 2), (half + 1) * (N // 2))
                    dve.wait_ge(joins_kept, g + 2)
                    dve.wait_ge(pairs_added, 2 * g + 2)
                    q = pairs[:, bass.ds(block_no, 1), cols].rearrange("p t c -> p (t c)")
                    dve.tensor_tensor(q, q, joins_sb[:, cols], ALU.add).then_inc(pairs_added, 1)

                def group(g, r, i, first, last):
                    for j in range(G):
                        T, b = g * G + j, j % 2

                        def dot_on(m):
                            dve.scalar_tensor_tensor(dot[:, b, m, :], at_s[:, r, j, (1 + m) * MUL:(2 + m) * MUL],
                                                     rec[:, r, j, 33 + m:34 + m], dot[:, b, m - 1, :],
                                                     ALU.mult, ALU.add).then_inc(dotted, 1)

                        dve.wait_ge(dot_begun, T + 1)
                        dot_on(1)
                        dve.wait_ge(wa_kept, T + 2)
                        dve.wait_ge(wb_filled, T + 1)
                        dve.tensor_tensor(ww[:, b, :], wb[:, :], wa_sb[:, b, :], ALU.mult).then_inc(ww_set, 1)
                        if j == 0 and not first:
                            block_no = block_of(g - 1)
                            add_sums(g - 1, block_no)
                        if j in (1, 2) and not first:
                            add_joins(g - 1, block_no, j - 1)
                        dve.wait_ge(dotted, 2 * T + 1)
                        dot_on(2)
                        dve.wait_ge(ww_set, T + 2)
                        dve.tensor_tensor(vec[:, b, :], ww[:, b, MUL:2 * MUL], at_s[:, r, j, 0:MUL],
                                          ALU.mult).then_inc(vec_set, 1)
                        if j == 3 and not last:
                            soften(g + 1, (r + 1) % RING)
                        dve.wait_ge(prescaled, T + 1)
                        dve.wait_ge(sums_filled, T + 1)
                        dve.tensor_tensor(msg[:, b, MUL:D].rearrange("p (m u) -> p m u", m=3),
                                          s_scaled[:, b, MUL:D].rearrange("p (m u) -> p m u", m=3),
                                          ww[:, b, 256:384].unsqueeze(1).to_broadcast([128, 3, MUL]),
                                          ALU.mult).then_inc(vectors_set, 1)
                        dve.wait_ge(dotted, 2 * T + 2)
                        dve.tensor_tensor(last_part[:, :], ww[:, b, 384:512], dot[:, b, 2, :], ALU.mult)
                        dve.tensor_tensor(msg[:, b, 0:MUL], ww[:, b, 0:MUL], s_scaled[:, b, 0:MUL],
                                          ALU.mult).then_inc(parts_set, 1)
                        if j + 1 < G:
                            ones(g, r, i, j + 1)
                        elif not last:
                            ones(g + 1, *after(r, i), 0)
                        dve.wait_ge(vectors_set, T + 1)
                        dve.wait_ge(vec_scaled, T + 1)
                        dve.tensor_tensor(msg[:, b, MUL:D], msg[:, b, MUL:D], vec_sh[:, :, :].rearrange("p m u -> p (m u)"),
                                          ALU.add)
                        dve.wait_ge(parts_set, T + 1)
                        dve.tensor_tensor(msg[:, b, 0:MUL], msg[:, b, 0:MUL], last_part[:, :], ALU.add).then_inc(msg_set, 1)

                soften(0, 0)
                ones(0, 0, 0, 0)
                groups(dve, group)
                block_no = block_of(LAST)
                add_sums(LAST, block_no)
                add_joins(LAST, block_no, 0)
                add_joins(LAST, block_no, 1)


def stage_irreps_out(nc, k, w, acc, x, x_dram):
    with ExitStack() as ctx:
        s = Shop(nc, ctx, "irout")
        o0, o1 = s.sb("o0", [128, MUL]), s.sb("o1", [128, MUL])
        b_o0 = s.sb("b_o0", [P, MUL])
        accT = s.sb("accT", [128, 2, KD, P])
        turn = s.ps("turn", [128, 2, 512])
        outp = s.ps("outp", [128, 2, 512])
        loaded, turned, kept, filled, added, biased = (
            s.sem(n) for n in ("loaded", "turned", "kept", "filled", "added", "biased"))
        with nc.Block() as block:
            @block.sync
            def _(sp):
                sp.dma_start(x[:, :, :], tiles_of(x_dram)).then_inc(loaded, 16)
                sp.dma_start(o0[:, :], w["L0_gnn_W_o0"]).then_inc(loaded, 16)
                sp.dma_start(o1[:, :], w["L0_gnn_W_o1"]).then_inc(loaded, 16)
                sp.dma_start(b_o0[:, :], row(w["L0_gnn_b_o0"], P)).then_inc(loaded, 16)

            @block.tensor
            def _(pe):
                def turn_tile(t):
                    if t >= 2:
                        pe.wait_ge(kept, t - 1)
                    for c in range(KD):
                        last = pe.transpose(turn[:, t % 2, c * P:(c + 1) * P], acc[:, t, c * 128:(c + 1) * 128],
                                            k.ident[0:P, 0:P])
                    last.then_inc(turned, 1)

                turn_tile(0)
                pe.wait_ge(loaded, 64)
                for t in range(TILES):
                    if t + 1 < TILES:
                        turn_tile(t + 1)
                    pe.wait_ge(kept, t + 1)
                    if t >= 2:
                        pe.wait_ge(added, t - 1)
                    for c in range(KD):
                        last = pe.matmul(outp[0:P, t % 2, c * MUL:(c + 1) * MUL], accT[:, t % 2, c, :],
                                         o0[:, :] if c == 0 else o1[:, :], start=True, stop=True)
                    last.then_inc(filled, 1)

            @block.scalar
            def _(act):
                for t in range(TILES):
                    act.wait_ge(turned, t + 1)
                    if t >= 2:
                        act.wait_ge(filled, t - 1)
                    act.activation(accT[:, t % 2, :, :], turn[:, t % 2, 0:KD * P].rearrange("p (c n) -> p c n", c=KD),
                                   ACT.Copy).then_inc(kept, 1)

            @block.vector
            def _(dve):
                dve.wait_ge(loaded, 64)
                for t in range(TILES):
                    dve.wait_ge(filled, t + 1)
                    dve.tensor_tensor(x[:, t, 0:MUL], x[:, t, 0:MUL], outp[0:P, t % 2, 0:MUL], ALU.add)
                    v = x[:, t, MUL:D].rearrange("p (u m) -> p m u", m=3)
                    dve.tensor_tensor(v, v, outp[0:P, t % 2, MUL:D].rearrange("p (m u) -> p m u", m=3),
                                      ALU.add).then_inc(added, 1)
                dve.wait_ge(added, TILES)
                for t in range(TILES):
                    dve.tensor_tensor(x[:, t, 0:MUL], x[:, t, 0:MUL], b_o0[:, :], ALU.add).then_inc(biased, 1)
                dve.wait_ge(biased, TILES)


def stage_linear(nc, k, tag, aT, weight, bias, x):
    wt = weight.tensors[0]
    with ExitStack() as ctx:
        s = Shop(nc, ctx, tag)
        outp = s.ps("outp", [128, 2, 512])
        filled, added, biased = (s.sem(n) for n in ("filled", "added", "biased"))
        with nc.Block() as block:
            @block.tensor
            def _(pe):
                pe.wait_ge(weight.loaded, 16 * len(weight.tensors))
                for t in range(TILES):
                    if t >= 2:
                        pe.wait_ge(added, t - 1)
                    for c in range(KD):
                        last = pe.matmul(outp[0:P, t % 2, :], aT[:, c, t * P:(t + 1) * P], wt[:, c, :],
                                         start=(c == 0), stop=(c == KD - 1))
                    last.then_inc(filled, 1)

            @block.vector
            def _(dve):
                if bias:
                    dve.wait_ge(weight.loaded, 32)
                for t in range(TILES):
                    dve.wait_ge(filled, t + 1)
                    dve.tensor_tensor(x[:, t, :], x[:, t, :], outp[0:P, t % 2, :], ALU.add).then_inc(added, 1)
                    if bias:
                        dve.wait_ge(added, t + 1)
                        dve.tensor_tensor(x[:, t, :], x[:, t, :], weight.tensors[1][:], ALU.add).then_inc(biased, 1)


def stage_shared_hidden(nc, k, weights, xT, hT):
    with ExitStack() as ctx:
        s = Shop(nc, ctx, "shared")
        w1, w3 = weights.tensors
        e = s.sb("e", [128, 2, CH])
        pair = s.ps("pair", [128, 2, 512])
        filled, exped, chain, used = (s.sem(n) for n in ("filled", "exped", "chain", "used"))
        jobs = [(q, c) for q in range(KD) for c in range(CHUNKS)]
        with nc.Block() as block:
            @block.tensor
            def _(pe):
                pe.wait_ge(weights.loaded, 32)
                for n, (q, c) in enumerate(jobs):
                    if n >= 2:
                        pe.wait_ge(used, n - 1)
                    for h, wt in enumerate((w1, w3)):
                        for r in range(KD):
                            last = pe.matmul(pair[:, n % 2, h * CH:(h + 1) * CH], wt[:, r, q * 128:(q + 1) * 128],
                                             xT[:, r, c * CH:(c + 1) * CH], start=(r == 0), stop=(r == KD - 1))
                    last.then_inc(filled, 1)

            @block.scalar
            def _(act):
                act.preload_act_table_set(EXP_LN)
                for n in range(len(jobs)):
                    act.wait_ge(filled, n + 1)
                    if n >= 2:
                        act.wait_ge(used, n - 1)
                    act.activation(e[:, n % 2, :], pair[:, n % 2, 0:CH], ACT.Exp, scale=-1.0).then_inc(exped, 1)

            @block.vector
            def _(dve):
                m = 0

                def link(ins):
                    nonlocal m
                    m += 1
                    ins.then_inc(chain, 1)
                    dve.wait_ge(chain, m)

                for n, (q, c) in enumerate(jobs):
                    dve.wait_ge(exped, n + 1)
                    g, out = e[:, n % 2, :], hT[:, q, c * CH:(c + 1) * CH]
                    link(dve.tensor_scalar(g, g, 1.0, None, ALU.add))
                    link(dve.reciprocal(g, g))
                    link(dve.tensor_tensor(out, pair[:, n % 2, 0:CH], g, ALU.mult))
                    dve.tensor_tensor(out, pair[:, n % 2, CH:2 * CH], out, ALU.mult).then_inc(used, 1)


EXPERTS, HID, CAP = 64, 256, 1024
STILES = 84
MRING = 4
assert STILES >= (2 * N + EXPERTS * 127) // 128 and STILES % MRING == 0


def stage_route(nc, k, w, xT, slots, weights, weight_rows, token_rows, tokens_dram):
    with ExitStack() as ctx:
        s = Shop(nc, ctx, "route")
        gate = s.sb("gate", [128, KD, EXPERTS])
        logits = s.sb("logits", [P, TILES, EXPERTS])
        best = s.sb("best", [P, TILES, 8])
        best_at = s.sb("best_at", [P, TILES, 8], mybir.dt.uint32)
        best_f = s.sb("best_f", [P, TILES, 2])
        hot = s.sb("hot", [P, 2, TILES, EXPERTS])
        count = s.sb("count", [P, TILES, EXPERTS])
        before = s.sb("before", [P, TILES + 1, EXPERTS])
        place = s.sb("place", [P, TILES, EXPERTS])
        rank = s.sb("rank", [P, TILES, EXPERTS])
        term = s.sb("term", [P, TILES, EXPERTS])
        whole = s.sb("whole", [128, 2, EXPERTS], I32)
        small = s.sb("small", [128, 3, EXPERTS])
        compare = s.sb("compare", [128, STILES, EXPERTS])
        of_tile = s.sb("of_tile", [128, 2, STILES])
        slot_f = s.sb("slot_f", [P, TILES, 2])
        pos_f = s.sb("pos_f", [P, TILES, 2])
        sig = s.sb("sig", [P, TILES, 2])
        sig_sum = s.sb("sig_sum", [P, TILES])
        token = s.sb("token", [P, TILES])
        none = s.sb("none", [STILES, 128])
        listed = s.sb("listed", [STILES, 128])
        lg = s.ps("lg", [128, 2, 512])
        rk = s.ps("rk", [128, 2, 512])
        tot = s.ps("tot", [128, 512])
        (loaded, scored, chain, counted, ranked, exp_asked, exped, placed, zeroed, emptied, scattered, listed_in, turned,
         numbered) = (s.sem(n) for n in (
             "loaded", "scored", "chain", "counted", "ranked", "exp_asked", "exped", "placed", "zeroed", "emptied",
             "scattered", "listed_in", "turned", "numbered"))
        with nc.Block() as block:
            @block.sync
            def _(sp):
                sp.dma_start(gate[:, :, :], w["L0_ffn_gate_w"].rearrange("(c p) n -> p c n", p=128)).then_inc(loaded, 16)
                sp.wait_ge(scattered, 16 * 2 * TILES)
                sp.dma_start(listed[:, :], tokens_dram.rearrange("(i p) o -> i (p o)", p=128)).then_inc(listed_in, 16)

            @block.gpsimd
            def _(pool):
                pool.memset(none[:, :], 0.0).then_inc(zeroed, 1)
                pool.iota(token[:, :], pattern=[[P, TILES]], base=0, channel_multiplier=1,
                          allow_small_or_imprecise_dtypes=True).then_inc(numbered, 1)
                pool.wait_ge(zeroed, 1)
                pool.wait_ge(numbered, 1)
                pool.dma_start(tokens_dram.rearrange("(i p) o -> i (p o)", p=128), none[:, :]).then_inc(emptied, 16)
                pool.wait_ge(emptied, 16)
                pool.wait_ge(placed, 1)
                for t in range(TILES):
                    for q in range(2):
                        pool.indirect_dma_start(out=tokens_dram, out_offset=bass.IndirectOffsetOnAxis(
                            ap=slots[:, t, q:q + 1], axis=0), in_=token[:, t:t + 1], in_offset=None).then_inc(scattered, 16)
                pool.wait_ge(scattered, 16 * 2 * TILES)

            @block.tensor
            def _(pe):
                pe.wait_ge(loaded, 16)
                for t in range(TILES):
                    for c in range(KD):
                        last = pe.matmul(lg[0:P, t // 5, (t % 5) * EXPERTS:(t % 5 + 1) * EXPERTS],
                                         xT[:, c, t * P:(t + 1) * P], gate[:, c, :], start=(c == 0), stop=(c == KD - 1))
                last.then_inc(scored, 1)
                pe.wait_ge(counted, 1)
                for h in range(2):
                    out = rk[0:P, h, 0:5 * EXPERTS]
                    pe.matmul(out, k.before[0:P, 0:P], count[:, 5 * h:5 * h + 5, :].rearrange("p t e -> p (t e)"),
                              start=True, stop=False)
                    pe.matmul(out, k.ones[0:P, 0:P], before[:, 5 * h:5 * h + 5, :].rearrange("p t e -> p (t e)"),
                              start=False, stop=True)
                pe.matmul(tot[:, 0:EXPERTS], k.ones[0:P, :], before[:, TILES, :], start=True, stop=True).then_inc(ranked, 1)
                pe.wait_ge(listed_in, 16)
                pe.transpose(tot[:, 128:128 + STILES], listed[:, :], k.ident[0:STILES, 0:STILES]).then_inc(turned, 1)

            @block.scalar
            def _(act):
                act.wait_ge(exp_asked, 1)
                act.activation(sig[:, :, :], best[:, :, 0:2], ACT.Exp, scale=-1.0).then_inc(exped, 1)

            @block.vector
            def _(dve):
                n = 0

                def link(ins):
                    nonlocal n
                    n += 1
                    ins.then_inc(chain, 1)
                    dve.wait_ge(chain, n)

                dve.wait_ge(scored, 1)
                for h in range(2):
                    last = dve.tensor_copy(logits[:, 5 * h:5 * h + 5, :].rearrange("p t e -> p (t e)"),
                                           lg[0:P, h, 0:5 * EXPERTS])
                link(last)
                for t in range(TILES):
                    last = dve.max(best[:, t, :], logits[:, t, :])
                link(last)
                for t in range(TILES):
                    last = dve.max_index(best_at[:, t, :], best[:, t, :], logits[:, t, :])
                last.then_inc(exp_asked, 1)
                dve.wait_ge(exp_asked, 1)
                link(dve.tensor_copy(best_f[:, :, :], best_at[:, :, 0:2]))
                for t in range(TILES):
                    for q in range(2):
                        last = dve.tensor_scalar(hot[:, q, t, :], k.iota_f[0:P, 0:EXPERTS], best_f[:, t, q:q + 1], None,
                                                 ALU.is_equal)
                link(last)
                link(dve.tensor_tensor(count[:, :, :], hot[:, 0, :, :], hot[:, 1, :, :], ALU.add))
                link(dve.memset(before[:, 0, :], 0.0))
                for t in range(TILES):
                    link(dve.tensor_tensor(before[:, t + 1, :], before[:, t, :], count[:, t, :], ALU.add))
                dve.sem_inc(counted, 1)
                dve.wait_ge(exped, 1)
                link(dve.tensor_scalar(sig[:, :, :], sig[:, :, :], 1.0, None, ALU.add))
                link(dve.reciprocal(sig[:, :, :], sig[:, :, :]))
                link(dve.tensor_tensor(sig_sum[:, :], sig[:, :, 0], sig[:, :, 1], ALU.add))
                link(dve.tensor_scalar(sig_sum[:, :], sig_sum[:, :], 1e-20, None, ALU.add))
                link(dve.reciprocal(sig_sum[:, :], sig_sum[:, :]))
                link(dve.tensor_tensor(sig[:, :, :], sig[:, :, :], sig_sum[:, :].unsqueeze(2).to_broadcast([P, TILES, 2]),
                                       ALU.mult))
                dve.wait_ge(ranked, 1)
                link(dve.tensor_scalar(whole[:, 0, :], tot[:, 0:EXPERTS], 127.0, None, ALU.add))
                link(dve.tensor_single_scalar(whole[:, 1, :], whole[:, 0, :], 7, ALU.logical_shift_right))
                link(dve.tensor_copy(small[:, 0, :], whole[:, 1, :]))
                link(dve.tensor_tensor_scan(small[:, 1, :], k.ones[:, 0:EXPERTS], small[:, 0, :], 0.0, ALU.mult, ALU.add))
                link(dve.tensor_tensor(small[:, 2, :], small[:, 1, :], small[:, 0, :], ALU.subtract))
                for h in range(2):
                    last = dve.tensor_copy(rank[:, 5 * h:5 * h + 5, :].rearrange("p t e -> p (t e)"), rk[0:P, h, 0:5 * EXPERTS])
                link(last)
                link(dve.scalar_tensor_tensor(place[:, :, :], small[0:P, 2, :].unsqueeze(1).to_broadcast([P, TILES, EXPERTS]),
                                              128.0, rank[:, :, :], ALU.mult, ALU.add))
                for q in range(2):
                    link(dve.tensor_tensor(term[:, :, :], hot[:, q, :, :], place[:, :, :], ALU.mult))
                    link(dve.tensor_reduce(slot_f[:, :, q], term[:, :, :], AX.X, ALU.add))
                    link(dve.tensor_tensor(term[:, :, :], hot[:, q, :, :], rank[:, :, :], ALU.mult))
                    link(dve.tensor_reduce(pos_f[:, :, q], term[:, :, :], AX.X, ALU.add))
                dve.tensor_copy(slots[:, :, :], slot_f[:, :, :]).then_inc(placed, 1)
                link(dve.tensor_scalar(pos_f[:, :, :], pos_f[:, :, :], float(CAP), 2.5, ALU.is_lt, ALU.mult))
                link(dve.tensor_tensor(weights[:, :, :], sig[:, :, :], pos_f[:, :, :], ALU.mult))
                link(dve.tensor_tensor(compare[:, :, :], k.iota_f[:, 0:STILES].unsqueeze(2).to_broadcast([128, STILES, EXPERTS]),
                                       small[:, 2, :].unsqueeze(1).to_broadcast([128, STILES, EXPERTS]), ALU.is_ge))
                link(dve.tensor_reduce(of_tile[:, 0, :], compare[:, :, :], AX.X, ALU.add))
                link(dve.tensor_scalar(of_tile[:, 0, :], of_tile[:, 0, :], 128.0, k.part_f[:, 0:1], ALU.mult, ALU.add))
                link(dve.tensor_scalar(of_tile[:, 1, :], k.iota_f[:, 0:STILES], small[:, 1, EXPERTS - 1:EXPERTS],
                                       float(EXPERTS * 128), ALU.is_ge, ALU.mult))
                link(dve.tensor_tensor(of_tile[:, 0, :], of_tile[:, 0, :], of_tile[:, 1, :], ALU.add))
                link(dve.tensor_scalar(weight_rows[:, :], of_tile[:, 0, :], -128.0, None, ALU.add))
                dve.wait_ge(turned, 1)
                link(dve.tensor_copy(token_rows[:, :], tot[:, 128:128 + STILES]))


def stage_experts(nc, k, w, weight_rows, token_rows, xn_dram, y_dram):
    HC = HID // 128
    mats = (w["L0_ffn_w1"].rearrange("e (p c) h -> (e p) (c h)", p=128),
            w["L0_ffn_w3"].rearrange("e (p c) h -> (e p) (c h)", p=128),
            w["L0_ffn_w2"].rearrange("e (p c) d -> (e p) (c d)", p=128))
    R = MRING
    with ExitStack() as ctx:
        s = Shop(nc, ctx, "experts")
        rows = s.sb("rows", [128, R, 2], I32)
        mat = s.sb("mat", [128, R, 3, 1024])
        xg = s.sb("xg", [128, R, D])
        xgT = s.sb("xgT", [128, 2, KD, 128])
        e = s.sb("e", [128, 2, HID])
        hT = s.sb("hT", [128, 2, HID])
        y = s.sb("y", [128, 2, D])
        turn = s.ps("turn", [128, 2, 512])
        hid = s.ps("hid", [128, 2, 512])
        outp = s.ps("outp", [128, 2, 512])
        (rows_set, turned, turn_kept, filled, exped, plus_one, inverted, gated, hidden_set, out_filled,
         y_set, pool_passed) = (s.sem(n) for n in (
             "rows_set", "turned", "turn_kept", "filled", "exped", "plus_one", "inverted",
             "gated", "hidden_set", "out_filled", "y_set", "pool_passed"))
        x_in = [s.sem(f"x_in{r}") for r in range(R)]
        m_in = [[s.sem(f"m_in{r}{q}") for q in range(3)] for r in range(R)]
        y_out = [s.sem(f"y_out{b}") for b in range(2)]

        def turns(eng, step):
            with eng.Fori(0, STILES // R - 1) as i:
                for u in range(R):
                    step(i * R + u, u, i, R)
            i = STILES // R - 1
            for u in range(R):
                step(i * R + u, u, i, R - 1 - u)

        with nc.Block() as block:
            @block.gpsimd
            def _(pool):
                with pool.Fori(0, STILES // R) as i:
                    for r in range(R):
                        pool.wait_ge(rows_set, i * R + (r + 1))
                        pool.sem_inc(pool_passed, 1)
                        pool.indirect_dma_start(out=xg[:, r, :], out_offset=None, in_=xn_dram,
                                                in_offset=bass.IndirectOffsetOnAxis(ap=rows[:, r, 0:1], axis=0)
                                                ).then_inc(x_in[r], 16)
                        for q in range(3):
                            pool.indirect_dma_start(out=mat[:, r, q, :], out_offset=None, in_=mats[q],
                                                    in_offset=bass.IndirectOffsetOnAxis(ap=rows[:, r, 1:2], axis=0),
                                                    bounds_check=EXPERTS * 128 - 1, oob_is_err=False
                                                    ).then_inc(m_in[r][q], 16)

            @block.sync
            def _(sp):
                out = y_dram.rearrange("(i p) d -> p i d", p=128)
                with sp.Fori(0, STILES // 2) as i:
                    for b in range(2):
                        sp.wait_ge(y_set, i * 2 + (b + 3))
                        sp.dma_start(out[:, bass.ds(i * 2 + b, 1), :].rearrange("p i d -> p (i d)"),
                                     y[:, b, :]).then_inc(y_out[b], 16)
                for b in range(2):
                    sp.wait_ge(y_out[b], 16 * (STILES // 2) + 16)

            @block.tensor
            def _(pe):
                def turn_rows(n, r, i):
                    b = r % 2
                    pe.wait_ge(x_in[r], i * 16 + 16)
                    pe.wait_ge(turn_kept, n + 1)
                    for c in range(KD):
                        last = pe.transpose(turn[:, b, c * 128:(c + 1) * 128], xg[:, r, c:D:KD], k.ident[:, :])
                    last.then_inc(turned, 1)

                def hidden(n, r, i):
                    b, lap = r % 2, i * 16 + 16
                    pe.wait_ge(turn_kept, n + 3)
                    pe.wait_ge(hidden_set, n + 1)
                    for q in range(2):
                        pe.wait_ge(m_in[r][q], lap)
                        for h in range(HC):
                            for c in range(KD):
                                last = pe.matmul(hid[:, b, q * HID + h * 128:q * HID + (h + 1) * 128],
                                                 mat[:, r, q, c * HID + h:(c + 1) * HID:HC], xgT[:, b, c, :],
                                                 start=(c == 0), stop=(c == KD - 1))
                    last.then_inc(filled, 1)

                def step(n, u, i, left):
                    if left >= 1:
                        hidden(n + 1, (u + 1) % R, i + (u + 1) // R)
                    if left >= 2:
                        turn_rows(n + 2, (u + 2) % R, i + (u + 2) // R)
                    b = u % 2
                    pe.wait_ge(hidden_set, n + 3)
                    pe.wait_ge(y_set, n + 1)
                    pe.wait_ge(m_in[u][2], i * 16 + 16)
                    for h in range(HC):
                        last = pe.matmul(outp[:, b, :], hT[:, b, h * 128:(h + 1) * 128],
                                         mat[:, u, 2, h * D:(h + 1) * D], start=(h == 0), stop=(h == HC - 1))
                    last.then_inc(out_filled, 1)

                turn_rows(0, 0, 0)
                hidden(0, 0, 0)
                turn_rows(1, 1, 0)
                turns(pe, step)

            @block.scalar
            def _(act):
                act.sem_inc(turn_kept, 2)
                act.sem_inc(y_set, 2)
                for b in range(2):
                    act.sem_inc(y_out[b], 16)
                act.preload_act_table_set(EXP_LN)

                def keep_turned(n, b):
                    act.wait_ge(turned, n + 1)
                    act.activation(xgT[:, b, :, :].rearrange("p c n -> p (c n)"), turn[:, b, :],
                                   ACT.Copy).then_inc(turn_kept, 1)

                def hidden(n, b):
                    act.wait_ge(filled, n + 1)
                    act.activation(e[:, b, :], hid[:, b, 0:HID], ACT.Exp, scale=-1.0).then_inc(exped, 1)

                def step(n, u, i, left):
                    if left >= 1:
                        hidden(n + 1, (u + 1) % 2)
                    if left >= 2:
                        keep_turned(n + 2, u % 2)
                    act.wait_ge(out_filled, n + 1)
                    act.wait_ge(y_out[u % 2], i * (16 * R // 2) + 16 * (u // 2 + 1))
                    act.activation(y[:, u % 2, :], outp[:, u % 2, :], ACT.Copy).then_inc(y_set, 1)

                keep_turned(0, 0)
                hidden(0, 0)
                keep_turned(1, 1)
                turns(act, step)

            @block.vector
            def _(dve):
                dve.sem_inc(hidden_set, 2)

                def ids(n, r):
                    dve.tensor_copy(rows[:, r, 0:1], token_rows[:, bass.ds(n, 1)])
                    dve.tensor_copy(rows[:, r, 1:2], weight_rows[:, bass.ds(n, 1)]).then_inc(rows_set, 1)

                def hidden(n, b):
                    dve.wait_ge(exped, n + 1)
                    dve.tensor_scalar(e[:, b, :], e[:, b, :], 1.0, None, ALU.add).then_inc(plus_one, 1)
                    dve.wait_ge(plus_one, n + 1)
                    dve.reciprocal(e[:, b, :], e[:, b, :]).then_inc(inverted, 1)
                    dve.wait_ge(inverted, n + 1)
                    dve.tensor_tensor(e[:, b, :], hid[:, b, 0:HID], e[:, b, :], ALU.mult).then_inc(gated, 1)
                    dve.wait_ge(gated, n + 1)
                    dve.tensor_tensor(hT[:, b, :], hid[:, b, HID:2 * HID], e[:, b, :], ALU.mult).then_inc(hidden_set, 1)

                def step(n, u, i, left):
                    if left >= 1:
                        hidden(n + 1, (u + 1) % 2)
                    dve.wait_ge(out_filled, n + 1)
                    if left >= R:
                        ids(n + R, u)

                for r in range(R):
                    ids(r, r)
                hidden(0, 0)
                turns(dve, step)


def stage_combine(nc, k, x, slots, weights, y_dram):
    with ExitStack() as ctx:
        s = Shop(nc, ctx, "combine")
        got = s.sb("got", [P, TILES, 2, D])
        fetched = [s.sem(f"fetched{t}") for t in range(TILES)]
        added = s.sem("added")
        with nc.Block() as block:
            @block.gpsimd
            def _(pool):
                for t in range(TILES):
                    for q in range(2):
                        pool.indirect_dma_start(out=got[:, t, q, :], out_offset=None, in_=y_dram,
                                                in_offset=bass.IndirectOffsetOnAxis(ap=slots[:, t, q:q + 1], axis=0)
                                                ).then_inc(fetched[t], 16)

            @block.vector
            def _(dve):
                for t in range(TILES):
                    dve.wait_ge(fetched[t], 32)
                    for q in range(2):
                        dve.scalar_tensor_tensor(x[:, t, :], got[:, t, q, :], weights[:, t, q:q + 1], x[:, t, :],
                                                 ALU.mult, ALU.add).then_inc(added, 1)
                        dve.wait_ge(added, 2 * t + q + 1)


def stage_graph_convolution(nc, k, w, xT, counts, x, wt, wt_in):
    with ExitStack() as ctx:
        s = Shop(nc, ctx, "conv")
        bias = s.sb("bias", [P, D])
        h = s.sb("h", [P, TILES, D])
        deg = s.sb("deg", [P, TILES])
        inv = s.sb("inv", [P, TILES])
        dis = s.sb("dis", [P, TILES])
        tmp = s.sb("tmp", [P, 2, D])
        pairs = s.sb("pairs", [P, TILES, N])
        outp = s.ps("outp", [128, 2, 512])
        loaded, chain, inverted, rooted, filled, kept, converted, scaled = (
            s.sem(n) for n in ("loaded", "chain", "inverted", "rooted", "filled", "kept", "converted", "scaled"))
        with nc.Block() as block:
            @block.sync
            def _(sp):
                sp.dma_start(bias[:, :], row(w["L1_gnn_b"], P)).then_inc(loaded, 16)

            @block.tensor
            def _(pe):
                pe.wait_ge(wt_in, 16)
                for t in range(TILES):
                    if t >= 2:
                        pe.wait_ge(kept, t - 1)
                    for c in range(KD):
                        last = pe.matmul(outp[0:P, t % 2, :], xT[:, c, t * P:(t + 1) * P], wt[:, c, :],
                                         start=(c == 0), stop=(c == KD - 1))
                    last.then_inc(filled, 1)
                pe.wait_ge(kept, TILES)
                pe.wait_ge(converted, TILES)
                for t in range(TILES):
                    if t >= 2:
                        pe.wait_ge(kept, TILES + t - 1)
                    for r in range(TILES):
                        if t == 0:
                            pe.wait_ge(scaled, r + 1)
                        last = pe.matmul(outp[0:P, t % 2, :], pairs[:, r, t * P:(t + 1) * P], h[:, r, :],
                                         start=(r == 0), stop=(r == TILES - 1))
                    last.then_inc(filled, 1)

            @block.scalar
            def _(act):
                for t in range(TILES):
                    act.activation(pairs[:, t, :], counts[:, t, :], ACT.Copy).then_inc(converted, 1)
                act.wait_ge(inverted, 1)
                act.activation(dis[:, :], inv[:, :], ACT.Sqrt).then_inc(rooted, 1)

            @block.vector
            def _(dve):
                n = 0

                def link(ins):
                    nonlocal n
                    n += 1
                    ins.then_inc(chain, 1)
                    dve.wait_ge(chain, n)

                dve.wait_ge(loaded, 16)
                for t in range(TILES):
                    dve.wait_ge(filled, t + 1)
                    dve.tensor_tensor(h[:, t, :], outp[0:P, t % 2, :], bias[:, :], ALU.add).then_inc(kept, 1)
                    dve.wait_ge(converted, t + 1)
                    last = dve.tensor_reduce(deg[:, t:t + 1], pairs[:, t, :], AX.X, ALU.add)
                link(last)
                link(dve.tensor_scalar(deg[:, :], deg[:, :], 1.0, None, ALU.add))
                dve.reciprocal(inv[:, :], deg[:, :]).then_inc(inverted, 1)
                dve.wait_ge(rooted, 1)
                for t in range(TILES):
                    dve.tensor_scalar(h[:, t, :], h[:, t, :], dis[:, t:t + 1], None, ALU.mult).then_inc(scaled, 1)
                dve.wait_ge(scaled, TILES)
                for t in range(TILES):
                    dve.wait_ge(filled, TILES + t + 1)
                    link(dve.tensor_tensor(tmp[:, t % 2, :], outp[0:P, t % 2, :], h[:, t, :], ALU.add))
                    link(dve.tensor_scalar(tmp[:, t % 2, :], tmp[:, t % 2, :], dis[:, t:t + 1], 0.0, ALU.mult, ALU.max))
                    dve.tensor_tensor(x[:, t, :], x[:, t, :], tmp[:, t % 2, :], ALU.add).then_inc(kept, 1)


FEATURES, EPS = 266, 1e-4
FCH = ((0, 89), (89, 178), (178, 266))
VW = DH + 1


def stage_queries_and_keys(nc, k, w, weights, xT, v, qkT_all, diag, top):
    norm = DH ** -0.25
    with ExitStack() as ctx:
        s = Shop(nc, ctx, "keymax")
        wv, wq, wk = weights.tensors
        halves = s.sb("halves", [128, 2])
        square = s.sb("square", [128, 3, CH])
        projT = s.sb("projT", [128, 2, FEATURES])
        most = s.sb("most", [P, HEADS * TILES])
        one = s.sb("one", [128, 4])
        bank = s.ps("bank", [128, 2, 512])
        feat = s.ps("feat", [128, 4, 512])
        tail = s.ps("tail", [128, 512])
        diagp = s.ps("diagp", [128, 512])
        (loaded, v_filled, v_kept, filled, kept, feat_filled, feat_read, chain, asked, answered, squared,
         diag_filled) = (s.sem(n) for n in (
            "loaded", "v_filled", "v_kept", "filled", "kept", "feat_filled", "feat_read", "chain", "asked", "answered", "squared",
            "diag_filled"))
        jobs = [(b, p, c) for b in range(2) for p in range(HEADS // 2) for c in range(CHUNKS)]
        with nc.Block() as block:
            @block.sync
            def _(sp):
                sp.wait_ge(chain, 6)
                for h in range(2):
                    sp.dma_start(projT[h * DH:(h + 1) * DH, h, :], w["L1_mix_proj"]).then_inc(loaded, 16)

            @block.tensor
            def _(pe):
                pe.wait_ge(weights.loaded, 48)
                pe.wait_ge(loaded, 32)
                for t in range(TILES):
                    if t >= 2:
                        pe.wait_ge(v_kept, t - 1)
                    for c in range(KD):
                        last = pe.matmul(bank[0:P, t % 2, :], xT[:, c, t * P:(t + 1) * P], wv[:, c, :],
                                         start=(c == 0), stop=(c == KD - 1))
                    last.then_inc(v_filled, 1)
                pe.wait_ge(v_kept, TILES)

                def diagonal(n):
                    pe.wait_ge(squared, n + 1)
                    for t in range(2):
                        col = (n * 2 + t) * 2
                        last = pe.matmul(diagp[0:P, col:col + 2], square[:, n % 3, t * P:(t + 1) * P], halves[:, :],
                                         start=True, stop=True)
                    last.then_inc(diag_filled, 1)

                for n, (b, p, c) in enumerate(jobs):
                    if n >= 2:
                        pe.wait_ge(kept, n - 1)
                        pe.wait_ge(squared, n - 1)
                    for r in range(KD):
                        last = pe.matmul(bank[:, n % 2, 0:CH], (wq, wk)[b][:, r, p * 128:(p + 1) * 128],
                                         xT[:, r, c * CH:(c + 1) * CH], start=(r == 0), stop=(r == KD - 1))
                    last.then_inc(filled, 1)
                    if n >= 1:
                        diagonal(n - 1)
                diagonal(len(jobs) - 1)
                for p in range(HEADS // 2):
                    pe.wait_ge(kept, len(jobs))
                    for h in range(2):
                        for t in range(TILES):
                            n = (p * 2 + h) * TILES + t
                            if n >= 4:
                                pe.wait_ge(feat_read, n - 3)
                            pe.matmul(feat[0:P, n % 4, 0:FEATURES], qkT_all[:, 1, p, t * P:(t + 1) * P],
                                      projT[:, h, :], start=True, stop=True).then_inc(feat_filled, 1)
                pe.wait_ge(asked, 1)
                pe.transpose(tail[0:1, 0:P], one[0:P, 0:1], k.ident[0:P, 0:P]).then_inc(answered, 1)
                pe.wait_ge(asked, 2)
                pe.matmul(tail[:, 256:257], k.ones[0:1, :], one[0:1, 1:2], start=True, stop=True).then_inc(answered, 1)

            @block.scalar
            def _(act):
                for t in range(TILES):
                    act.wait_ge(v_filled, t + 1)
                    act.activation(v[:, t, :, 0:DH], bank[0:P, t % 2, :].rearrange("p (h d) -> p h d", h=HEADS),
                                   ACT.Copy).then_inc(v_kept, 1)
                for n, (b, p, c) in enumerate(jobs):
                    act.wait_ge(filled, n + 1)
                    act.activation(qkT_all[:, b, p, c * CH:(c + 1) * CH], bank[:, n % 2, 0:CH], ACT.Copy).then_inc(kept, 1)
                    if n >= 3:
                        act.wait_ge(diag_filled, n - 2)
                    act.activation(square[:, n % 3, :], bank[:, n % 2, 0:CH], ACT.Square).then_inc(squared, 1)

            @block.vector
            def _(dve):
                dve.memset(v[:, :, :, DH], 1.0).then_inc(chain, 1)
                dve.memset(projT[:, :, :], 0.0).then_inc(chain, 1)
                for h in range(2):
                    dve.memset(halves[h * DH:(h + 1) * DH, h:h + 1], 1.0).then_inc(chain, 1)
                    dve.memset(halves[h * DH:(h + 1) * DH, 1 - h:2 - h], 0.0).then_inc(chain, 1)
                dve.wait_ge(diag_filled, len(jobs))
                dve.tensor_scalar(diag, diagp[0:P, 0:4 * len(jobs)], 0.5 * norm * norm, None, ALU.mult).then_inc(chain, 1)
                for n in range(HEADS * TILES):
                    dve.wait_ge(feat_filled, n + 1)
                    dve.tensor_reduce(most[:, n:n + 1], feat[0:P, n % 4, 0:FEATURES], AX.X, ALU.max).then_inc(feat_read, 1)
                dve.wait_ge(feat_read, HEADS * TILES)
                dve.tensor_reduce(one[0:P, 0:1], most[:, :], AX.X, ALU.max).then_inc(asked, 1)
                dve.wait_ge(answered, 1)
                dve.tensor_reduce(one[0:1, 1:2], tail[0:1, 0:P], AX.X, ALU.max).then_inc(asked, 1)
                dve.wait_ge(answered, 2)
                dve.tensor_scalar(top[:, :], tail[:, 256:257], norm, None, ALU.mult).then_inc(chain, 1)
                dve.wait_ge(chain, 8)


def stage_random_features(nc, k, w, v, qkT_all, diag_all, top, attended):
    norm = DH ** -0.25
    ratio = FEATURES ** -0.5
    with ExitStack() as ctx:
        s = Shop(nc, ctx, "feat")
        projT = s.sb("projT", [128, 2, FEATURES])
        qkT = s.sb("qkT", [128, 2, N])
        diag = s.sb("diag", [P, TILES, 2])
        kbias = s.sb("kbias", [P, TILES, 2])
        qbias = s.sb("qbias", [P, 2, TILES])
        most = s.sb("most", [P, 2, TILES])
        expd = s.sb("expd", [P, 3, FEATURES])
        mapped = s.sb("mapped", [P, 3, FEATURES])
        context = s.sb("context", [128, 2, 3, VW])
        turned_sb = s.sb("turned_sb", [128, 2, 3, P])
        inv = s.sb("inv", [P, 2])
        feat = s.ps("feat", [128, 4, 512])
        turn = s.ps("turn", [128, 2, 512])
        outp = s.ps("outp", [128, 2, 512])
        (proj_in, pair_set, diag_set, feat_filled, peaked, bias_set, exped, mapped_set,
         mapped_used, ctx_kept, turn_kept, out_filled, out_kept, inverted, cleared) = (s.sem(n) for n in (
             "proj_in", "pair_set", "diag_set", "feat_filled", "peaked",
             "bias_set", "exped", "mapped_set", "mapped_used", "ctx_kept", "turn_kept",
             "out_filled", "out_kept", "inverted", "cleared"))
        JOBS = 4 * TILES
        with nc.Block() as block:
            @block.sync
            def _(sp):
                sp.wait_ge(cleared, 1)
                for h in range(2):
                    sp.dma_start(projT[h * DH:(h + 1) * DH, h, :], w["L1_mix_proj"]).then_inc(proj_in, 16)

            @block.tensor
            def _(pe):
                pe.wait_ge(proj_in, 32)
                pe.sem_inc(mapped_used, 3)
                pe.sem_inc(out_filled, 2)
                with pe.Fori(0, HEADS // 2) as i:
                    pe.wait_ge(pair_set, i * 2 + 2)

                    def features(n):
                        h, q, t = n // (2 * TILES), 1 - (n // TILES) % 2, n % TILES
                        pe.wait_ge(exped, i * JOBS + (n + 1))
                        pe.matmul(feat[0:P, n % 4, 0:FEATURES], qkT[:, q, t * P:(t + 1) * P], projT[:, h, :],
                                  start=True, stop=True).then_inc(feat_filled, 1)

                    def use(n):
                        h, q, t = n // (2 * TILES), 1 - (n // TILES) % 2, n % TILES
                        m = h * TILES + t
                        pe.wait_ge(mapped_set, i * JOBS + (n + 4))
                        if q == 1:
                            if t == 0:
                                pe.wait_ge(ctx_kept, i * 2 + (h + 1))
                                pe.wait_ge(turn_kept, i * (2 * TILES) + (h * TILES + 2))
                            for c, (a, b) in enumerate(FCH):
                                last = pe.matmul(turn[0:b - a, 1, c * VW:(c + 1) * VW], mapped[:, n % 3, a:b],
                                                 v[:, t, bass.ds(i * 2 + h, 1), :].rearrange("p h d -> p (h d)"),
                                                 start=(t == 0 and c == 0), stop=(t == TILES - 1 and c == 2),
                                                 skip_group_check=True)
                            last.then_inc(mapped_used, 1)
                            return
                        pe.wait_ge(turn_kept, i * (2 * TILES) + (m + 1))
                        pe.wait_ge(ctx_kept, i * 2 + (h + 2))
                        for c, (a, b) in enumerate(FCH):
                            last = pe.transpose(turn[0:b - a, m % 2, c * P:(c + 1) * P], mapped[:, n % 3, a:b],
                                                k.ident[0:P, 0:P])
                        last.then_inc(mapped_used, 1)

                    def weigh(m):
                        h = m // TILES
                        pe.wait_ge(turn_kept, i * (2 * TILES) + (m + 3))
                        pe.wait_ge(out_kept, i * (2 * TILES) + (m + 1))
                        for c, (a, b) in enumerate(FCH):
                            last = pe.matmul(outp[0:P, m % 2, 0:VW], turned_sb[0:b - a, m % 2, c, :],
                                             context[0:b - a, h, c, :], start=(c == 0), stop=(c == 2))
                        last.then_inc(out_filled, 1)

                    for n in range(3):
                        features(n)
                    for n in range(JOBS):
                        if n + 3 < JOBS:
                            features(n + 3)
                        use(n)
                        q, m = 1 - (n // TILES) % 2, (n // (2 * TILES)) * TILES + n % TILES
                        if q == 0 and m % TILES >= 1:
                            weigh(m - 1)
                        if q == 0 and m % TILES == TILES - 1:
                            weigh(m)

            @block.scalar
            def _(act):
                act.preload_act_table_set(EXP_LN)
                act.sem_inc(exped, 4)
                act.sem_inc(turn_kept, 2)
                act.sem_inc(ctx_kept, 1)
                with act.Fori(0, HEADS // 2) as i:
                    act.wait_ge(out_filled, i * (2 * TILES) + 2)
                    for q in (1, 0):
                        act.activation(qkT[:, q, :], qkT_all[:, q, bass.ds(i, 1), :].rearrange("p o n -> p (o n)"),
                                       ACT.Copy).then_inc(pair_set, 1)

                    def keep_turned(m):
                        act.wait_ge(mapped_used, i * JOBS + ((m // TILES) * 2 * TILES + TILES + m % TILES + 4))
                        act.wait_ge(out_filled, i * (2 * TILES) + (m + 1))
                        for c, (a, b) in enumerate(FCH):
                            last = act.activation(turned_sb[0:b - a, m % 2, c, :], turn[0:b - a, m % 2, c * P:(c + 1) * P],
                                                  ACT.Copy)
                        last.then_inc(turn_kept, 1)

                    for n in range(JOBS):
                        h, q, t = n // (2 * TILES), 1 - (n // TILES) % 2, n % TILES
                        act.wait_ge(feat_filled, i * JOBS + (n + 1))
                        if q == 1:
                            act.wait_ge(diag_set, i * 2 + 2)
                            bias = kbias[:, t, h:h + 1]
                        else:
                            act.wait_ge(bias_set, i * (2 * TILES) + (h * TILES + t + 1))
                            bias = qbias[:, h, t:t + 1]
                        act.wait_ge(mapped_set, i * JOBS + (n + 1))
                        act.activation(expd[:, n % 3, :], feat[0:P, n % 4, 0:FEATURES], ACT.Exp, scale=norm,
                                       bias=bias).then_inc(exped, 1)
                        if q == 0 and t == 0:
                            act.wait_ge(mapped_used, i * JOBS + (n + 3))
                            for c, (a, b) in enumerate(FCH):
                                last = act.activation(context[0:b - a, h, c, :], turn[0:b - a, 1, c * VW:(c + 1) * VW], ACT.Copy)
                            last.then_inc(ctx_kept, 1)
                        if q == 0 and t >= 1:
                            keep_turned(h * TILES + t - 1)
                        if q == 0 and t == TILES - 1:
                            keep_turned(h * TILES + t)

            @block.vector
            def _(dve):
                dve.sem_inc(out_kept, 2)
                dve.sem_inc(mapped_set, 3)
                dve.memset(projT[:, :, :], 0.0).then_inc(cleared, 1)
                with dve.Fori(0, HEADS // 2) as i:
                    def of_pair(q):
                        return diag_all[:, q, bass.ds(i, 1), :, :].rearrange("p o t h -> p (o t) h")

                    dve.wait_ge(exped, i * JOBS + 4)
                    dve.tensor_copy(diag[:, :, :], of_pair(0)).then_inc(diag_set, 1)
                    dve.tensor_scalar(kbias[:, :, :], of_pair(1), top[0:P, 0:1], -1.0, ALU.add,
                                      ALU.mult).then_inc(diag_set, 1)
                    dve.wait_ge(diag_set, i * 2 + 2)

                    def take(m):
                        h, t = m // TILES, m % TILES
                        dve.wait_ge(out_filled, i * (2 * TILES) + (m + 3))
                        dve.reciprocal(inv[:, m % 2:m % 2 + 1], outp[0:P, m % 2, DH:DH + 1]).then_inc(inverted, 1)
                        dve.wait_ge(inverted, i * (2 * TILES) + (m + 1))
                        dve.tensor_scalar(attended[:, t, bass.ds(i * 128 + h * DH, DH)], outp[0:P, m % 2, 0:DH],
                                          inv[:, m % 2:m % 2 + 1], None, ALU.mult).then_inc(out_kept, 1)

                    def peak(n):
                        h, t = n // (2 * TILES), n % TILES
                        m = h * TILES + t
                        dve.wait_ge(feat_filled, i * JOBS + (n + 1))
                        dve.tensor_reduce(most[:, h, t:t + 1], feat[0:P, n % 4, 0:FEATURES], AX.X, ALU.max).then_inc(peaked, 1)
                        dve.wait_ge(peaked, i * (2 * TILES) + (m + 1))
                        dve.tensor_scalar(qbias[:, h, t:t + 1], most[:, h, t:t + 1], -norm, diag[:, t, h:h + 1],
                                          ALU.mult, ALU.subtract).then_inc(bias_set, 1)

                    def is_query(n):
                        return n < JOBS and (n // TILES) % 2 == 1

                    for n in range(JOBS):
                        q, m = 1 - (n // TILES) % 2, (n // (2 * TILES)) * TILES + n % TILES
                        if is_query(n + 1):
                            peak(n + 1)
                        dve.wait_ge(exped, i * JOBS + (n + 5))
                        dve.wait_ge(mapped_used, i * JOBS + (n + 1))
                        dve.tensor_scalar(mapped[:, n % 3, :], expd[:, n % 3, :], EPS, ratio, ALU.add,
                                          ALU.mult).then_inc(mapped_set, 1)
                        if q == 0 and m % TILES >= 2:
                            take(m - 2)
                        if q == 0 and m % TILES == TILES - 1:
                            take(m - 1)
                            take(m)


SWITCH, SCAP = 16, int(1.2 * N / 16)
AHEAD = 13


def expert_weights(w, e):
    return w["L1_ffn_expert_w"][e].rearrange("(c p) n -> p c n", p=128)


def stage_switch_route(nc, k, w, xT, gather_slots, share, keep, token_rows, tokens_dram):
    W = TILES * SWITCH
    with ExitStack() as ctx:
        s = Shop(nc, ctx, "switch")
        gate = s.sb("gate", [128, KD, SWITCH])
        bias = s.sb("bias", [P, SWITCH])
        logits = s.sb("logits", [P, TILES, SWITCH])
        shifted = s.sb("shifted", [P, TILES, SWITCH])
        best = s.sb("best", [P, TILES, 8])
        best_at = s.sb("best_at", [P, TILES, 8], mybir.dt.uint32)
        best_f = s.sb("best_f", [P, TILES])
        hot = s.sb("hot", [P, TILES, SWITCH])
        before = s.sb("before", [P, TILES, SWITCH])
        rank = s.sb("rank", [P, TILES, SWITCH])
        pos = s.sb("pos", [P, TILES])
        near = s.sb("near", [P, TILES])
        place = s.sb("place", [P, 3, TILES])
        put = s.sb("put", [P, TILES], I32)
        total = s.sb("total", [P, TILES])
        token = s.sb("token", [P, TILES])
        none = s.sb("none", [SWITCH, 128])
        listed = s.sb("listed", [SWITCH, 128])
        lg = s.ps("lg", [128, 512])
        rk = s.ps("rk", [128, 512])
        (loaded, scored, chain, counted, ranked, exp_asked, exped, placed, zeroed, emptied, scattered, listed_in, turned,
         numbered) = (s.sem(n) for n in (
             "loaded", "scored", "chain", "counted", "ranked", "exp_asked", "exped", "placed", "zeroed", "emptied",
             "scattered", "listed_in", "turned", "numbered"))
        with nc.Block() as block:
            @block.sync
            def _(sp):
                sp.dma_start(gate[:, :, :], w["L1_ffn_switch_w"].rearrange("(c p) n -> p c n", p=128)).then_inc(loaded, 16)
                sp.dma_start(bias[:, :], row(w["L1_ffn_switch_b"], P)).then_inc(loaded, 16)
                sp.wait_ge(scattered, 16 * TILES)
                sp.dma_start(listed[:, :], tokens_dram.rearrange("(i p) o -> i (p o)", p=128)).then_inc(listed_in, 16)

            @block.gpsimd
            def _(pool):
                pool.memset(none[:, :], 0.0).then_inc(zeroed, 1)
                pool.iota(token[:, :], pattern=[[P, TILES]], base=0, channel_multiplier=1,
                          allow_small_or_imprecise_dtypes=True).then_inc(numbered, 1)
                pool.wait_ge(zeroed, 1)
                pool.wait_ge(numbered, 1)
                pool.dma_start(tokens_dram.rearrange("(i p) o -> i (p o)", p=128), none[:, :]).then_inc(emptied, 16)
                pool.wait_ge(emptied, 16)
                pool.wait_ge(placed, 1)
                for t in range(TILES):
                    pool.indirect_dma_start(out=tokens_dram, out_offset=bass.IndirectOffsetOnAxis(
                        ap=put[:, t:t + 1], axis=0), in_=token[:, t:t + 1], in_offset=None,
                        bounds_check=SWITCH * 128 - 1, oob_is_err=False).then_inc(scattered, 16)
                pool.wait_ge(scattered, 16 * TILES)

            @block.tensor
            def _(pe):
                pe.wait_ge(loaded, 32)
                for t in range(TILES):
                    for c in range(KD):
                        last = pe.matmul(lg[0:P, t * SWITCH:(t + 1) * SWITCH], xT[:, c, t * P:(t + 1) * P], gate[:, c, :],
                                         start=(c == 0), stop=(c == KD - 1))
                last.then_inc(scored, 1)
                pe.wait_ge(counted, 1)
                pe.matmul(rk[0:P, 0:W], k.before[0:P, 0:P], hot[:, :, :].rearrange("p t e -> p (t e)"),
                          start=True, stop=False)
                pe.matmul(rk[0:P, 0:W], k.ones[0:P, 0:P], before[:, :, :].rearrange("p t e -> p (t e)"),
                          start=False, stop=True).then_inc(ranked, 1)
                pe.wait_ge(listed_in, 16)
                pe.transpose(rk[:, 256:256 + SWITCH], listed[:, :], k.ident[0:SWITCH, 0:SWITCH]).then_inc(turned, 1)

            @block.scalar
            def _(act):
                act.wait_ge(exp_asked, 1)
                act.activation(shifted[:, :, :], shifted[:, :, :], ACT.Exp).then_inc(exped, 1)

            @block.vector
            def _(dve):
                n = 0

                def link(ins):
                    nonlocal n
                    n += 1
                    ins.then_inc(chain, 1)
                    dve.wait_ge(chain, n)

                dve.wait_ge(scored, 1)
                link(dve.tensor_tensor(logits[:, :, :], lg[0:P, 0:W].rearrange("p (t e) -> p t e", t=TILES),
                                       bias[:, :].unsqueeze(1).to_broadcast([P, TILES, SWITCH]), ALU.add))
                for t in range(TILES):
                    last = dve.max(best[:, t, :], logits[:, t, :])
                link(last)
                for t in range(TILES):
                    last = dve.max_index(best_at[:, t, :], best[:, t, :], logits[:, t, :])
                link(last)
                dve.tensor_tensor(shifted[:, :, :], logits[:, :, :], best[:, :, 0:1].to_broadcast([P, TILES, SWITCH]),
                                  ALU.subtract).then_inc(exp_asked, 1)
                link(dve.tensor_copy(best_f[:, :], best_at[:, :, 0]))
                for t in range(TILES):
                    last = dve.tensor_scalar(hot[:, t, :], k.iota_f[0:P, 0:SWITCH], best_f[:, t:t + 1], None, ALU.is_equal)
                link(last)
                link(dve.memset(before[:, 0, :], 0.0))
                for t in range(TILES - 1):
                    link(dve.tensor_tensor(before[:, t + 1, :], before[:, t, :], hot[:, t, :], ALU.add))
                dve.sem_inc(counted, 1)
                dve.wait_ge(exped, 1)
                link(dve.tensor_reduce(total[:, :], shifted[:, :, :], AX.X, ALU.add))
                link(dve.reciprocal(share[:, :], total[:, :]))
                dve.wait_ge(ranked, 1)
                link(dve.tensor_tensor(rank[:, :, :], rk[0:P, 0:W].rearrange("p (t e) -> p t e", t=TILES), hot[:, :, :],
                                       ALU.mult))
                link(dve.tensor_reduce(pos[:, :], rank[:, :, :], AX.X, ALU.add))
                link(dve.tensor_scalar(keep[:, :], pos[:, :], float(SCAP), None, ALU.is_lt))
                link(dve.tensor_scalar(near[:, :], pos[:, :], float(SCAP - 1), None, ALU.min))
                link(dve.scalar_tensor_tensor(place[:, 0, :], best_f[:, :], 128.0, near[:, :], ALU.mult, ALU.add))
                link(dve.tensor_copy(gather_slots[:, :], place[:, 0, :]))
                link(dve.tensor_scalar(place[:, 1, :], keep[:, :], -float(SWITCH * 128), float(SWITCH * 128), ALU.mult, ALU.add))
                link(dve.tensor_tensor(place[:, 2, :], place[:, 0, :], place[:, 1, :], ALU.add))
                dve.tensor_copy(put[:, :], place[:, 2, :]).then_inc(placed, 1)
                dve.wait_ge(turned, 1)
                link(dve.tensor_copy(token_rows[:, :], rk[:, 256:256 + SWITCH]))


def stage_switch_experts(nc, k, w, weights, token_rows, xn_dram, y_dram):
    with ExitStack() as ctx:
        s = Shop(nc, ctx, "swexp")
        bias = s.sb("bias", [128, 4, D])
        xg = s.sb("xg", [128, 4, D])
        xgT = s.sb("xgT", [128, 2, KD, 128])
        y = s.sb("y", [128, 2, D])
        turn = s.ps("turn", [128, 2, 512])
        outp = s.ps("outp", [128, 2, 512])
        turned, turn_kept, out_filled, y_set = (s.sem(n) for n in ("turned", "turn_kept", "out_filled", "y_set"))
        y_out = [s.sem(f"y_out{b}") for b in range(2)]
        x_in = [s.sem(f"x_in{r}") for r in range(4)]
        b_in = [s.sem(f"b_in{r}") for r in range(4)]
        w_in = [s.sem(f"w_in{r}") for r in range(SWITCH - AHEAD)]
        wt = weights.tensors
        with nc.Block() as block:
            @block.sync
            def _(sp):
                for e in range(SWITCH):
                    if e >= 4:
                        sp.wait_ge(y_set, e - 3)
                    sp.dma_start(bias[:, e % 4, :], row(w["L1_ffn_expert_b"][e], 128)).then_inc(b_in[e % 4], 16)
                    if 4 <= e < 4 + SWITCH - AHEAD:
                        n = e - 4
                        sp.dma_start(wt[n][:], expert_weights(w, AHEAD + n)).then_inc(w_in[n], 16)

            @block.gpsimd
            def _(pool):
                for e in range(SWITCH):
                    if e >= 4:
                        pool.wait_ge(turned, e - 3)
                    pool.indirect_dma_start(out=xg[:, e % 4, :], out_offset=None, in_=xn_dram,
                                            in_offset=bass.IndirectOffsetOnAxis(ap=token_rows[:, e:e + 1], axis=0)
                                            ).then_inc(x_in[e % 4], 16)

            @block.tensor
            def _(pe):
                def turn_rows(e):
                    pe.wait_ge(x_in[e % 4], 16 * (e // 4 + 1))
                    if e >= 2:
                        pe.wait_ge(turn_kept, e - 1)
                    for c in range(KD):
                        last = pe.transpose(turn[:, e % 2, c * 128:(c + 1) * 128], xg[:, e % 4, c * 128:(c + 1) * 128],
                                            k.ident[:, :])
                    last.then_inc(turned, 1)

                turn_rows(0)
                for e in range(SWITCH):
                    if e + 1 < SWITCH:
                        turn_rows(e + 1)
                    pe.wait_ge(turn_kept, e + 1)
                    if e < AHEAD:
                        pe.wait_ge(weights.loaded, 16 * AHEAD)
                    else:
                        pe.wait_ge(w_in[e - AHEAD], 16)
                    if e >= 2:
                        pe.wait_ge(y_set, e - 1)
                    for c in range(KD):
                        last = pe.matmul(outp[:, e % 2, :], xgT[:, e % 2, c, :], wt[e % AHEAD][:, c, :],
                                         start=(c == 0), stop=(c == KD - 1))
                    last.then_inc(out_filled, 1)

            @block.scalar
            def _(act):
                def keep_turned(e):
                    act.wait_ge(turned, e + 1)
                    if e >= 2:
                        act.wait_ge(out_filled, e - 1)
                    act.activation(xgT[:, e % 2, :, :].rearrange("p c n -> p (c n)"), turn[:, e % 2, :],
                                   ACT.Copy).then_inc(turn_kept, 1)

                keep_turned(0)
                for e in range(SWITCH):
                    if e + 1 < SWITCH:
                        keep_turned(e + 1)
                    act.wait_ge(y_set, e + 1)
                    act.dma_start(y_dram[e * 128:(e + 1) * 128, :], y[:, e % 2, :]).then_inc(y_out[e % 2], 16)
                for b in range(2):
                    act.wait_ge(y_out[b], 16 * (SWITCH // 2))

            @block.vector
            def _(dve):
                for e in range(SWITCH):
                    dve.wait_ge(out_filled, e + 1)
                    dve.wait_ge(b_in[e % 4], 16 * (e // 4 + 1))
                    if e >= 2:
                        dve.wait_ge(y_out[e % 2], 16 * (e // 2))
                    dve.tensor_tensor(y[:, e % 2, :], outp[:, e % 2, :], bias[:, e % 4, :], ALU.add).then_inc(y_set, 1)


def stage_switch_combine(nc, k, x, xn, gather_slots, share, keep, y_dram, out):
    with ExitStack() as ctx:
        s = Shop(nc, ctx, "swcomb")
        got = s.sb("got", [P, TILES, D])
        fetched = [s.sem(f"fetched{t}") for t in range(TILES)]
        chain, saved = s.sem("chain"), s.sem("saved")
        kept = s.sb("kept", [P, TILES], I32)
        final = s.sem("final")
        with nc.Block() as block:
            @block.gpsimd
            def _(pool):
                for t in range(TILES):
                    pool.indirect_dma_start(out=got[:, t, :], out_offset=None, in_=y_dram,
                                            in_offset=bass.IndirectOffsetOnAxis(ap=gather_slots[:, t:t + 1], axis=0)
                                            ).then_inc(fetched[t], 16)

            @block.vector
            def _(dve):
                dve.tensor_copy(kept[:, :], keep[:, :]).then_inc(chain, 1)
                dve.wait_ge(chain, 1)
                for t in range(TILES):
                    dve.wait_ge(fetched[t], 16)
                    dve.copy_predicated(xn[:, t, :], kept[:, t:t + 1].to_broadcast([P, D]), got[:, t, :]).then_inc(chain, 1)
                    dve.wait_ge(chain, t + 2)
                    dve.scalar_tensor_tensor(x[:, t, :], xn[:, t, :], share[:, t:t + 1], x[:, t, :],
                                             ALU.mult, ALU.add).then_inc(final, 1)

            @block.sync
            def _(sp):
                for t in range(0, TILES, 2):
                    sp.wait_ge(final, t + 2)
                    sp.dma_start(tiles_of(out)[:, t:t + 2, :], x[:, t:t + 2, :]).then_inc(saved, 16)
                sp.wait_ge(saved, 16 * (TILES // 2))


class Kept:
    pass


def chunked(weight):
    return weight.rearrange("(c p) n -> p c n", p=128)


def program(nc, w, out):
    k = Kept()
    Shop.in_use, Shop.spent = 0, []

    def dram(name, shape, dt=F32):
        return nc.dram_tensor(name, shape, dt, kind="Internal").ap()

    table_d, table_s = dram("table_d", (N, WD)), dram("table_s", (N, WS))
    meta, slots = dram("meta", (E, 4)), dram("slots", (E,), I32)
    records = dram("records", (GROUPS * GROUP, REC))
    x_dram, att_dram = dram("x_dram", (N, D)), dram("att_dram", (N, D))
    xn1_dram, xn3_dram = dram("xn1_dram", (N, D)), dram("xn3_dram", (N, D))
    tokens1, tokens3 = dram("tokens1", (STILES * 128, 1)), dram("tokens3", (SWITCH * 128, 1))
    y1_dram, y3_dram = dram("y1_dram", (STILES * 128, D)), dram("y3_dram", (SWITCH * 128, D))
    with ExitStack() as whole:
        s = Shop(nc, whole, "k")
        k.ident, k.before, k.ones, k.iota_f = (s.sb(n, [128, 128]) for n in ("ident", "before", "ones", "iota_f"))
        k.half = s.sb("half", [128, 1])
        k.part_f = s.sb("part_f", [128, 1])
        k.iota_h = s.sb("iota_h", [128, N], F16)
        k.s1_pair = s.sb("s1_pair", [128, 32])
        k.block_of = s.sb("block_of", [1, GROUPS], I32)
        stage_constants(nc, k)
        acc = s.sb("acc", [P, TILES, D])
        with ExitStack() as turned:
            stage_edge_places(nc, k, w["src"], w["dst"], meta, slots)
            scatter = RecordScatter(Shop(nc, turned, "records"), w, meta, slots, records)
            xT = Shop(nc, turned, "turned").sb("xT", [128, KD, N])
            with ExitStack() as rows:
                x = Shop(nc, rows, "rows").sb("x", [P, TILES, D])
                stage_norm(nc, k, "norm0", w["x"], x, acc, xT, True, residual_dram=x_dram,
                           scatter=scatter)
                stage_node_tables(nc, k, w, xT, acc, table_d, table_s, scatter)
            with ExitStack() as rows:
                attended = Shop(nc, rows, "mixed").sb("attended", [P, TILES, D])
                stage_relu_attention(nc, k, w, xT, attended, att_dram, scatter)
        with ExitStack() as joined:
            pairs = Shop(nc, joined, "joined").sb("pairs", [P, TILES, N], mybir.dt.uint16)
            stage_edges(nc, k, w, table_d, table_s, records, acc, pairs)
            with ExitStack() as late:
                s3 = Shop(nc, late, "late")
                x, xT = s3.sb("x1", [P, TILES, D]), s3.sb("xT1", [128, KD, N])
                square = [128, KD, D]
                stage_irreps_out(nc, k, w, acc, x, x_dram)
                with ExitStack() as mix:
                    w_mix = Ahead(Shop(nc, mix, "mix"), "out", (square, [P, D]))
                    stage_norm(nc, k, "mixnorm", att_dram, acc, acc, xT, False,
                               affine=(w["L0_mix_ln_gamma"], w["L0_mix_ln_beta"]),
                               ahead=((w_mix, (chunked(w["L0_mix_w_out"]), row(w["L0_mix_b_out"], P))),))
                    stage_linear(nc, k, "mixout", xT, w_mix, True, x)
                with ExitStack() as ffn:
                    s4 = Shop(nc, ffn, "ffn")
                    slots2, shares = s4.sb("slots2", [P, TILES, 2], I32), s4.sb("shares", [P, TILES, 2])
                    weight_rows = s4.sb("weight_rows", [128, STILES], I32)
                    token_rows = s4.sb("token_rows", [128, STILES], I32)
                    sharing = ffn.enter_context(ExitStack())
                    w_hidden = Ahead(Shop(nc, sharing, "sharing"), "hidden", (square, square))
                    w_out = Ahead(Shop(nc, sharing, "sharing"), "out", (square,))
                    stage_norm(nc, k, "norm1", None, x, acc, xT, False, xn_dram=xn1_dram,
                               ahead=((w_hidden, (chunked(w["L0_ffn_sw1"]), chunked(w["L0_ffn_sw3"]))),
                                      (w_out, (chunked(w["L0_ffn_sw2"]),))))
                    stage_route(nc, k, w, xT, slots2, shares, weight_rows, token_rows, tokens1)
                    with ExitStack() as hid:
                        hT = Shop(nc, hid, "hid").sb("hT", [128, KD, N])
                        stage_shared_hidden(nc, k, w_hidden, xT, hT)
                        stage_linear(nc, k, "sharedout", hT, w_out, False, x)
                    sharing.close()
                    stage_experts(nc, k, w, weight_rows, token_rows, xn1_dram, y1_dram)
                    stage_combine(nc, k, x, slots2, shares, y1_dram)
                w_conv = Ahead(s3, "conv", (square,))
                stage_norm(nc, k, "norm2", None, x, acc, xT, False, ahead=((w_conv, (chunked(w["L1_gnn_W"]),)),))
                stage_graph_convolution(nc, k, w, xT, pairs, x, w_conv.tensors[0], w_conv.loaded)
                save(nc, s3, x, x_dram)
        with ExitStack() as last:
            s3 = Shop(nc, last, "last")
            xT = s3.sb("xT2", [128, KD, N])
            with ExitStack() as feat:
                s4 = Shop(nc, feat, "perf")
                v = s4.sb("v", [P, TILES, HEADS, VW])
                qkT_all = s4.sb("qkT_all", [128, 2, HEADS // 2, N])
                diag = s4.sb("diag", [P, 2, HEADS // 2, TILES, 2])
                top = s4.sb("top", [128, 1])
                w_feat = Ahead(Shop(nc, feat.enter_context(ExitStack()), "featin"), "qkv", (square, square, square))
                turn_again(nc, k, "again", acc, xT, ahead=((w_feat, (chunked(w["L1_mix_Wv"]), chunked(w["L1_mix_Wq"]),
                                                                     chunked(w["L1_mix_Wk"]))),))
                stage_queries_and_keys(nc, k, w, w_feat, xT, v, qkT_all, diag[:, :, :, :, :].rearrange("p q a t h -> p (q a t h)"), top)
                stage_random_features(nc, k, w, v, qkT_all, diag, top, acc)
            x = s3.sb("x2", [P, TILES, D])
            s4 = Shop(nc, last, "sw")
            w_switch = Ahead(s4, "switch", [square] * AHEAD)
            with ExitStack() as mix:
                w_mix = Ahead(Shop(nc, mix, "mix1"), "out", (square, [P, D]))
                turn_again(nc, k, "mixed1", acc, xT, x, x_dram,
                           ahead=((w_mix, (chunked(w["L1_mix_Wo"]), row(w["L1_mix_bo"], P))),
                                  (w_switch, [expert_weights(w, e) for e in range(AHEAD)])))
                stage_linear(nc, k, "featout", xT, w_mix, True, x)
            gather_slots, token_rows = s4.sb("gather_slots", [P, TILES], I32), s4.sb("token_rows3", [128, SWITCH], I32)
            share, keep = s4.sb("share", [P, TILES]), s4.sb("keep", [P, TILES])
            stage_norm(nc, k, "norm3", None, x, acc, xT, False, xn_dram=xn3_dram)
            stage_switch_route(nc, k, w, xT, gather_slots, share, keep, token_rows, tokens3)
            stage_switch_experts(nc, k, w, w_switch, token_rows, xn3_dram, y3_dram)
            stage_switch_combine(nc, k, x, acc, gather_slots, share, keep, y3_dram, out)


def save(nc, shop, x, x_dram):
    saved = shop.sem("x_saved")
    with nc.Block() as block:
        @block.sync
        def _(sp):
            sp.dma_start(tiles_of(x_dram), x[:, :, :]).then_inc(saved, 16)
            sp.wait_ge(saved, 16)


def turn_again(nc, k, tag, a, aT, x=None, x_dram=None, ahead=()):
    with ExitStack() as ctx:
        s = Shop(nc, ctx, tag)
        turn = s.ps("turn", [128, 2, 512])
        turned, kept, loaded = s.sem("turned"), s.sem("kept"), s.sem("loaded")
        with nc.Block() as block:
            @block.sync
            def _(sp):
                if x is not None:
                    sp.dma_start(x[:, :, :], tiles_of(x_dram)).then_inc(loaded, 16)
                for weights, sources in ahead:
                    weights.load(sp, sources)
                if x is not None:
                    sp.wait_ge(loaded, 16)

            @block.tensor
            def _(pe):
                for t in range(TILES):
                    if t >= 2:
                        pe.wait_ge(kept, t - 1)
                    for c in range(KD):
                        last = pe.transpose(turn[:, t % 2, c * P:(c + 1) * P], a[:, t, c * 128:(c + 1) * 128],
                                            k.ident[0:P, 0:P])
                    last.then_inc(turned, 1)

            @block.scalar
            def _(act):
                for t in range(TILES):
                    act.wait_ge(turned, t + 1)
                    act.activation(aT[:, :, t * P:(t + 1) * P],
                                   turn[:, t % 2, 0:KD * P].rearrange("p (c n) -> p c n", c=KD), ACT.Copy).then_inc(kept, 1)


def laid_out(inputs):
    import numpy as _np
    a = {n: _np.asarray(v) for n, v in inputs.items()}

    def columns(v):
        return v.reshape(-1, 128).T

    for n in ("L0_gnn_b_pre0", "L0_gnn_b_g1", "L0_gnn_b_g2", "L0_mix_ln_gamma", "L0_mix_ln_beta"):
        a[n] = columns(a[n])
    for n in ("L0_ffn_gate_w", "L1_gnn_W", "L1_mix_proj", "L1_ffn_switch_w"):
        a[n] = a[n].T
    a["L1_ffn_expert_w"] = a["L1_ffn_expert_w"].transpose(0, 2, 1)
    a["edges"] = _np.concatenate([a.pop("edge_attr_32"), a.pop("edge_attr_4"),
                                  _np.zeros((a["src"].shape[0], 4), _np.float32)], axis=1)
    return {n: _np.ascontiguousarray(v) for n, v in a.items()}


def kernel(**inputs):
    import concourse.bacc as _bacc
    from concourse import mybir as _mybir
    from concourse.bass_utils import run_bass_kernel_spmd as _run

    nc = _bacc.Bacc("TRN2", target_bir_lowering=False, num_devices=1)
    arrays, w = {}, {}
    for name, a in laid_out(inputs).items():
        arrays[f"in_{name}_dram"] = a
        w[name] = nc.dram_tensor(f"in_{name}_dram", a.shape, _mybir.dt.from_np(a.dtype), kind="ExternalInput").ap()
    out = nc.dram_tensor("out_0_dram", (N, D), F32, kind="ExternalOutput").ap()
    program(nc, w, out)
    r = _run(nc, [arrays], core_ids=[0])
    return r.results[0]["out_0_dram"]
```
